# Optimizing a Trainium2 kernel written in Bass

```python
import numpy as np
import jax
import jax.numpy as jnp

def _softmax(x, axis=-1):
    return jax.nn.softmax(x, axis=axis)

def _gelu(x):
    return jax.nn.gelu(x, approximate=True)

def _silu(x):
    return jax.nn.silu(x)

def _sigmoid(x):
    return jax.nn.sigmoid(x)

def _layernorm(x, axis=-1, eps=1e-05):
    m = jnp.mean(x, axis=axis, keepdims=True)
    v = jnp.var(x, axis=axis, keepdims=True)
    return (x - m) / jnp.sqrt(v + eps)

def _scatter_add(tgt, idx, src, axis=0):
    return tgt.at[idx].add(src)

def _segment_sum(src, seg, n):
    return jax.ops.segment_sum(src, seg, n)
kernel_name = 'mk_adaln_ffn_d1_seqx_r8_534d3f'

def setup_inputs(seed: int=0):
    np.random.seed(seed)
    _w = jnp.asarray

    def _rec_inputs():
        import jax
        import jax.numpy as jnp
        _rk = jax.random.key(seed)
        x = -0.0003929 + 0.9999 * jax.random.normal(jax.random.fold_in(_rk, 1), (128, 32, 512), jnp.float32)
        _lenS = 32 - jax.random.randint(jax.random.fold_in(_rk, 7), (128,), 0, max(1, 32 // 4) + 1, jnp.int32)
        _lenS2 = 32 - jax.random.randint(jax.random.fold_in(_rk, 8), (128,), 0, max(1, 32 // 4) + 1, jnp.int32)
        cond_512 = 0.00782532 + 1.00527 * jax.random.normal(jax.random.fold_in(_rk, 11), (128, 64), jnp.float32)
        return (x, cond_512)
    x, cond_512 = _rec_inputs()

    def _L0_cond_setup():
        import jax, jax.numpy as jnp
        from jax import lax
        import numpy as np
        CIN, COUT, K, STYLE_DIM = (32, 32, 3, 64)
        N_LAYERS = 4
        TYPES = ('same', 'upsample', 'same', 'downsample')
        SCALE = 1.0 / float(np.sqrt(CIN * K ** 2))
        EPS = 1e-08
        _BK = np.array([1.0, 3.0, 3.0, 1.0], dtype=np.float32)
        BLUR_K = _BK / _BK.sum()

        def _blur(x, kern, pad):
            B, C, _ = x.shape
            xp = jnp.pad(x, ((0, 0), (0, 0), (pad[0], pad[1])))
            w = jnp.broadcast_to(kern.astype(x.dtype)[None, None, :], (C, 1, kern.shape[0]))
            return lax.conv_general_dilated(xp, w, (1,), 'VALID', feature_group_count=C, dimension_numbers=('NCH', 'OIH', 'NCH'))

        def _conv_same(x, w):
            p = (K - 1) // 2
            return lax.conv_general_dilated(x[None], w, (1,), [(p, p)], dimension_numbers=('NCH', 'OIH', 'NCH'))[0]

        def _conv_down(x, w):
            return lax.conv_general_dilated(x[None], w, (2,), 'VALID', dimension_numbers=('NCH', 'OIH', 'NCH'))[0]

        def _conv_up(x, w_t):
            return lax.conv_transpose(x[None], w_t, (2,), 'VALID', dimension_numbers=('NCH', 'IOH', 'NCH'), transpose_kernel=True)[0]

        def _layer(x, style, w, b, mw, mb, typ):
            s = style @ mw.T + mb
            weight = SCALE * w * s[:, None, :, None]
            demod = lax.rsqrt(jnp.sum(weight * weight, axis=(2, 3)) + EPS)
            weight = weight * demod[:, :, None, None]
            blur_k = jnp.asarray(BLUR_K)
            if typ == 'same':
                out = jax.vmap(_conv_same)(x, weight) + b[None, :, None]
            elif typ == 'upsample':
                out = jax.vmap(_conv_up)(x, weight.transpose(0, 2, 1, 3)) + b[None, :, None]
                out = _blur(out, 2.0 * blur_k, (1, 1))
            elif typ == 'downsample':
                xb = _blur(x, blur_k, (2, 2))
                out = jax.vmap(_conv_down)(xb, weight) + b[None, :, None]
            else:
                raise NotImplementedError(typ)
            return out
        key = jax.random.key(seed)
        ks = jax.random.split(key, 6)
        B, L = (16, 512)
        return {'x': jax.random.normal(ks[0], (B, CIN, L), dtype=jnp.float32), 'style': jax.random.normal(ks[1], (B, STYLE_DIM), dtype=jnp.float32), 'weights': jax.random.normal(ks[2], (N_LAYERS, COUT, CIN, K), dtype=jnp.float32), 'biases': jax.random.normal(ks[3], (N_LAYERS, COUT), dtype=jnp.float32) * 0.1, 'mod_w': jax.random.normal(ks[4], (N_LAYERS, CIN, STYLE_DIM), dtype=jnp.float32) / np.sqrt(STYLE_DIM), 'mod_b': 1.0 + 0.1 * jax.random.normal(ks[5], (N_LAYERS, CIN), dtype=jnp.float32)}
    _L0_cond_all = _L0_cond_setup()
    _L0_cond_in = {k: v for k, v in _L0_cond_all.items() if k in ('weights', 'biases', 'mod_w', 'mod_b')}
    del _L0_cond_all

    def _L0_ffn_setup():
        import jax, jax.numpy as jnp
        import numpy as np
        H = 512
        I = 256
        E = 16
        TOPK = 4
        SI = 256
        key = jax.random.key(seed)
        ks = jax.random.split(key, 9)
        s = 0.02
        return {'hidden_states': jax.random.normal(ks[0], (2, 256, H), dtype=jnp.float32), 'gate_w': jax.random.normal(ks[1], (E, H), dtype=jnp.float32) * s, 'bias': jnp.zeros((E,), dtype=jnp.float32), 'Wg': jax.random.normal(ks[2], (E, I, H), dtype=jnp.float32) * s, 'Wu': jax.random.normal(ks[3], (E, I, H), dtype=jnp.float32) * s, 'Wd': jax.random.normal(ks[4], (E, H, I), dtype=jnp.float32) * s, 'Sg': jax.random.normal(ks[5], (SI, H), dtype=jnp.float32) * s, 'Su': jax.random.normal(ks[6], (SI, H), dtype=jnp.float32) * s, 'Sd': jax.random.normal(ks[7], (H, SI), dtype=jnp.float32) * s}
    _L0_ffn_all = _L0_ffn_setup()
    _L0_ffn_in = {k: v for k, v in _L0_ffn_all.items() if k in ('gate_w', 'bias', 'Wg', 'Wu', 'Wd', 'Sg', 'Su', 'Sd')}
    del _L0_ffn_all
    return {'x': x, 'cond_512': cond_512, 'L0_cond_weights': _L0_cond_in['weights'], 'L0_cond_biases': _L0_cond_in['biases'], 'L0_cond_mod_w': _L0_cond_in['mod_w'], 'L0_cond_mod_b': _L0_cond_in['mod_b'], 'L0_ffn_gate_w': _L0_ffn_in['gate_w'], 'L0_ffn_bias': _L0_ffn_in['bias'], 'L0_ffn_Wg': _L0_ffn_in['Wg'], 'L0_ffn_Wu': _L0_ffn_in['Wu'], 'L0_ffn_Wd': _L0_ffn_in['Wd'], 'L0_ffn_Sg': _L0_ffn_in['Sg'], 'L0_ffn_Su': _L0_ffn_in['Su'], 'L0_ffn_Sd': _L0_ffn_in['Sd']}

def reference(x, cond_512, L0_cond_weights, L0_cond_biases, L0_cond_mod_w, L0_cond_mod_b, L0_ffn_gate_w, L0_ffn_bias, L0_ffn_Wg, L0_ffn_Wu, L0_ffn_Wd, L0_ffn_Sg, L0_ffn_Su, L0_ffn_Sd):
    import jax
    import jax.numpy as jnp

    def _L0_cond_ref(x, style, weights, biases, mod_w, mod_b):
        import jax, jax.numpy as jnp
        from jax import lax
        import numpy as np
        CIN, COUT, K, STYLE_DIM = (32, 32, 3, 64)
        N_LAYERS = 4
        TYPES = ('same', 'upsample', 'same', 'downsample')
        SCALE = 1.0 / float(np.sqrt(CIN * K ** 2))
        EPS = 1e-08
        _BK = np.array([1.0, 3.0, 3.0, 1.0], dtype=np.float32)
        BLUR_K = _BK / _BK.sum()

        def _blur(x, kern, pad):
            B, C, _ = x.shape
            xp = jnp.pad(x, ((0, 0), (0, 0), (pad[0], pad[1])))
            w = jnp.broadcast_to(kern.astype(x.dtype)[None, None, :], (C, 1, kern.shape[0]))
            return lax.conv_general_dilated(xp, w, (1,), 'VALID', feature_group_count=C, dimension_numbers=('NCH', 'OIH', 'NCH'))

        def _conv_same(x, w):
            p = (K - 1) // 2
            return lax.conv_general_dilated(x[None], w, (1,), [(p, p)], dimension_numbers=('NCH', 'OIH', 'NCH'))[0]

        def _conv_down(x, w):
            return lax.conv_general_dilated(x[None], w, (2,), 'VALID', dimension_numbers=('NCH', 'OIH', 'NCH'))[0]

        def _conv_up(x, w_t):
            return lax.conv_transpose(x[None], w_t, (2,), 'VALID', dimension_numbers=('NCH', 'IOH', 'NCH'), transpose_kernel=True)[0]

        def _layer(x, style, w, b, mw, mb, typ):
            s = style @ mw.T + mb
            weight = SCALE * w * s[:, None, :, None]
            demod = lax.rsqrt(jnp.sum(weight * weight, axis=(2, 3)) + EPS)
            weight = weight * demod[:, :, None, None]
            blur_k = jnp.asarray(BLUR_K)
            if typ == 'same':
                out = jax.vmap(_conv_same)(x, weight) + b[None, :, None]
            elif typ == 'upsample':
                out = jax.vmap(_conv_up)(x, weight.transpose(0, 2, 1, 3)) + b[None, :, None]
                out = _blur(out, 2.0 * blur_k, (1, 1))
            elif typ == 'downsample':
                xb = _blur(x, blur_k, (2, 2))
                out = jax.vmap(_conv_down)(xb, weight) + b[None, :, None]
            else:
                raise NotImplementedError(typ)
            return out
        out = x
        for i, typ in enumerate(TYPES):
            out = _layer(out, style, weights[i], biases[i], mod_w[i], mod_b[i], typ)
        return out

    def _L0_ffn_ref(hidden_states, gate_w, bias, Wg, Wu, Wd, Sg, Su, Sd):
        import jax, jax.numpy as jnp
        import numpy as np
        H = 512
        I = 256
        E = 16
        TOPK = 4
        SI = 256
        orig_shape = hidden_states.shape
        x = hidden_states.reshape(-1, orig_shape[-1])
        scores = jax.nn.sigmoid(x @ gate_w.T) + bias
        topk_w, topk_idx = jax.lax.top_k(scores, TOPK)
        topk_w = topk_w / (jnp.sum(topk_w, axis=-1, keepdims=True) + 1e-20)
        cw = jnp.sum(jax.nn.one_hot(topk_idx, E, dtype=x.dtype) * topk_w[..., None], axis=1)
        g = jnp.einsum('th,eih->eti', x, Wg)
        u = jnp.einsum('th,eih->eti', x, Wu)
        z = jax.nn.silu(g) * u
        zw = z * cw.T[:, :, None]
        out = jnp.einsum('eti,ehi->th', zw, Wd)
        out = out + jax.nn.silu(x @ Sg.T) * (x @ Su.T) @ Sd.T
        return out.reshape(orig_shape)
    x = x + _L0_ffn_ref(_L0_cond_ref(x, cond_512, L0_cond_weights, L0_cond_biases, L0_cond_mod_w, L0_cond_mod_b), L0_ffn_gate_w, L0_ffn_bias, L0_ffn_Wg, L0_ffn_Wu, L0_ffn_Wd, L0_ffn_Sg, L0_ffn_Su, L0_ffn_Sd)
    return x

_drawn_inputs = setup_inputs


def setup_inputs(seed=0):
    import zlib

    import numpy as np

    out = dict(_drawn_inputs(seed))
    spreads = {'L0_ffn_bias': (0.0, 0.8)}
    factors = {'L0_cond_biases': 5.876,
     'L0_cond_mod_b': 8.0,
     'L0_ffn_gate_w': 7.847,
     'L0_ffn_Wg': 5.924,
     'L0_ffn_Wu': 5.851,
     'L0_ffn_Wd': 5.824,
     'L0_ffn_Sg': 2.967,
     'L0_ffn_Su': 2.9,
     'L0_ffn_Sd': 2.936}
    for name, (base, spread) in spreads.items():
        noise = np.random.default_rng([zlib.crc32(name.encode()), seed]).standard_normal(out[name].shape)
        drawn = base * np.exp(spread * noise) if base else spread * noise
        out[name] = jnp.asarray(drawn.astype(out[name].dtype))
    for name, factor in factors.items():
        out[name] = (out[name] * factor).astype(out[name].dtype)
    return out
```

```python
from contextlib import ExitStack

import concourse.bass as bass
from concourse import mybir

P = 128
F32 = mybir.dt.float32
F32R = mybir.dt.float32r
I32 = mybir.dt.int32
U32 = mybir.dt.uint32
ALU = mybir.AluOpType
ACT = mybir.ActivationFunctionType
AX_X = mybir.AxisListType.X

SPLIT = ((0, 0), (0, 1), (1, 0))


def mk_adaln_ffn(nc, x, style, cw, cb, mod_w, mod_b, gate_w, ebias, Wg, Wu, Wd, Sg, Su, Sd, out):
    B, C, L = x.shape
    NL, _, _, K = cw.shape
    SD = style.shape[1]
    E, I, H = Wg.shape
    TOPK = 4
    T = B * C
    G = T // P
    NB = P // C
    HC = H // P
    IC = I // P
    JOB = 2 * P
    MAXJOBS = T // JOB
    COLS = T // P
    NCOL = TOPK * T // P + 2 * E + 2
    NCOL = NCOL + COLS
    PAD = 2 * P
    TAPS = (3, 6, 3, 6)
    TAP0 = (0, 3, 9, 12)
    NT = sum(TAPS)
    SCALE = 1.0 / float(C * K * K) ** 0.5
    assert L == 512 and H == L and C * NB == P and 2 * I == 512 and NL == 4 and K == 3
    WBANK = (0, 1, 2, 3, 6, 7)
    BK = (1 / 8, 3 / 8, 3 / 8, 1 / 8)
    UPK = tuple(2 * b for b in BK)

    x_rows = x.rearrange("b c l -> (b c) l")
    h_rows = nc.dram_tensor("h_rows", [T + PAD, H], F32, kind="Internal").ap()
    lists = nc.dram_tensor("lists", [P * E * COLS, 2], F32, kind="Internal").ap()

    with ExitStack() as ctx:
        def sb(name, shape, dt=F32):
            return ctx.enter_context(nc.sbuf_tensor(name, shape, dt))

        def sem(name):
            return ctx.enter_context(nc.semaphore(name))

        bank = [ctx.enter_context(nc.psum_tensor(f"bank{i}", [P, 512], F32)) for i in range(8)]

        ident = sb("ident", [P, P])
        tri = sb("tri", [P, P])
        ones = sb("ones", [P, P])
        iota_e = sb("iota_e", [P, E])
        iota_ei = sb("iota_ei", [P, E], I32)
        region = sb("region", [P, E])
        thresh = sb("thresh", [P, E])
        tok = sb("tok", [P, 1])
        tok_i = sb("tok_i", [P, 1], I32)
        pad_i = sb("pad_i", [P, 2], I32)
        wnat = sb("wnat", [P, NL, C, K])
        mats = sb("mats", [P, NT + 4, C])
        wsq = sb("wsq", [P, NL, C, K])
        diag = sb("diag", [P, NT + 4, NB, C])
        cwt = [sb("cwt_hi", [P, NT, P], F32R), sb("cwt_lo", [P, NT, P], F32R)]
        wsqt = sb("wsqt", [P, NL, P])
        modw = sb("modw", [P, SD])
        modwt = sb("modwt", [SD, NL, NB, C])
        sty = sb("sty", [P, SD])
        styt = sb("styt", [SD, B])
        modb = sb("modb", [P, NL])
        cbias = sb("cbias", [P, NL])
        s = sb("s", [P, NL, G])
        s2 = sb("s2", [P, NL, G])
        dv = sb("dv", [P, NL, G])
        d = sb("d", [P, NL, G])
        cA = sb("cA", [P, NL, G])
        cB = sb("cB", [P, NL, G])
        edge = sb("edge", [P, G])
        epsb = sb("epsb", [P, 1])
        biasrow = sb("biasrow", [P, E])
        gnat = sb("gnat", [E, H])
        gwt = [sb("gwt_hi", [P, HC, E], F32R), sb("gwt_lo", [P, HC, E], F32R)]
        listinit = sb("listinit", [P, E * COLS, 2])
        zrow = sb("zrow", [P, H])

        wraw = sb("wraw", [P, 2 * IC, H])
        wdraw = sb("wdraw", [P, HC, I])
        wup = [sb("wup_hi", [P, HC, 2 * I], F32R), sb("wup_lo", [P, HC, 2 * I], F32R)]
        wdn = [sb("wdn_hi", [P, IC, H], F32R), sb("wdn_lo", [P, IC, H], F32R)]

        xraw = sb("xraw", [P, 2, L])
        xbase = sb("xbase", [P, 2, L])
        x0 = [sb("x0_hi", [P, L + 2], F32R), sb("x0_lo", [P, L + 2], F32R)]
        x1 = [sb("x1_hi", [P, L + 2], F32R), sb("x1_lo", [P, L + 2], F32R)]
        x2 = [sb("x2_hi", [P, 2, L + 2], F32R), sb("x2_lo", [P, 2, L + 2], F32R)]
        x3 = [sb("x3_hi", [P, 2, L + 2], F32R), sb("x3_lo", [P, 2, L + 2], F32R)]
        t1 = sb("t1", [P, L])
        t2 = sb("t2", [P, 2, L])
        t3 = sb("t3", [P, 2, L])
        hrow = sb("hrow", [P, 2, L])
        orow = sb("orow", [P, 2, L])
        xt = [sb("xt_hi", [P, 2, HC, P], F32R), sb("xt_lo", [P, 2, HC, P], F32R)]
        sg = sb("sg", [P, 2, I])
        z = sb("z", [P, 2, I])
        zt = [sb("zt_hi", [P, 2, IC, P], F32R), sb("zt_lo", [P, 2, IC, P], F32R)]
        sig = sb("sig", [P, E])
        sc = sb("sc", [P, E])
        top = sb("top", [P, 8])
        topi = sb("topi", [P, 8], U32)
        topf = sb("topf", [P, TOPK])
        tsum = sb("tsum", [P, 1])
        tsum2 = sb("tsum2", [P, 1])
        trec = sb("trec", [P, 1])
        hot = sb("hot", [P, TOPK, E])
        mask = sb("mask", [P, E])
        cum = sb("cum", [P, 2, E])
        pos = sb("pos", [P, E])
        hotpos = sb("hotpos", [P, TOPK, E])
        key = sb("key", [P, TOPK])
        key_i = sb("key_i", [P, TOPK], I32)
        lane_i = sb("lane_i", [P, TOPK], I32)
        col_i = sb("col_i", [P, TOPK], I32)
        place = sb("place", [P, 2, TOPK], I32)
        entry = sb("entry", [P, 2, TOPK, 2])
        cnt = sb("cnt", [P, E])
        over = sb("over", [P, E, E])
        njobs = sb("njobs", [P, E])
        job0 = sb("job0", [P, E + 1])
        job0_i = sb("job0_i", [P, E + 1], I32)
        all_lists = sb("all_lists", [P, E * COLS, 2])
        job_lists = sb("job_lists", [P, NCOL, 2])
        job_ids = sb("job_ids", [P, NCOL], I32)
        gid = sb("gid", [P, 2, 1], I32)
        sid = sb("sid", [P, 2, 1], I32)
        xg = sb("xg", [P, 2, H])
        yb = sb("yb", [P, 2, H])

        names = ("setup_loaded iota_done consts_done dve_step mats_ready modt_ready modt_copied "
                 "s_psum diag_t wts_hi wts_lo dem_psum sqrt_done scales_ready gate_t "
                 "raw_loaded w_t w_hi w_lo pads_zero fill_written "
                 "x_loaded0 x_loaded1 base_loaded0 base_loaded1 x0_hi x0_lo "
                 "l0_done l1_done l2_done l3_done t1_ready t2_ready t3_ready h_ready "
                 "x1_ready x2_ready x3_ready xt_t xt_hi xt_lo up_done sg_ready z_ready "
                 "logits_done sig_ready mask_ready prefix_done place_ready zt_t zt_hi zt_lo down_done "
                 "o_ready h_written0 h_written1 o_written0 o_written1 scattered0 scattered1 "
                 "lists_loaded count_done jobs_ready job_lists_ready "
                 "gather_id b_gathered0 b_gathered1 b_xt_t b_xt_hi b_xt_lo b_up b_sg b_z b_zt_t b_zt_hi b_zt_lo "
                 "b_down b_y scatter_id b_added landed_pool landed_act landed_dve landed_pe").split()
        S = {n: sem(n) for n in names}

        LANDS = {nc.gpsimd.engine: "pool", nc.scalar.engine: "act", nc.vector.engine: "dve", nc.tensor.engine: "pe"}

        def land(eng):
            eng.sem_inc(S[f"landed_{LANDS[eng.engine]}"], 1)

        def mm3(pe, dst, lhs, rhs, first, last):
            for n, (a, b) in enumerate(SPLIT):
                r = pe.matmul(dst, lhs[a], rhs[b], start=first and n == 0, stop=last and n == 2)
            return r

        block = ctx.enter_context(nc.Block())

        @block.sync
        def _(sp):
            for l in range(NL):
                for b in range(NB):
                    sp.dma_start(wnat[C * b:C * b + C, l].rearrange("o i k -> o (i k)"),
                                 cw[l].rearrange("o i k -> o (i k)")).then_inc(S["setup_loaded"], 16)
            for b in range(NB):
                sp.dma_start(modb[C * b:C * b + C, :], mod_b.rearrange("l c -> c l"), allow_slow_non_contiguous=True).then_inc(S["setup_loaded"], 16)
                sp.dma_start(cbias[C * b:C * b + C, :], cb.rearrange("l c -> c l"), allow_slow_non_contiguous=True).then_inc(S["setup_loaded"], 16)
            sp.dma_start(modw[:], mod_w.rearrange("l c d -> (l c) d")).then_inc(S["setup_loaded"], 16)
            sp.dma_start(sty[:], style).then_inc(S["setup_loaded"], 16)
            sp.dma_start(gnat[:], gate_w).then_inc(S["setup_loaded"], 16)
            sp.dma_start(biasrow[:], ebias.rearrange("(a e) -> a e", a=1).broadcast_to([P, E])).then_inc(S["setup_loaded"], 16)
            sp.dma_start(wraw[:, 0:IC, :], Sg.rearrange("(m p) h -> p m h", p=P)).then_inc(S["raw_loaded"], 16)
            sp.dma_start(wraw[:, IC:, :], Su.rearrange("(m p) h -> p m h", p=P)).then_inc(S["raw_loaded"], 16)
            sp.dma_start(wdraw[:], Sd.rearrange("(m p) i -> p m i", p=P)).then_inc(S["raw_loaded"], 16)
            for g in range(2):
                sp.dma_start(xraw[:, g, :], x_rows[P * g:P * g + P, :]).then_inc(S[f"x_loaded{g}"], 16)
                sp.dma_start(xbase[:, g, :], x_rows[P * g:P * g + P, :]).then_inc(S[f"base_loaded{g}"], 16)
            sp.wait_ge(S["consts_done"], 1)
            for n in range(PAD // P):
                sp.dma_start(h_rows[T + P * n:T + P * n + P, :], zrow[:]).then_inc(S["fill_written"], 16)
            sp.dma_start(lists.rearrange("(p n) w -> p n w", p=P), listinit[:]).then_inc(S["fill_written"], 16)
            sp.wait_ge(S["w_t"], HC + IC)
            sp.dma_start(wraw[:, 0:IC, :], Wg[0].rearrange("(m p) h -> p m h", p=P)).then_inc(S["raw_loaded"], 16)
            sp.dma_start(wraw[:, IC:, :], Wu[0].rearrange("(m p) h -> p m h", p=P)).then_inc(S["raw_loaded"], 16)
            sp.dma_start(wdraw[:], Wd[0].rearrange("(m p) i -> p m i", p=P)).then_inc(S["raw_loaded"], 16)

            def body(g, par, k, head=False, tail=0):
                if tail < 2:
                    if tail < 1:
                        sp.wait_ge(S["x0_hi"], g + 1)
                        sp.wait_ge(S["x0_lo"], g + 1)
                        sp.dma_start(xraw[:, par, :], x_rows[bass.ds(P * (g + 2), P), :]).then_inc(S[f"x_loaded{par}"], 16)
                    sp.wait_ge(S["h_ready"], g + 1)
                    sp.dma_start(h_rows[bass.ds(P * g, P), :], hrow[:, par, :]).then_inc(S[f"h_written{par}"], 16)
                if not head:
                    sp.wait_ge(S["o_ready"], g)
                    sp.dma_start(out[bass.ds(P * (g - 1), P), :], orow[:, 1 - par, :]).then_inc(S[f"o_written{1 - par}"], 16)
                    if tail < 1:
                        sp.dma_start(xbase[:, 1 - par, :], x_rows[bass.ds(P * (g + 1), P), :]).then_inc(S[f"base_loaded{1 - par}"], 16)

            body(0, 0, 0, head=True)
            body(1, 1, None)
            body(2, 0, None)
            with sp.Fori(1, (G - 4) // 2) as it:
                for u in range(2):
                    body(it * 2 + (1 + u), (1 + u) % 2, None)
            body(G - 3, 1, None)
            body(G - 2, 0, None, tail=1)
            sp.dma_start(xbase[:, 1, :], x_rows[P * (G - 1):P * G, :]).then_inc(S["base_loaded1"], 16)
            body(G - 1, 1, None, tail=1)
            body(G, 0, None, tail=2)
            sp.wait_ge(S["scattered0"], 16 * TOPK * (G // 2))
            sp.wait_ge(S["scattered1"], 16 * TOPK * (G // 2))
            sp.dma_start(all_lists[:], lists.rearrange("(p n) w -> p n w", p=P)).then_inc(S["lists_loaded"], 16)
            with sp.Fori(1, E) as e:
                sp.wait_ge(S["w_t"], (e + 1) * (HC + IC))
                sp.dma_start(wraw[:, 0:IC, :], Wg[bass.ds(e, 1)].rearrange("a (m p) h -> p (a m) h", p=P)).then_inc(S["raw_loaded"], 16)
                sp.dma_start(wraw[:, IC:, :], Wu[bass.ds(e, 1)].rearrange("a (m p) h -> p (a m) h", p=P)).then_inc(S["raw_loaded"], 16)
                sp.dma_start(wdraw[:], Wd[bass.ds(e, 1)].rearrange("a (m p) i -> p (a m) i", p=P)).then_inc(S["raw_loaded"], 16)

        @block.gpsimd
        def _(pool):
            pool.iota(iota_ei[:], pattern=[[1, E]], base=0, channel_multiplier=0).then_inc(S["iota_done"], 1)
            pool.iota(tok_i[:], pattern=[[0, 1]], base=0, channel_multiplier=1).then_inc(S["iota_done"], 1)
            pool.iota(pad_i[:], pattern=[[P, 2]], base=T, channel_multiplier=1).then_inc(S["iota_done"], 1)
            pool.memset(ident[:], 0.0).then_inc(S["iota_done"], 1)
            pool.memset(tri[:], 1.0).then_inc(S["iota_done"], 1)
            pool.memset(ones[:], 1.0).then_inc(S["iota_done"], 1)
            pool.wait_ge(S["iota_done"], 6)
            pool.affine_select(out=ident[:], in_=ident[:], compare_op=ALU.not_equal, fill=1.0, base=0,
                               pattern=[[-1, P]], channel_multiplier=1).then_inc(S["iota_done"], 1)
            pool.affine_select(out=tri[:], in_=tri[:], compare_op=ALU.is_gt, fill=0.0, base=0,
                               pattern=[[1, P]], channel_multiplier=-1).then_inc(S["iota_done"], 1)
            pool.wait_ge(S["fill_written"], 16 * (PAD // P + 1))
            for n in range(PAD // P):
                pool.dma_start(out[T + P * n:T + P * n + P, :], zrow[:]).then_inc(S["b_added"], 16)

            def scatter(g, par):
                pool.wait_ge(S["place_ready"], g + 1)
                land(pool)
                for k in range(TOPK):
                    pool.indirect_dma_start(
                        out=lists, out_offset=bass.IndirectOffsetOnAxis(ap=place[:, par, k:k + 1], axis=0),
                        in_=entry[:, par, k, :], in_offset=None).then_inc(S[f"scattered{par}"], 16)

            with pool.Fori(0, G // 2) as it:
                for u in range(2):
                    scatter(it * 2 + u, u)

            pool.wait_ge(S["job_lists_ready"], 2)
            pool.wait_ge(S["h_written0"], 16 * (G // 2))
            pool.wait_ge(S["h_written1"], 16 * (G // 2))
            for u in range(2):
                pool.tensor_copy(gid[:, u, :], job_ids[:, u:u + 1]).then_inc(S["gather_id"], 1)
            pool.wait_ge(S["gather_id"], 2)
            for u in range(2):
                pool.indirect_dma_start(out=xg[:, u, :], out_offset=None, in_=h_rows,
                                        in_offset=bass.IndirectOffsetOnAxis(ap=gid[:, u, :], axis=0)).then_inc(S[f"b_gathered{u}"], 16)
            pool.wait_ge(S["o_written0"], 16 * (G // 2))
            pool.wait_ge(S["o_written1"], 16 * (G // 2))
            with pool.Fori(0, E) as e:
                first = pool.value_load(job0_i[0:1, bass.ds(e, 1)], min_val=0, max_val=TOPK * T // JOB + E)
                end = pool.value_load(job0_i[0:1, bass.ds(e + 1, 1)], min_val=1, max_val=TOPK * T // JOB + E)
                with pool.Fori(first, end) as j:
                    for u in range(2):
                        pool.wait_ge(S[f"b_gathered{u}"], 16 * (j + 1))
                        land(pool)
                        pool.tensor_copy(gid[:, u, :], job_ids[:, bass.ds(j * 2 + (2 + u), 1)]).then_inc(S["gather_id"], 1)
                    for u in range(2):
                        pool.wait_ge(S["gather_id"], j * 2 + (3 + u))
                        pool.wait_ge(S["b_xt_t"], j * 2 + (1 + u))
                        land(pool)
                        pool.indirect_dma_start(out=xg[:, u, :], out_offset=None, in_=h_rows,
                                                in_offset=bass.IndirectOffsetOnAxis(ap=gid[:, u, :], axis=0)).then_inc(S[f"b_gathered{u}"], 16)
                    pool.wait_ge(S["b_added"], 32 * (j + 1))
                    land(pool)
                    for u in range(2):
                        pool.tensor_copy(sid[:, u, :], job_ids[:, bass.ds(j * 2 + u, 1)]).then_inc(S["scatter_id"], 1)
                    for u in range(2):
                        pool.wait_ge(S["scatter_id"], j * 2 + (1 + u))
                        pool.wait_ge(S["b_y"], j * 2 + (3 + u))
                        land(pool)
                        pool.indirect_dma_start(out=out, out_offset=bass.IndirectOffsetOnAxis(ap=sid[:, u, :], axis=0),
                                                in_=yb[:, u, :], in_offset=None, compute_op=ALU.add).then_inc(S["b_added"], 16)
            end = pool.value_load(job0_i[0:1, E:E + 1], min_val=1, max_val=TOPK * T // JOB + E)
            pool.wait_ge(S["b_added"], 32 * (end + 1))
            pool.wait_ge(S["b_gathered0"], 16 * (end + 1))
            pool.wait_ge(S["b_gathered1"], 16 * (end + 1))

        @block.scalar
        def _(act):
            def weights_hi(n):
                for c in range(HC):
                    act.wait_ge(S["w_t"], n * (HC + IC) + (c + 1))
                    act.activation(wup[0][:, c, :], bank[WBANK[c]][:], ACT.Copy).then_inc(S["w_hi"], 1)
                for c in range(IC):
                    act.wait_ge(S["w_t"], n * (HC + IC) + (HC + c + 1))
                    act.activation(wdn[0][:, c, :], bank[WBANK[HC + c]][:], ACT.Copy).then_inc(S["w_hi"], 1)

            act.wait_ge(S["dem_psum"], 1)
            act.wait_ge(S["consts_done"], 1)
            act.activation(dv[:].rearrange("p l g -> p (l g)"), bank[5][:, 0:NL * G], ACT.Sqrt,
                           scale=SCALE * SCALE, bias=epsb[:]).then_inc(S["sqrt_done"], 1)
            for n in range(3):
                act.wait_ge(S["diag_t"], n + 1)
                dst = cwt[0][:, (0, 9, 12)[n]:(3, 12, 18)[n], :].rearrange("p t m -> p (t m)")
                if n < 2:
                    act.activation(dst, bank[n][:, 0:3 * P], ACT.Copy).then_inc(S["wts_hi"], 1)
                else:
                    act.activation(cwt[0][:, 12:15, :].rearrange("p t m -> p (t m)"), bank[2][:, 0:3 * P], ACT.Copy).then_inc(S["wts_hi"], 1)
                    act.activation(cwt[0][:, 15:18, :].rearrange("p t m -> p (t m)"), bank[3][:, 0:3 * P], ACT.Copy).then_inc(S["wts_hi"], 1)
            act.wait_ge(S["mats_ready"], 2)
            act.activation(cwt[0][:, 3:9, :].rearrange("p t m -> p (t m)"),
                           diag[:, 3:9].rearrange("p t b c -> p (t b c)"), ACT.Copy).then_inc(S["wts_hi"], 1)
            act.wait_ge(S["gate_t"], 1)
            act.activation(gwt[0][:].rearrange("p c e -> p (c e)"), bank[6][:, 0:HC * E], ACT.Copy).then_inc(S["wts_hi"], 1)
            act.wait_ge(S["wts_hi"], 6)
            weights_hi(0)

            def first_in(g, par, k):
                act.wait_ge(S[f"x_loaded{par}"], 16 * (k + 1))
                land(act)
                act.activation(x0[0][:, 1:L + 1], xraw[:, par, :], ACT.Copy, scale=s[:, 0, bass.ds(g, 1)]).then_inc(S["x0_hi"], 1)

            def evac(g, src, dst, l, done):
                act.activation(dst, src, ACT.Identity, scale=cA[:, l, bass.ds(g, 1)], bias=cB[:, l, bass.ds(g, 1)]).then_inc(done, 1)

            def layer0(g):
                act.wait_ge(S["l0_done"], g + 1)
                if not (isinstance(g, int) and g == 0):
                    act.wait_ge(S["x1_ready"], g * 2)
                land(act)
                evac(g, bank[0][:], t1[:], 0, S["t1_ready"])

            def body(g, par, k, head=False, tail=0):
                if tail < 1:
                    act.wait_ge(S["l0_done"], g + 1)
                    first_in(g + 1, 1 - par, k[1])
                if tail < 2:
                    for ph in range(2):
                        act.wait_ge(S["l1_done"], g * 2 + (ph + 1))
                        if not head:
                            act.wait_ge(S["x2_ready"], g * 4 - 2 + 2 * ph)
                        land(act)
                        evac(g, bank[1 + ph][:], t2[:, ph, :], 1, S["t2_ready"])
                if not head:
                    act.wait_ge(S["xt_t"], g)
                    act.activation(xt[0][:, 0].rearrange("p c t -> p (c t)"), bank[5][:], ACT.Copy).then_inc(S["xt_hi"], 1)
                if tail < 2:
                    for ph in range(2):
                        act.wait_ge(S["l2_done"], g * 2 + (ph + 1))
                        if not head:
                            act.wait_ge(S["x3_ready"], g * 4 - 2 + 2 * ph)
                        land(act)
                        evac(g, bank[3 + ph][:], t3[:, ph, :], 2, S["t3_ready"])
                if not head:
                    act.wait_ge(S["up_done"], g)
                    if not (isinstance(g, int) and g == 1):
                        act.wait_ge(S["z_ready"], g - 1)
                    act.activation(sg[:, 0, :], bank[6][:, 0:I], ACT.Sigmoid).then_inc(S["sg_ready"], 1)
                    act.wait_ge(S["logits_done"], g)
                    if not (isinstance(g, int) and g == 1):
                        act.wait_ge(S["place_ready"], g - 1)
                    act.activation(sig[:], bank[0][:, 0:E], ACT.Sigmoid).then_inc(S["sig_ready"], 1)
                if tail < 2:
                    act.wait_ge(S["l3_done"], g + 1)
                    if not (isinstance(g, int) and g < 2):
                        act.wait_ge(S[f"h_written{par}"], k[0] * 16)
                        act.wait_ge(S["xt_t"], g - 1)
                    land(act)
                    evac(g, bank[1][:], hrow[:, par, :], 3, S["h_ready"])
                if not head:
                    act.wait_ge(S["zt_t"], g)
                    act.activation(zt[0][:, 0].rearrange("p c t -> p (c t)"), bank[7][:, 0:I], ACT.Copy).then_inc(S["zt_hi"], 1)
                if tail < 1:
                    layer0(g + 1)

            act.wait_ge(S["scales_ready"], 1)
            act.wait_ge(S["pads_zero"], 1)
            first_in(0, 0, 0)
            layer0(0)
            body(0, 0, (0, 0), head=True)
            body(1, 1, (0, 1))
            body(2, 0, (1, 1))
            with act.Fori(1, (G - 4) // 2) as it:
                body(it * 2 + 1, 1, (it, it + 1))
                body(it * 2 + 2, 0, (it + 1, it + 1))
            body(G - 3, 1, ((G - 3) // 2, (G - 2) // 2))
            body(G - 2, 0, ((G - 2) // 2, (G - 1) // 2))
            body(G - 1, 1, ((G - 1) // 2, 0), tail=1)
            body(G, 0, (0, 0), tail=2)

            def turned_in(j, u):
                act.wait_ge(S["b_xt_t"], j * 2 + (u + 1))
                act.activation(xt[0][:, u].rearrange("p c t -> p (c t)"), bank[4 + u][:], ACT.Copy).then_inc(S["b_xt_hi"], 1)

            for u in range(2):
                turned_in(0, u)
            act.wait_ge(S["jobs_ready"], 1)
            with act.Fori(0, E) as e:
                first = act.value_load(job0_i[0:1, bass.ds(e, 1)], min_val=0, max_val=TOPK * T // JOB + E)
                end = act.value_load(job0_i[0:1, bass.ds(e + 1, 1)], min_val=1, max_val=TOPK * T // JOB + E)
                weights_hi(e + 1)
                with act.Fori(first, end) as j:
                    for u in range(2):
                        act.wait_ge(S["b_up"], j * 2 + (u + 1))
                        act.activation(sg[:, u, :], bank[u][:, 0:I], ACT.Sigmoid).then_inc(S["b_sg"], 1)
                        act.wait_ge(S["b_zt_t"], j * 2 + (u + 1))
                        act.activation(zt[0][:, u].rearrange("p c t -> p (c t)"), bank[2 + u][:, 0:I], ACT.Copy).then_inc(S["b_zt_hi"], 1)
                    for u in range(2):
                        turned_in(j + 1, u)

        @block.vector
        def _(dve):
            count = [0]

            def link(ins):
                ins.then_inc(S["dve_step"], 1)
                count[0] += 1
                dve.wait_ge(S["dve_step"], count[0])

            flat = lambda a: a.rearrange("p l i k -> p (l i) k")
            dve.memset(zrow[:], 0.0)
            dve.memset(epsb[:], 1e-8)
            dve.memset(diag[:].rearrange("p t b c -> p (t b c)"), 0.0)
            for a in range(2):
                for t in (x0[a], x1[a]):
                    dve.memset(t[:, 0:L + 2:L + 1].bitcast(F32), 0.0)
                for t in (x2[a], x3[a]):
                    dve.memset(t[:, :, 0:L + 2:L + 1].bitcast(F32), 0.0)
            dve.memset(cum[:].rearrange("p a e -> p (a e)"), 0.0)
            link(dve.memset(job_lists[:].rearrange("p n w -> p (n w)"), 0.0))
            dve.wait_ge(S["iota_done"], 8)
            link(dve.memset(listinit[:].rearrange("p n w -> p (n w)"), 0.0))
            dve.tensor_copy(listinit[:, :, 0].rearrange("p (n a) -> p n a", a=2),
                            pad_i[:].rearrange("p (n a) -> p n a", n=1).broadcast_to([P, E * COLS // 2, 2]))
            link(dve.tensor_copy(iota_e[:], iota_ei[:]))
            dve.tensor_copy(tok[:], tok_i[:])
            dve.tensor_scalar(region[:], iota_e[:], float(T), None, ALU.mult)
            link(dve.tensor_scalar(thresh[:], iota_e[:], float(JOB), None, ALU.mult))
            link(dve.memset(thresh[:, 0:1], -1.0))
            dve.memset(tsum[:], 0.0).then_inc(S["consts_done"], 1)

            dve.wait_ge(S["setup_loaded"], 16 * (NL * NB + 2 * NB + 4))
            for l in (0, 2):
                dve.tensor_copy(mats[:, TAP0[l]:TAP0[l] + 3, :], wnat[:, l].rearrange("p i k -> p k i"))
            w = lambda l, k: wnat[:, l, :, k]
            plans = []
            for dd in range(-3, 3):
                plans.append((TAP0[1] + dd + 3, 1, [(UPK[q], dd + q) for q in range(4) if 0 <= dd + q < K]))
            for q in range(6):
                plans.append((TAP0[3] + q, 3, [(BK[q - m], m) for m in range(K) if 0 <= q - m < 4]))
            for n in range(K):
                for at, l, terms in plans:
                    if n < len(terms):
                        c, k = terms[n]
                        if n == 0:
                            r = dve.tensor_scalar(mats[:, at, :], w(l, k), c, None, ALU.mult)
                        else:
                            r = dve.scalar_tensor_tensor(out=mats[:, at, :], in0=w(l, k), scalar=c, in1=mats[:, at, :],
                                                         op0=ALU.mult, op1=ALU.add)
                link(r)
            link(dve.tensor_tensor(wsq[:].rearrange("p l i k -> p (l i k)"), wnat[:].rearrange("p l i k -> p (l i k)"),
                                   wnat[:].rearrange("p l i k -> p (l i k)"), ALU.mult))
            link(dve.reduce_sum(mats[:, NT:NT + 4, :].rearrange("p l i -> p (l i)"), flat(wsq[:]), AX_X))
            for b in range(NB):
                r = dve.tensor_copy(diag[C * b:C * b + C, :, b, :], mats[C * b:C * b + C])
            r.then_inc(S["mats_ready"], 2)
            dve.wait_ge(S["modt_ready"], 1)
            dve.tensor_copy(styt[:], bank[6][0:SD, P:2 * P])
            dve.tensor_copy(modwt[:], bank[6][0:SD, 0:P].rearrange("d (l a c) -> d l a c", l=NL, a=1).broadcast_to([SD, NL, NB, C])).then_inc(S["modt_copied"], 1)
            dve.wait_ge(S["s_psum"], 1)
            for b in range(NB):
                q = slice(C * b, C * b + C)
                r = dve.tensor_tensor(s[q], bank[4][q].rearrange("p (l g r) -> p l g r", l=NL, r=NB)[:, :, :, b],
                                      modb[q].rearrange("p (l a) -> p l a", a=1).broadcast_to([C, NL, G]), ALU.add)
            link(r)
            link(dve.tensor_tensor(s2[:].rearrange("p l g -> p (l g)"), s[:].rearrange("p l g -> p (l g)"),
                                   s[:].rearrange("p l g -> p (l g)"), ALU.mult))
            dve.wait_ge(S["diag_t"], 4)
            dve.tensor_copy(wsqt[:].rearrange("p l m -> p (l m)"), bank[5][:]).then_inc(S["modt_copied"], 1)
            dve.wait_ge(S["sqrt_done"], 1)
            link(dve.reciprocal(d[:].rearrange("p l g -> p (l g)"), dv[:].rearrange("p l g -> p (l g)")))
            stt = dve.scalar_tensor_tensor
            stt(out=cA[:, 0, :], in0=d[:, 0, :], scalar=SCALE, in1=d[:, 1, :], op0=ALU.mult, op1=ALU.mult)
            stt(out=cA[:, 1, :], in0=s[:, 1, :], scalar=SCALE, in1=s[:, 2, :], op0=ALU.mult, op1=ALU.mult)
            stt(out=cA[:, 2, :], in0=d[:, 2, :], scalar=SCALE, in1=s[:, 3, :], op0=ALU.mult, op1=ALU.mult)
            dve.tensor_scalar(cA[:, 3, :], d[:, 3, :], SCALE, None, ALU.mult)
            dve.tensor_scalar(cB[:, 0, :], d[:, 1, :], cbias[:, 0:1], None, ALU.mult)
            dve.tensor_scalar(cB[:, 1, :], s[:, 2, :], cbias[:, 1:2], sum(UPK), ALU.mult, ALU.mult)
            dve.tensor_scalar(cB[:, 2, :], s[:, 3, :], cbias[:, 2:3], None, ALU.mult)
            dve.tensor_scalar(cB[:, 3, :], ones[:, 0:G], cbias[:, 3:4], None, ALU.mult)
            dve.tensor_scalar(edge[:], s[:, 2, :], cbias[:, 1:2], -UPK[0], ALU.mult, ALU.mult).then_inc(S["scales_ready"], 1)
            for n, (src, at, m) in enumerate(((bank[0], 0, 3), (bank[1], 9, 3), (bank[2], 12, 3), (bank[3], 15, 3), (None, 3, 6))):
                dve.wait_ge(S["wts_hi"], n + 1)
                a = diag[:, 3:9].rearrange("p t b c -> p (t b c)") if src is None else src[:, 0:m * P]
                dve.tensor_tensor(cwt[1][:, at:at + m, :].rearrange("p t m -> p (t m)"), a,
                                  cwt[0][:, at:at + m, :].rearrange("p t m -> p (t m)").bitcast(F32), ALU.subtract).then_inc(S["wts_lo"], 1)
            dve.wait_ge(S["wts_hi"], 6)
            dve.tensor_tensor(gwt[1][:].rearrange("p c e -> p (c e)"), bank[6][:, 0:HC * E],
                              gwt[0][:].rearrange("p c e -> p (c e)").bitcast(F32), ALU.subtract).then_inc(S["wts_lo"], 1)

            def weights_lo(n):
                for c in range(HC):
                    dve.wait_ge(S["w_hi"], n * (HC + IC) + (c + 1))
                    dve.tensor_tensor(wup[1][:, c, :], bank[WBANK[c]][:], wup[0][:, c, :].bitcast(F32), ALU.subtract).then_inc(S["w_lo"], 1)
                for c in range(IC):
                    dve.wait_ge(S["w_hi"], n * (HC + IC) + (HC + c + 1))
                    dve.tensor_tensor(wdn[1][:, c, :], bank[WBANK[HC + c]][:], wdn[0][:, c, :].bitcast(F32), ALU.subtract).then_inc(S["w_lo"], 1)

            weights_lo(0)
            dve.memset(tsum[:], 0.0).then_inc(S["pads_zero"], 1)

            base = [count[0], 0, None]

            def step(ins):
                base[1] += 1
                ins.then_inc(S["dve_step"], 1)
                dve.wait_ge(S["dve_step"], base[0] + base[1] if base[2] is None else base[2] + base[1])

            def split(hi, lo, src, ready):
                ins = dve.tensor_copy(hi, src)
                ins.then_inc(ready, 1)
                return lambda n: (dve.wait_ge(ready, n), dve.tensor_tensor(lo, src, hi.bitcast(F32), ALU.subtract).then_inc(ready, 1))

            def first_in(g, par, k):
                dve.wait_ge(S["x0_hi"], g + 1)
                dve.scalar_tensor_tensor(out=x0[1][:, 1:L + 1], in0=xraw[:, par, :], scalar=s[:, 0, bass.ds(g, 1)],
                                         in1=x0[0][:, 1:L + 1].bitcast(F32), op0=ALU.mult, op1=ALU.subtract).then_inc(S["x0_lo"], 1)

            def layer0(g):
                dve.wait_ge(S["t1_ready"], g + 1)
                split(x1[0][:, 1:L + 1], x1[1][:, 1:L + 1], t1[:], S["x1_ready"])(g * 2 + 1)

            def body(g, par, k, head=False, tail=0):
                if tail < 1:
                    first_in(g + 1, 1 - par, None)
                if tail < 2:
                    for ph in range(2):
                        dve.wait_ge(S["t2_ready"], g * 2 + (ph + 1))
                        at = t2[:, ph, 0:1] if ph == 0 else t2[:, ph, L - 1:L]
                        step(dve.tensor_tensor(at, at, edge[:, bass.ds(g, 1)], ALU.add))
                        split(x2[0][:, ph, 1:L + 1], x2[1][:, ph, 1:L + 1], t2[:, ph, :], S["x2_ready"])(g * 4 + (2 * ph + 1))
                if not head:
                    dve.wait_ge(S["xt_hi"], g)
                    dve.tensor_tensor(xt[1][:, 0].rearrange("p c t -> p (c t)"), bank[5][:],
                                      xt[0][:, 0].rearrange("p c t -> p (c t)").bitcast(F32), ALU.subtract).then_inc(S["xt_lo"], 1)
                if tail < 2:
                    for ph in range(2):
                        dve.wait_ge(S["t3_ready"], g * 2 + (ph + 1))
                        split(x3[0][:, ph, 1:L + 1], x3[1][:, ph, 1:L + 1], t3[:, ph, :], S["x3_ready"])(g * 4 + (2 * ph + 1))
                if not head:
                    dve.wait_ge(S["sg_ready"], g)
                    step(dve.tensor_tensor(z[:, 0, :], sg[:, 0, :], bank[6][:, 0:I], ALU.mult))
                    dve.tensor_tensor(z[:, 0, :], z[:, 0, :], bank[6][:, I:2 * I], ALU.mult).then_inc(S["z_ready"], 1)
                    dve.wait_ge(S["sig_ready"], g)
                    step(dve.tensor_tensor(sc[:], sig[:], biasrow[:], ALU.add))
                    land(dve)
                    step(dve.max(top[:], sc[:]))
                    dve.reduce_sum(tsum[:], top[:, 0:TOPK], AX_X)
                    step(dve.max_index(topi[:], top[:], sc[:]))
                    dve.tensor_scalar(tsum2[:], tsum[:], 1e-20, None, ALU.add)
                    step(dve.tensor_copy(topf[:], topi[:, 0:TOPK]))
                    dve.reciprocal(trec[:], tsum2[:])
                    step(dve.tensor_tensor(hot[:], iota_e[:].rearrange("p (a e) -> p a e", a=1).broadcast_to([P, TOPK, E]),
                                           topf[:].rearrange("p (k a) -> p k a", a=1).broadcast_to([P, TOPK, E]), ALU.is_equal))
                    dve.reduce_sum(mask[:], hot[:].rearrange("p k e -> p e k"), AX_X).then_inc(S["mask_ready"], 1)
                    if not (isinstance(g, int) and g < 3):
                        dve.wait_ge(S[f"scattered{1 - par}"], k * (16 * TOPK))
                    dve.tensor_scalar(entry[:, 1 - par, :, 1], top[:, 0:TOPK], trec[:], None, ALU.mult)
                    dve.tensor_copy(entry[:, 1 - par, :, 0], tok[:].broadcast_to([P, TOPK]))
                    dve.wait_ge(S["prefix_done"], g)
                    dve.tensor_tensor(cum[:, par, :], cum[:, 1 - par, :], mask[:], ALU.add)
                    step(dve.tensor_tensor(pos[:], bank[2][:, 0:E], region[:], ALU.add))
                    step(dve.tensor_tensor(hotpos[:], hot[:], pos[:].rearrange("p (a e) -> p a e", a=1).broadcast_to([P, TOPK, E]), ALU.mult))
                    dve.tensor_scalar(tok[:], tok[:], float(P), None, ALU.add)
                    step(dve.reduce_sum(key[:], hotpos[:], AX_X))
                    step(dve.tensor_copy(key_i[:], key[:]))
                    dve.tensor_scalar(lane_i[:], key_i[:], P - 1, 9, ALU.bitwise_and, ALU.logical_shift_left)
                    step(dve.tensor_scalar(col_i[:], key_i[:], 7, None, ALU.logical_shift_right))
                    land(dve)
                    dve.tensor_tensor(place[:, 1 - par, :], lane_i[:], col_i[:], ALU.add).then_inc(S["place_ready"], 1)
                    dve.wait_ge(S["zt_hi"], g)
                    dve.tensor_tensor(zt[1][:, 0].rearrange("p c t -> p (c t)"), bank[7][:, 0:I],
                                      zt[0][:, 0].rearrange("p c t -> p (c t)").bitcast(F32), ALU.subtract).then_inc(S["zt_lo"], 1)
                if tail < 1:
                    layer0(g + 1)
                if not head:
                    dve.wait_ge(S["down_done"], g)
                    dve.wait_ge(S[f"base_loaded{1 - par}"], (k + 1) * 16)
                    if not (isinstance(g, int) and g < 3):
                        dve.wait_ge(S[f"o_written{1 - par}"], k * 16)
                    dve.tensor_tensor(orow[:, 1 - par, :], xbase[:, 1 - par, :], bank[5][:], ALU.add).then_inc(S["o_ready"], 1)

            assert P * E * COLS == P << 9 and COLS * P == T and P == 1 << 7
            first_in(0, 0, None)
            layer0(0)
            body(0, 0, None, head=True)
            base[0], base[1] = base[0] + base[1], 0
            per_group = 13
            start = base[0]
            body(1, 1, 0)
            body(2, 0, 0)
            base[1] = 0
            with dve.Fori(1, (G - 4) // 2) as it:
                base[2] = it * (2 * per_group) + start
                body(it * 2 + 1, 1, it)
                assert base[1] == per_group, base[1]
                body(it * 2 + 2, 0, it)
            base[:] = [start + (G - 4) * per_group, 0, None]
            body(G - 3, 1, (G - 4) // 2)
            body(G - 2, 0, (G - 3) // 2)
            body(G - 1, 1, (G - 2) // 2, tail=1)
            body(G, 0, (G - 1) // 2, tail=2)
            count[0] = base[0] + base[1]

            dve.wait_ge(S["count_done"], 1)
            link(dve.tensor_copy(cnt[:], bank[2][:, 0:E]))
            link(dve.tensor_tensor(over[:], cnt[:].rearrange("p (e a) -> p e a", a=1).broadcast_to([P, E, E]),
                                   thresh[:].rearrange("p (a m) -> p a m", a=1).broadcast_to([P, E, E]), ALU.is_gt))
            link(dve.reduce_sum(njobs[:], over[:], AX_X))
            link(dve.memset(job0[:, 0:1], 0.0))
            for e in range(E):
                link(dve.tensor_tensor(job0[:, e + 1:e + 2], job0[:, e:e + 1], njobs[:, e:e + 1], ALU.add))
            dve.tensor_copy(job0_i[:], job0[:]).then_inc(S["jobs_ready"], 1)
            dve.wait_ge(S["lists_loaded"], 16)
            dve.wait_ge(S["jobs_ready"], 1)
            with dve.Fori(0, E) as e:
                first = dve.value_load(job0_i[0:1, bass.ds(e, 1)], min_val=0, max_val=TOPK * T // JOB + E)
                dve.tensor_copy(job_lists[:, bass.ds(first * 2, COLS), :], all_lists[:, bass.ds(e * COLS, COLS), :]).then_inc(S["dve_step"], 1)
                dve.wait_ge(S["dve_step"], e + (count[0] + 1))
            dve.tensor_copy(job_ids[:], job_lists[:, :, 0]).then_inc(S["job_lists_ready"], 2)

            def turned_in(j, u):
                dve.wait_ge(S["b_xt_hi"], j * 2 + (u + 1))
                dve.tensor_tensor(xt[1][:, u].rearrange("p c t -> p (c t)"), bank[4 + u][:],
                                  xt[0][:, u].rearrange("p c t -> p (c t)").bitcast(F32), ALU.subtract).then_inc(S["b_xt_lo"], 1)

            dve.memset(tsum[:], 0.0).then_inc(S["b_zt_lo"], 2)
            dve.memset(tsum2[:], 0.0).then_inc(S["b_y"], 2)
            for u in range(2):
                turned_in(0, u)
            count[0] += E
            with dve.Fori(0, E) as e:
                first = dve.value_load(job0_i[0:1, bass.ds(e, 1)], min_val=0, max_val=TOPK * T // JOB + E)
                end = dve.value_load(job0_i[0:1, bass.ds(e + 1, 1)], min_val=1, max_val=TOPK * T // JOB + E)
                weights_lo(e + 1)
                with dve.Fori(first, end) as j:
                    def weighted(u):
                        dve.wait_ge(S["b_down"], j * 2 + (u + 1))
                        dve.wait_ge(S["b_added"], 32 * (j + 1))
                        dve.tensor_scalar(yb[:, u, :], bank[6 + u][:], job_lists[:, bass.ds(j * 2 + u, 1), 1], None,
                                          ALU.mult).then_inc(S["b_y"], 1)

                    for u in range(2):
                        dve.wait_ge(S["b_sg"], j * 2 + (u + 1))
                        dve.tensor_tensor(z[:, u, :], sg[:, u, :], bank[u][:, 0:I], ALU.mult).then_inc(S["dve_step"], 1)
                        dve.wait_ge(S["dve_step"], j * 2 + (count[0] + u + 1))
                        dve.tensor_tensor(z[:, u, :], z[:, u, :], bank[u][:, I:2 * I], ALU.mult).then_inc(S["b_z"], 1)
                        dve.wait_ge(S["b_zt_hi"], j * 2 + (u + 1))
                        dve.tensor_tensor(zt[1][:, u].rearrange("p c t -> p (c t)"), bank[2 + u][:, 0:I],
                                          zt[0][:, u].rearrange("p c t -> p (c t)").bitcast(F32), ALU.subtract).then_inc(S["b_zt_lo"], 1)
                    weighted(0)
                    for u in range(2):
                        turned_in(j + 1, u)
                    weighted(1)

        @block.tensor
        def _(pe):
            pe.wait_ge(S["setup_loaded"], 16 * (NL * NB + 2 * NB + 4))
            pe.wait_ge(S["iota_done"], 8)
            pe.transpose(bank[6][0:SD, 0:P], modw[:], ident[:])
            pe.transpose(bank[6][0:SD, P:2 * P], sty[:], ident[:]).then_inc(S["modt_ready"], 1)
            pe.wait_ge(S["modt_copied"], 1)
            for l in range(NL):
                r = pe.matmul(bank[4][:, l * B:(l + 1) * B], modwt[:, l].rearrange("d a c -> d (a c)"), styt[:], start=True, stop=True)
            r.then_inc(S["s_psum"], 1)
            pe.wait_ge(S["mats_ready"], 2)
            for dst, at, n, done in ((0, 0, 3, 1), (1, 9, 3, 1), (2, 12, 3, 0), (3, 15, 3, 1), (5, NT, 4, 1)):
                for t in range(n):
                    r = pe.transpose(bank[dst][:, P * t:P * t + P], diag[:, at + t].rearrange("p b c -> p (b c)"), ident[:])
                if done:
                    r.then_inc(S["diag_t"], 1)
            for c in range(HC):
                r = pe.transpose(bank[6][:, c * E:(c + 1) * E], gnat[:, P * c:P * c + P], ident[0:E, 0:E])
            r.then_inc(S["gate_t"], 1)
            pe.wait_ge(S["modt_copied"], 2)
            for l in range(NL):
                r = pe.matmul(bank[5][:, l * G:(l + 1) * G], wsqt[:, l, :], s2[:, l, :], start=True, stop=True)
            r.then_inc(S["dem_psum"], 1)

            def turn_weights(n):
                pe.wait_ge(S["raw_loaded"], n * 48 + 48)
                for c in range(HC):
                    for m in range(2 * IC):
                        r = pe.transpose(bank[WBANK[c]][:, P * m:P * m + P], wraw[:, m, P * c:P * c + P], ident[:])
                    r.then_inc(S["w_t"], 1)
                for c in range(IC):
                    for m in range(HC):
                        r = pe.transpose(bank[WBANK[HC + c]][:, P * m:P * m + P], wdraw[:, m, P * c:P * c + P], ident[:])
                    r.then_inc(S["w_t"], 1)

            pe.wait_ge(S["wts_lo"], 6)
            pe.wait_ge(S["sqrt_done"], 1)
            turn_weights(0)

            def up(u, dst, c0, c1, first, last):
                for c in range(c0, c1):
                    r = mm3(pe, dst, [xt[a][:, u, c, :] for a in range(2)], [wup[a][:, c, :] for a in range(2)],
                            first and c == c0, last and c == c1 - 1)
                return r

            def down(u, dst):
                for c in range(IC):
                    r = mm3(pe, dst, [zt[a][:, u, c, :] for a in range(2)], [wdn[a][:, c, :] for a in range(2)],
                            c == 0, c == IC - 1)
                return r

            def turn_z(u, dst):
                for c in range(IC):
                    r = pe.transpose(dst[:, P * c:P * c + P], z[:, u, P * c:P * c + P], ident[:])
                return r

            def conv(dst, taps, done):
                for n, (t, planes, at) in enumerate(taps):
                    r = mm3(pe, dst, [cwt[a][:, t, :] for a in range(2)], [planes[a][:, at:at + L] for a in range(2)],
                            n == 0, n == len(taps) - 1)
                if done is not None:
                    r.then_inc(done, 1)

            def layer0(g):
                pe.wait_ge(S["x0_hi"], g + 1)
                pe.wait_ge(S["x0_lo"], g + 1)
                if isinstance(g, int) and g == 0:
                    pe.wait_ge(S["w_lo"], HC + IC)
                else:
                    pe.wait_ge(S["t1_ready"], g)
                conv(bank[0][:], [(k, x0, k) for k in range(K)], S["l0_done"])

            E2, O2 = [[t[:, ph] for t in x2] for ph in range(2)]
            E3, O3 = [[t[:, ph] for t in x3] for ph in range(2)]

            def body(g, par, k, head=False, tail=0):
                if tail < 2:
                    pe.wait_ge(S["x1_ready"], g * 2 + 2)
                    for ph in range(2):
                        if not head:
                            if ph == 0:
                                pe.wait_ge(S["h_ready"], g)
                            elif not (isinstance(g, int) and g == 1):
                                pe.wait_ge(S["place_ready"], g - 1)
                        conv(bank[1 + ph][:], [(TAP0[1] + 3 + ph - 1 - 2 * dk, x1, 1 + dk) for dk in (-1, 0, 1)], S["l1_done"])
                if not head:
                    pe.wait_ge(S["h_ready"], g)
                    if not (isinstance(g, int) and g == 1):
                        pe.wait_ge(S["o_ready"], g - 1)
                    for c in range(HC):
                        r = pe.transpose(bank[5][:, P * c:P * c + P], hrow[:, 1 - par, P * c:P * c + P], ident[:])
                    r.then_inc(S["xt_t"], 1)
                if tail < 2:
                    if not head:
                        pe.wait_ge(S["t3_ready"], g * 2)
                    pe.wait_ge(S["x2_ready"], g * 4 + 2)
                    w0, w1, w2 = (TAP0[2] + n for n in range(3))
                    for n, (t, planes, at) in enumerate(((w1, E2, 1),)):
                        mm3(pe, bank[3][:], [cwt[a][:, t, :] for a in range(2)], [planes[a][:, at:at + L] for a in range(2)], True, False)
                    for n, (t, planes, at) in enumerate(((w0, E2, 1), (w2, E2, 2))):
                        mm3(pe, bank[4][:], [cwt[a][:, t, :] for a in range(2)], [planes[a][:, at:at + L] for a in range(2)], n == 0, False)
                    pe.wait_ge(S["x2_ready"], g * 4 + 4)
                    for n, (t, planes, at) in enumerate(((w0, O2, 0), (w2, O2, 1))):
                        r = mm3(pe, bank[3][:], [cwt[a][:, t, :] for a in range(2)], [planes[a][:, at:at + L] for a in range(2)], False, n == 1)
                    r.then_inc(S["l2_done"], 1)
                    mm3(pe, bank[4][:], [cwt[a][:, w1, :] for a in range(2)], [O2[a][:, 1:1 + L] for a in range(2)], False, True).then_inc(S["l2_done"], 1)
                if not head:
                    pe.wait_ge(S["xt_hi"], g)
                    pe.wait_ge(S["xt_lo"], g)
                    if not (isinstance(g, int) and g == 1):
                        pe.wait_ge(S["z_ready"], g - 1)
                    up(0, bank[6][:], 0, HC, True, True).then_inc(S["up_done"], 1)
                    if tail < 2:
                        pe.wait_ge(S["t1_ready"], g + 1)
                    else:
                        pe.wait_ge(S["sig_ready"], g - 1)
                    for c in range(HC):
                        r = mm3(pe, bank[0][:, 0:E], [xt[a][:, 0, c, :] for a in range(2)], [gwt[a][:, c, :] for a in range(2)],
                                c == 0, c == HC - 1)
                    r.then_inc(S["logits_done"], 1)
                if tail < 2:
                    pe.wait_ge(S["t2_ready"], g * 2 + 1)
                    pe.wait_ge(S["x3_ready"], g * 4 + 2)
                    for n in range(3):
                        mm3(pe, bank[1][:], [cwt[a][:, TAP0[3] + 2 * n, :] for a in range(2)], [E3[a][:, n:n + L] for a in range(2)], n == 0, False)
                    pe.wait_ge(S["x3_ready"], g * 4 + 4)
                    for n in range(3):
                        r = mm3(pe, bank[1][:], [cwt[a][:, TAP0[3] + 2 * n + 1, :] for a in range(2)], [O3[a][:, n:n + L] for a in range(2)], False, n == 2)
                    r.then_inc(S["l3_done"], 1)
                if not head:
                    pe.wait_ge(S["mask_ready"], g)
                    if tail < 2:
                        pe.wait_ge(S["t2_ready"], g * 2 + 2)
                    pe.matmul(bank[2][:, 0:E], tri[:], mask[:], start=True, stop=False)
                    pe.matmul(bank[2][:, 0:E], ones[:], cum[:, 1 - par, :], start=False, stop=True).then_inc(S["prefix_done"], 1)
                    pe.wait_ge(S["z_ready"], g)
                    if not (isinstance(g, int) and g == 1):
                        pe.wait_ge(S["zt_lo"], g - 1)
                    turn_z(0, bank[7]).then_inc(S["zt_t"], 1)
                if tail < 1:
                    if not head:
                        pe.wait_ge(S["sig_ready"], g)
                    layer0(g + 1)
                if not head:
                    pe.wait_ge(S["zt_hi"], g)
                    pe.wait_ge(S["zt_lo"], g)
                    down(0, bank[5][:]).then_inc(S["down_done"], 1)

            layer0(0)
            body(0, 0, None, head=True)
            body(1, 1, None)
            body(2, 0, None)
            with pe.Fori(1, (G - 4) // 2) as it:
                body(it * 2 + 1, 1, None)
                body(it * 2 + 2, 0, None)
            body(G - 3, 1, None)
            body(G - 2, 0, None)
            body(G - 1, 1, None, tail=1)
            body(G, 0, None, tail=2)
            pe.wait_ge(S["place_ready"], G)
            pe.matmul(bank[2][:, 0:E], ones[:], cum[:, 0, :], start=True, stop=True).then_inc(S["count_done"], 1)

            def turn_in(j, u):
                pe.wait_ge(S[f"b_gathered{u}"], 16 * (j + 1))
                if isinstance(j, int):
                    pe.wait_ge(S["o_ready"], G)
                else:
                    pe.wait_ge(S["b_xt_lo"], j * 2 + (u - 1))
                for c in range(HC):
                    r = pe.transpose(bank[4 + u][:, P * c:P * c + P], xg[:, u, P * c:P * c + P], ident[:])
                r.then_inc(S["b_xt_t"], 1)

            for u in range(2):
                turn_in(0, u)
            pe.wait_ge(S["jobs_ready"], 1)
            with pe.Fori(0, E) as e:
                first = pe.value_load(job0_i[0:1, bass.ds(e, 1)], min_val=0, max_val=TOPK * T // JOB + E)
                end = pe.value_load(job0_i[0:1, bass.ds(e + 1, 1)], min_val=1, max_val=TOPK * T // JOB + E)
                pe.wait_ge(S["b_zt_lo"], first * 2 + 2)
                pe.wait_ge(S["b_y"], first * 2 + 2)
                turn_weights(e + 1)
                pe.wait_ge(S["w_lo"], (e + 1) * (HC + IC) + (HC + IC))
                land(pe)
                with pe.Fori(first, end) as j:
                    for u in range(2):
                        pe.wait_ge(S["b_xt_hi"], j * 2 + (u + 1))
                        pe.wait_ge(S["b_xt_lo"], j * 2 + (u + 1))
                        if u == 0:
                            up(0, bank[0][:], 0, HC, True, True).then_inc(S["b_up"], 1)
                    up(1, bank[1][:], 0, HC // 2, True, False)
                    pe.wait_ge(S["b_z"], j * 2 + 1)
                    turn_z(0, bank[2]).then_inc(S["b_zt_t"], 1)
                    up(1, bank[1][:], HC // 2, HC, False, True).then_inc(S["b_up"], 1)
                    pe.wait_ge(S["b_y"], j * 2 + 2)
                    pe.wait_ge(S["b_zt_hi"], j * 2 + 1)
                    pe.wait_ge(S["b_zt_lo"], j * 2 + 3)
                    down(0, bank[6][:]).then_inc(S["b_down"], 1)
                    pe.wait_ge(S["b_z"], j * 2 + 2)
                    turn_z(1, bank[3]).then_inc(S["b_zt_t"], 1)
                    for u in range(2):
                        turn_in(j + 1, u)
                    pe.wait_ge(S["b_zt_hi"], j * 2 + 2)
                    pe.wait_ge(S["b_zt_lo"], j * 2 + 4)
                    down(1, bank[7][:]).then_inc(S["b_down"], 1)


_INS = ["x", "cond_512", "L0_cond_weights", "L0_cond_biases", "L0_cond_mod_w", "L0_cond_mod_b", "L0_ffn_gate_w",
        "L0_ffn_bias", "L0_ffn_Wg", "L0_ffn_Wu", "L0_ffn_Wd", "L0_ffn_Sg", "L0_ffn_Su", "L0_ffn_Sd"]


def kernel(**inputs):
    import numpy as _np
    import concourse.bacc as _bacc
    from concourse import mybir as _mybir
    from concourse.bass_utils import run_bass_kernel_spmd as _run

    nc = _bacc.Bacc("TRN2", target_bir_lowering=False, num_devices=1)
    arrays, args = {}, []
    for name in _INS:
        a = _np.ascontiguousarray(inputs[name])
        arrays[f"in_{name}"] = a
        args.append(nc.dram_tensor(f"in_{name}", a.shape, _mybir.dt.from_np(a.dtype), kind="ExternalInput").ap())
    B, C, L = inputs["x"].shape
    out = nc.dram_tensor("out_rows", [B * C + 256, L], _mybir.dt.float32, kind="ExternalOutput").ap()
    mk_adaln_ffn(nc, *args, out)
    r = _run(nc, [arrays], core_ids=[0])
    return r.results[0]["out_rows"][:B * C].reshape(B, C, L)
```

```python
from contextlib import ExitStack

import concourse.bass as bass
from concourse import mybir

P = 128
F32 = mybir.dt.float32
F32R = mybir.dt.float32r
BF16 = mybir.dt.bfloat16
I32 = mybir.dt.int32
U32 = mybir.dt.uint32
ALU = mybir.AluOpType
ACT = mybir.ActivationFunctionType
AX_X = mybir.AxisListType.X



def mk_adaln_ffn(nc, x, style, cw, cb, mod_w, mod_b, gate_w, ebias, Wg, Wu, Wd, Sg, Su, Sd, out):
    B, C, L = x.shape
    NL, _, _, K = cw.shape
    SD = style.shape[1]
    E, I, H = Wg.shape
    TOPK = 4
    T = B * C
    G = T // P
    NB = P // C
    HC = H // P
    IC = I // P
    JOB = 2 * P
    MAXJOBS = T // JOB
    assert 2 * MAXJOBS == T // P
    COLS = T // P
    PAD = 2 * P
    TAPS = (3, 6, 3, 6)
    TAP0 = (0, 3, 9, 12)
    NT = sum(TAPS)
    SCALE = 1.0 / float(C * K * K) ** 0.5
    assert L == 512 and H == L and C * NB == P and 2 * I == 512 and NL == 4 and K == 3
    JOBS = TOPK * T // JOB + E
    WBANK = (2, 3, 6, 7, 0, 1)
    BK = (1 / 8, 3 / 8, 3 / 8, 1 / 8)
    UPK = tuple(2 * b for b in BK)

    x_rows = x.rearrange("b c l -> (b c) l")
    h_rows = nc.dram_tensor("h_rows", [T + PAD, H], F32, kind="Internal").ap()
    lists = nc.dram_tensor("lists", [P * E * COLS, 2], F32, kind="Internal").ap()

    with ExitStack() as ctx:
        def sb(name, shape, dt=F32):
            return ctx.enter_context(nc.sbuf_tensor(name, shape, dt))

        def sem(name):
            return ctx.enter_context(nc.semaphore(name))

        bank = [ctx.enter_context(nc.psum_tensor(f"bank{i}", [P, 512], F32)) for i in range(8)]

        ident = sb("ident", [P, P])
        tri = sb("tri", [P, P], BF16)
        ones = sb("ones", [P, P], BF16)
        iota_e = sb("iota_e", [P, E])
        iota_ei = sb("iota_ei", [P, E], I32)
        region = sb("region", [P, E])
        thresh = sb("thresh", [P, E])
        tok = sb("tok", [P, 1])
        tok_i = sb("tok_i", [P, 1], I32)
        pad_i = sb("pad_i", [P, 2], I32)
        wnat = sb("wnat", [P, NL, C, K])
        mats = sb("mats", [P, NT + 4, C])
        wsq = sb("wsq", [P, NL, C, K])
        diag = sb("diag", [P, NT + 4, NB, C])
        cwt = [sb("cwt_hi", [P, NT, P], F32R), sb("cwt_lo", [P, NT, P], F32R)]
        wsqt = sb("wsqt", [P, NL, P])
        modw = sb("modw", [P, SD])
        modwt = sb("modwt", [SD, NL, NB, C])
        sty = sb("sty", [P, SD])
        styt = sb("styt", [SD, B])
        modb = sb("modb", [P, NL])
        cbias = sb("cbias", [P, NL])
        s = sb("s", [P, NL, G])
        s2 = sb("s2", [P, NL, G])
        dv = sb("dv", [P, NL, G])
        d = sb("d", [P, NL, G])
        cA = sb("cA", [P, NL, G])
        cB = sb("cB", [P, NL, G])
        edge = sb("edge", [P, G])
        epsb = sb("epsb", [P, 1])
        biasrow = sb("biasrow", [P, E])
        gnat = sb("gnat", [E, H])
        gwt = sb("gwt", [P, HC, 2, E], F32R)
        listinit = sb("listinit", [P, E * COLS, 2])
        zrow = sb("zrow", [P, H])

        wraw = sb("wraw", [P, 2 * IC, H])
        wdraw = sb("wdraw", [P, HC, I])
        wup = [[sb(f"wup{b}_{x}", [P, HC, 2 * I], F32R) for x in ("hi", "lo")] for b in range(2)]
        wdn = [[sb(f"wdn{b}_{x}", [P, IC, H], F32R) for x in ("hi", "lo")] for b in range(2)]

        xraw = sb("xraw", [P, 2, L])
        xbase = sb("xbase", [P, 2, L])
        x0 = [sb("x0_hi", [P, L + 2], F32R), sb("x0_lo", [P, L + 2], F32R)]
        x1 = [sb("x1_hi", [P, L + 2], F32R), sb("x1_lo", [P, L + 2], F32R)]
        x2 = [sb("x2_hi", [P, 2, L + 2], F32R), sb("x2_lo", [P, 2, L + 2], F32R)]
        x3 = [sb("x3_hi", [P, 2, L + 2], F32R), sb("x3_lo", [P, 2, L + 2], F32R)]
        t1 = sb("t1", [P, L])
        t2 = sb("t2", [P, 2, L])
        t3 = sb("t3", [P, 2, L])
        hrow = sb("hrow", [P, 2, L])
        orow = sb("orow", [P, 2, L])
        xt = [sb("xt_hi", [P, 2, HC, P], F32R), sb("xt_lo", [P, 2, HC, P], F32R)]
        sg = sb("sg", [P, 2, I])
        z = sb("z", [P, 2, I])
        zt = [sb("zt_hi", [P, 2, IC, P], F32R), sb("zt_lo", [P, 2, IC, P], F32R)]
        logit = sb("logit", [P, E])
        lpart = sb("lpart", [P, E])
        sig = sb("sig", [P, E])
        sc = sb("sc", [P, E])
        top = sb("top", [P, 8])
        topi = sb("topi", [P, 8], U32)
        topf = sb("topf", [P, TOPK])
        tsum = sb("tsum", [P, 1])
        tsum2 = sb("tsum2", [P, 1])
        trec = sb("trec", [P, 1])
        hot = sb("hot", [P, TOPK, E])
        mask = sb("mask", [P, E], BF16)
        cum = sb("cum", [P, 2, E], BF16)
        pos = sb("pos", [P, E])
        hotpos = sb("hotpos", [P, TOPK, E])
        key = sb("key", [P, TOPK])
        key_i = sb("key_i", [P, TOPK], I32)
        lane_i = sb("lane_i", [P, TOPK], I32)
        col_i = sb("col_i", [P, TOPK], I32)
        place = sb("place", [P, 2, TOPK], I32)
        entry = sb("entry", [P, 2, TOPK, 2])
        cnt = sb("cnt", [P, E])
        over = sb("over", [P, E, E])
        njobs = sb("njobs", [P, E])
        before = sb("before", [P, E + 1, E])
        iota_b = sb("iota_b", [P, E + 1], I32)
        iota_bf = sb("iota_bf", [P, E + 1])
        spread = sb("spread", [P, 4, E + 1, E])
        job0 = sb("job0", [P, E + 1])
        rank = sb("rank", [P, E + 1])
        found = sb("found", [P, E + 1, E])
        order = sb("order", [P, E + 1])
        first = sb("first", [P, E + 1])
        beyond = sb("beyond", [P, E + 1])
        table = sb("table", [P, E + 1, 5], I32)
        ahalf = sb("ahalf", [P, E // 2])
        pairs = sb("pairs", [P, 1])
        meta = sb("meta", [P, 3], I32)
        all_lists = sb("all_lists", [P, E * COLS, 2])
        all_ids = sb("all_ids", [P, E * COLS], I32)
        gid = sb("gid", [P, 2, 1], I32)
        sid = sb("sid", [P, 2, 1], I32)
        sid_next = sb("sid_next", [P, 1], I32)
        xg = sb("xg", [P, 2, H])
        yb = sb("yb", [P, 2, H])

        names = ("setup_loaded iota_done consts_done dve_step mats_ready modt_ready modt_copied "
                 "s_psum diag_t wts_hi wts_lo dem_psum sqrt_done scales_ready gate_t "
                 "raw_loaded w_t w_hi w_lo pads_zero fill_written "
                 "x_loaded0 x_loaded1 base_loaded0 base_loaded1 x0_hi x0_lo "
                 "l0_done l1_done l2_done l3_done t1_ready t2_ready t3_ready h_ready "
                 "x1_ready x2_ready x3_ready xt_t xt_hi xt_lo up_done sg_ready z_ready "
                 "logits_done sig_ready mask_ready prefix_done place_ready zt_t zt_hi zt_lo down_done "
                 "o_ready h_written0 h_written1 o_written0 o_written1 scattered0 scattered1 "
                 "lists_loaded count_done table_ready ids_ready logit_ready "
                 "gather_id b_gathered0 b_gathered1 b_xt_t b_xt_hi b_xt_lo b_up b_sg b_z b_zt_t b_zt_hi b_zt_lo "
                 "b_down b_y scatter_id b_added0 b_added1 landed_pool landed_act landed_dve landed_pe landed_sp").split()
        S = {n: sem(n) for n in names}

        LANDS = {nc.gpsimd.engine: "pool", nc.scalar.engine: "act", nc.vector.engine: "dve", nc.tensor.engine: "pe"}

        def land(eng):
            eng.sem_inc(S[f"landed_{LANDS[eng.engine]}"], 1)

        def products(pe, hi, lo, hi_wait=None, lo_wait=None):
            for passes, wait in ((hi, hi_wait), (lo, lo_wait)):
                if wait is not None:
                    pe.wait_ge(*wait)
                for dst, a, b, start, stop in passes:
                    r = pe.matmul(dst, a, b, start=start, stop=stop)
            return r

        def in_passes(dst, fixed, data, fixed_first, first, last):
            order = (lambda f, x: (f, x)) if fixed_first else (lambda f, x: (x, f))
            hi = [(dst,) + order(f[a], x[0]) for f, x in zip(fixed, data) for a in range(2)]
            lo = [(dst,) + order(f[0], x[1]) for f, x in zip(fixed, data)]
            hi = [p + (first and n == 0, False) for n, p in enumerate(hi)]
            lo = [p + (False, last and n == len(lo) - 1) for n, p in enumerate(lo)]
            return hi, lo

        def in_lists(value, least, most):
            return nc.s_assert_within(value, least, most, skip_runtime_bounds_check_because=
                                      "an expert has at most MAXJOBS jobs, so its columns are its own in the lists")

        def routed(eng, expert):
            eng.wait_ge(S["table_ready"], 1)
            turns = eng.value_load(meta[0:1, 0:1], min_val=1, max_val=E // 2)
            experts = eng.value_load(meta[0:1, 1:2], min_val=1, max_val=E)
            with eng.Fori(0, turns) as p:
                for u in range(2):
                    i = p * 2 + u

                    def one():
                        first = eng.value_load(table[0:1, bass.ds(i, 1), 2], min_val=0, max_val=JOBS)
                        end = eng.value_load(table[0:1, bass.ds(i, 1), 3], min_val=1, max_val=JOBS)
                        expert(i, first, end, 1 - u)

                    if u == 0:
                        one()
                    else:
                        with eng.If(i < experts):
                            one()

        block = ctx.enter_context(nc.Block())

        @block.sync
        def _(sp):
            for l in range(NL):
                for b in range(NB):
                    sp.dma_start(wnat[C * b:C * b + C, l].rearrange("o i k -> o (i k)"),
                                 cw[l].rearrange("o i k -> o (i k)")).then_inc(S["setup_loaded"], 16)
            for b in range(NB):
                sp.dma_start(modb[C * b:C * b + C, :], mod_b.rearrange("l c -> c l"), allow_slow_non_contiguous=True).then_inc(S["setup_loaded"], 16)
                sp.dma_start(cbias[C * b:C * b + C, :], cb.rearrange("l c -> c l"), allow_slow_non_contiguous=True).then_inc(S["setup_loaded"], 16)
            sp.dma_start(modw[:], mod_w.rearrange("l c d -> (l c) d")).then_inc(S["setup_loaded"], 16)
            sp.dma_start(sty[:], style).then_inc(S["setup_loaded"], 16)
            sp.dma_start(gnat[:], gate_w).then_inc(S["setup_loaded"], 16)
            sp.dma_start(biasrow[:], ebias.rearrange("(a e) -> a e", a=1).broadcast_to([P, E])).then_inc(S["setup_loaded"], 16)
            sp.dma_start(wraw[:, 0:IC, :], Sg.rearrange("(m p) h -> p m h", p=P)).then_inc(S["raw_loaded"], 16)
            sp.dma_start(wraw[:, IC:, :], Su.rearrange("(m p) h -> p m h", p=P)).then_inc(S["raw_loaded"], 16)
            sp.dma_start(wdraw[:], Sd.rearrange("(m p) i -> p m i", p=P)).then_inc(S["raw_loaded"], 16)
            for g in range(2):
                sp.dma_start(xraw[:, g, :], x_rows[P * g:P * g + P, :]).then_inc(S[f"x_loaded{g}"], 16)
                sp.dma_start(xbase[:, g, :], x_rows[P * g:P * g + P, :]).then_inc(S[f"base_loaded{g}"], 16)
            sp.wait_ge(S["consts_done"], 1)
            for n in range(PAD // P):
                sp.dma_start(h_rows[T + P * n:T + P * n + P, :], zrow[:]).then_inc(S["fill_written"], 16)
            sp.dma_start(lists.rearrange("(p n) w -> p n w", p=P), listinit[:]).then_inc(S["fill_written"], 16)
            def body(g, par, k, head=False, tail=0):
                if tail < 2:
                    if tail < 1:
                        sp.wait_ge(S["x0_hi"], g + 1)
                        sp.wait_ge(S["x0_lo"], g + 1)
                        sp.dma_start(xraw[:, par, :], x_rows[bass.ds(P * (g + 2), P), :]).then_inc(S[f"x_loaded{par}"], 16)
                    sp.wait_ge(S["h_ready"], g + 1)
                    sp.dma_start(h_rows[bass.ds(P * g, P), :], hrow[:, par, :]).then_inc(S[f"h_written{par}"], 16)
                if not head:
                    sp.wait_ge(S["o_ready"], g)
                    sp.dma_start(out[bass.ds(P * (g - 1), P), :], orow[:, 1 - par, :]).then_inc(S[f"o_written{1 - par}"], 16)
                    if tail < 1:
                        sp.dma_start(xbase[:, 1 - par, :], x_rows[bass.ds(P * (g + 1), P), :]).then_inc(S[f"base_loaded{1 - par}"], 16)

            body(0, 0, 0, head=True)
            body(1, 1, None)
            body(2, 0, None)
            with sp.Fori(1, (G - 4) // 2) as it:
                for u in range(2):
                    body(it * 2 + (1 + u), (1 + u) % 2, None)
            body(G - 3, 1, None)
            body(G - 2, 0, None, tail=1)
            sp.dma_start(xbase[:, 1, :], x_rows[P * (G - 1):P * G, :]).then_inc(S["base_loaded1"], 16)
            body(G - 1, 1, None, tail=1)
            body(G, 0, None, tail=2)
            sp.wait_ge(S["scattered0"], 16 * TOPK * (G // 2))
            sp.wait_ge(S["scattered1"], 16 * TOPK * (G // 2))
            sp.dma_start(all_lists[:], lists.rearrange("(p n) w -> p n w", p=P)).then_inc(S["lists_loaded"], 16)

            def load_expert(i):
                number = sp.value_load(table[0:1, bass.ds(i, 1), 0], min_val=0, max_val=E - 1)
                sp.dma_start(wraw[:, 0:IC, :], Wg[bass.ds(number, 1)].rearrange("a (m p) h -> p (a m) h", p=P)).then_inc(S["raw_loaded"], 16)
                sp.dma_start(wraw[:, IC:, :], Wu[bass.ds(number, 1)].rearrange("a (m p) h -> p (a m) h", p=P)).then_inc(S["raw_loaded"], 16)
                sp.dma_start(wdraw[:], Wd[bass.ds(number, 1)].rearrange("a (m p) i -> p (a m) i", p=P)).then_inc(S["raw_loaded"], 16)

            sp.wait_ge(S["w_t"], HC + IC)
            sp.wait_ge(S["table_ready"], 1)
            load_expert(0)
            experts = sp.value_load(meta[0:1, 1:2], min_val=1, max_val=E)
            with sp.Fori(0, experts) as i:
                sp.wait_ge(S["w_t"], (i + 2) * (HC + IC))
                load_expert(i + 1)
            sp.wait_ge(S["raw_loaded"], (experts + 2) * 48)
            sp.sem_inc(S["landed_sp"], 1)

        @block.gpsimd
        def _(pool):
            pool.iota(iota_ei[:], pattern=[[1, E]], base=0, channel_multiplier=0).then_inc(S["iota_done"], 1)
            pool.iota(iota_b[:], pattern=[[1, E + 1]], base=0, channel_multiplier=0).then_inc(S["iota_done"], 1)
            pool.iota(tok_i[:], pattern=[[0, 1]], base=0, channel_multiplier=1).then_inc(S["iota_done"], 1)
            pool.iota(pad_i[:], pattern=[[P, 2]], base=T, channel_multiplier=1).then_inc(S["iota_done"], 1)
            pool.memset(ident[:], 0.0).then_inc(S["iota_done"], 1)
            pool.memset(tri[:], 1.0).then_inc(S["iota_done"], 1)
            pool.memset(ones[:], 1.0).then_inc(S["iota_done"], 1)
            pool.wait_ge(S["iota_done"], 7)
            pool.affine_select(out=ident[:], in_=ident[:], compare_op=ALU.not_equal, fill=1.0, base=0,
                               pattern=[[-1, P]], channel_multiplier=1).then_inc(S["iota_done"], 1)
            pool.affine_select(out=tri[:], in_=tri[:], compare_op=ALU.is_gt, fill=0.0, base=0,
                               pattern=[[1, P]], channel_multiplier=-1).then_inc(S["iota_done"], 1)
            pool.wait_ge(S["fill_written"], 16 * (PAD // P + 1))
            assert PAD // P == 2
            for n in range(PAD // P):
                pool.dma_start(out[T + P * n:T + P * n + P, :], zrow[:]).then_inc(S[f"b_added{n}"], 16)

            def scatter(g, par):
                pool.wait_ge(S["place_ready"], g + 1)
                land(pool)
                for k in range(TOPK):
                    pool.indirect_dma_start(
                        out=lists, out_offset=bass.IndirectOffsetOnAxis(ap=place[:, par, k:k + 1], axis=0),
                        in_=entry[:, par, k, :], in_offset=None).then_inc(S[f"scattered{par}"], 16)

            with pool.Fori(0, G // 2) as it:
                for u in range(2):
                    scatter(it * 2 + u, u)

            pool.wait_ge(S["table_ready"], 1)
            pool.wait_ge(S["ids_ready"], 1)
            pool.wait_ge(S["h_written0"], 16 * (G // 2))
            pool.wait_ge(S["h_written1"], 16 * (G // 2))

            def column(i):
                return pool.value_load(table[0:1, bass.ds(i, 1), 1], min_val=0, max_val=(E - 1) * COLS)

            def gather(u):
                pool.indirect_dma_start(out=xg[:, u, :], out_offset=None, in_=h_rows,
                                        in_offset=bass.IndirectOffsetOnAxis(ap=gid[:, u, :], axis=0)).then_inc(S[f"b_gathered{u}"], 16)

            start = column(0)
            for u in range(2):
                pool.tensor_copy(gid[:, u, :], all_ids[:, bass.ds(start + u, 1)]).then_inc(S["gather_id"], 1)
            pool.wait_ge(S["gather_id"], 2)
            for u in range(2):
                gather(u)
            pool.wait_ge(S["o_written0"], 16 * (G // 2))
            pool.wait_ge(S["o_written1"], 16 * (G // 2))

            def add(u):
                pool.indirect_dma_start(out=out, out_offset=bass.IndirectOffsetOnAxis(ap=sid[:, u, :], axis=0),
                                        in_=yb[:, u, :], in_offset=None, compute_op=ALU.add).then_inc(S[f"b_added{u}"], 16)

            def add_second(j):
                pool.wait_ge(S["scatter_id"], j * 3 + 1)
                land(pool)
                pool.tensor_copy(sid[:, 1, :], sid_next[:]).then_inc(S["scatter_id"], 1)
                pool.wait_ge(S["scatter_id"], j * 3 + 2)
                pool.wait_ge(S["b_y"], j * 2 + 2)
                land(pool)
                add(1)

            def job(j, here, ahead):
                for u in range(2):
                    pool.wait_ge(S[f"b_gathered{u}"], 16 * (j + 1))
                    land(pool)
                    pool.tensor_copy(gid[:, u, :], all_ids[:, bass.ds(ahead + u, 1)]).then_inc(S["gather_id"], 1)
                for u in range(2):
                    pool.wait_ge(S["gather_id"], j * 2 + (3 + u))
                    pool.wait_ge(S["b_xt_t"], j * 2 + (1 + u))
                    land(pool)
                    gather(u)
                add_second(j)
                pool.tensor_copy(sid_next[:], all_ids[:, bass.ds(here + 1, 1)]).then_inc(S["scatter_id"], 1)
                pool.wait_ge(S["b_added0"], 16 * (j + 1))
                land(pool)
                pool.tensor_copy(sid[:, 0, :], all_ids[:, bass.ds(here, 1)]).then_inc(S["scatter_id"], 1)
                pool.wait_ge(S["b_added1"], 16 * (j + 2))
                pool.wait_ge(S["scatter_id"], j * 3 + 4)
                pool.wait_ge(S["b_y"], j * 2 + 3)
                land(pool)
                add(0)

            pool.tensor_copy(sid_next[:], pad_i[:, 1:2]).then_inc(S["scatter_id"], 1)
            experts = pool.value_load(meta[0:1, 1:2], min_val=1, max_val=E)
            with pool.Fori(0, experts) as i:
                here, ahead = column(i), column(i + 1)
                first = pool.value_load(table[0:1, bass.ds(i, 1), 2], min_val=0, max_val=JOBS)
                last = pool.value_load(table[0:1, bass.ds(i, 1), 4], min_val=0, max_val=JOBS - 1)
                with pool.If(first < last):
                    with pool.Fori(first, last) as j:
                        at = in_lists((j - first) * 2 + here, 0, E * COLS - 4)
                        job(j, at, at + 2)
                job(last, in_lists((last - first) * 2 + here, 0, E * COLS - 2), ahead)
            jobs = pool.value_load(meta[0:1, 2:3], min_val=1, max_val=JOBS)
            add_second(jobs)
            pool.wait_ge(S["b_added0"], 16 * (jobs + 1))
            pool.wait_ge(S["b_added1"], 16 * (jobs + 2))
            pool.wait_ge(S["b_gathered0"], 16 * (jobs + 1))
            pool.wait_ge(S["b_gathered1"], 16 * (jobs + 1))

        @block.scalar
        def _(act):
            def weights_hi(n, b, c):
                dst = wup[b][0][:, c, :] if c < HC else wdn[b][0][:, c - HC, :]
                act.wait_ge(S["w_t"], n * (HC + IC) + (c + 1))
                act.activation(dst, bank[WBANK[c]][:], ACT.Copy).then_inc(S["w_hi"], 1)

            act.wait_ge(S["dem_psum"], 1)
            act.wait_ge(S["consts_done"], 1)
            act.activation(dv[:].rearrange("p l g -> p (l g)"), bank[5][:, 0:NL * G], ACT.Sqrt,
                           scale=SCALE * SCALE, bias=epsb[:]).then_inc(S["sqrt_done"], 1)
            for n in range(3):
                act.wait_ge(S["diag_t"], n + 1)
                dst = cwt[0][:, (0, 9, 12)[n]:(3, 12, 18)[n], :].rearrange("p t m -> p (t m)")
                if n < 2:
                    act.activation(dst, bank[n][:, 0:3 * P], ACT.Copy).then_inc(S["wts_hi"], 1)
                else:
                    act.activation(cwt[0][:, 12:15, :].rearrange("p t m -> p (t m)"), bank[2][:, 0:3 * P], ACT.Copy).then_inc(S["wts_hi"], 1)
                    act.activation(cwt[0][:, 15:18, :].rearrange("p t m -> p (t m)"), bank[3][:, 0:3 * P], ACT.Copy).then_inc(S["wts_hi"], 1)
            act.wait_ge(S["mats_ready"], 2)
            act.activation(cwt[0][:, 3:9, :].rearrange("p t m -> p (t m)"),
                           diag[:, 3:9].rearrange("p t b c -> p (t b c)"), ACT.Copy).then_inc(S["wts_hi"], 1)
            act.wait_ge(S["gate_t"], 1)
            act.activation(gwt[:, :, 0, :], bank[6][:, 0:HC * E].rearrange("p (c e) -> p c e", c=HC), ACT.Copy).then_inc(S["wts_hi"], 1)
            act.wait_ge(S["wts_hi"], 6)
            for c in range(HC + IC):
                weights_hi(0, 0, c)

            def first_in(g, par, k):
                act.wait_ge(S[f"x_loaded{par}"], 16 * (k + 1))
                land(act)
                act.activation(x0[0][:, 1:L + 1], xraw[:, par, :], ACT.Copy, scale=s[:, 0, bass.ds(g, 1)]).then_inc(S["x0_hi"], 1)

            def evac(g, src, dst, l, done):
                act.activation(dst, src, ACT.Identity, scale=cA[:, l, bass.ds(g, 1)], bias=cB[:, l, bass.ds(g, 1)]).then_inc(done, 1)

            def layer0(g):
                act.wait_ge(S["l0_done"], g + 1)
                if not (isinstance(g, int) and g == 0):
                    act.wait_ge(S["x1_ready"], g * 2)
                land(act)
                evac(g, bank[0][:], t1[:], 0, S["t1_ready"])

            def body(g, par, k, tail=0):
                early = isinstance(g, int)
                stage = not (early and g == 0)
                if tail < 1:
                    act.wait_ge(S["l0_done"], g + 1)
                    first_in(g + 1, 1 - par, k[1])
                if tail < 2:
                    for ph in range(2):
                        act.wait_ge(S["l1_done"], g * 2 + (ph + 1))
                        if stage:
                            act.wait_ge(S["x2_ready"], g * 4 - 2 + 2 * ph)
                        land(act)
                        evac(g, bank[1 + ph][:], t2[:, ph, :], 1, S["t2_ready"])
                if stage:
                    act.wait_ge(S["xt_t"], g)
                    act.activation(xt[0][:, 0].rearrange("p c t -> p (c t)"), bank[5][:], ACT.Copy).then_inc(S["xt_hi"], 1)
                if tail < 2:
                    for ph in range(2):
                        act.wait_ge(S["l2_done"], g * 2 + (ph + 1))
                        if stage:
                            act.wait_ge(S["x3_ready"], g * 4 - 2 + 2 * ph)
                        land(act)
                        evac(g, bank[3 + ph][:], t3[:, ph, :], 2, S["t3_ready"])
                if tail < 1:
                    layer0(g + 1)
                if stage:
                    act.wait_ge(S["up_done"], g)
                    if not (early and g == 1):
                        act.wait_ge(S["z_ready"], g - 1)
                    act.activation(sg[:, 0, :], bank[6][:, 0:I], ACT.Sigmoid).then_inc(S["sg_ready"], 1)
                if stage:
                    act.wait_ge(S["zt_t"], g)
                    act.activation(zt[0][:, 0].rearrange("p c t -> p (c t)"), bank[7][:, 0:I], ACT.Copy).then_inc(S["zt_hi"], 1)
                if tail < 2:
                    act.wait_ge(S["l3_done"], g + 1)
                    if not (early and g < 2):
                        act.wait_ge(S[f"h_written{par}"], k[0] * 16)
                        act.wait_ge(S["xt_t"], g - 1)
                    land(act)
                    evac(g, bank[1][:], hrow[:, par, :], 3, S["h_ready"])
                if stage:
                    act.wait_ge(S["logit_ready"], g)
                    if not (early and g == 1):
                        act.wait_ge(S["mask_ready"], g - 1)
                    act.activation(sig[:], logit[:], ACT.Sigmoid).then_inc(S["sig_ready"], 1)

            act.wait_ge(S["scales_ready"], 1)
            act.wait_ge(S["pads_zero"], 1)
            first_in(0, 0, 0)
            layer0(0)
            for g in range(3):
                body(g, g % 2, (g // 2, (g + 1) // 2))
            with act.Fori(0, (G - 6) // 2) as it:
                body(it * 2 + 3, 1, (it + 1, it + 2))
                body(it * 2 + 4, 0, (it + 2, it + 2))
            for g in range(G - 3, G + 1):
                body(g, g % 2, (g // 2, (g + 1) // 2), tail=max(0, g - G + 2))

            def turned_in(j, u):
                act.wait_ge(S["b_xt_t"], j * 2 + (u + 1))
                act.activation(xt[0][:, u].rearrange("p c t -> p (c t)"), bank[4 + u][:], ACT.Copy).then_inc(S["b_xt_hi"], 1)

            for c in range(HC + IC):
                weights_hi(1, 1, c)
            for u in range(2):
                turned_in(0, u)

            def job(j, ahead, b):
                def w(*chunks):
                    for c in chunks if ahead is not None else ():
                        weights_hi(ahead, 1 - b, c)

                def gate(u):
                    act.wait_ge(S["b_up"], j * 2 + (u + 1))
                    act.activation(sg[:, u, :], bank[u][:, 0:I], ACT.Sigmoid).then_inc(S["b_sg"], 1)

                def z_in(u):
                    act.wait_ge(S["b_zt_t"], j * 2 + (u + 1))
                    act.activation(zt[0][:, u].rearrange("p c t -> p (c t)"), bank[2 + u][:, 0:I], ACT.Copy).then_inc(S["b_zt_hi"], 1)

                w(0, 1)
                gate(0)
                w(2, 3)
                z_in(0)
                gate(1)
                turned_in(j + 1, 0)
                w(4)
                z_in(1)
                turned_in(j + 1, 1)
                w(5)

            def expert(i, first, end, b):
                job(first, i + 2, b)
                with act.If(first + 1 < end):
                    with act.Fori(first + 1, end) as j:
                        job(j, None, b)
                land(act)

            routed(act, expert)

        @block.vector
        def _(dve):
            count = [0]

            def link(ins):
                ins.then_inc(S["dve_step"], 1)
                count[0] += 1
                dve.wait_ge(S["dve_step"], count[0])

            flat = lambda a: a.rearrange("p l i k -> p (l i) k")
            dve.memset(zrow[:], 0.0)
            dve.memset(epsb[:], 1e-8)
            dve.memset(diag[:].rearrange("p t b c -> p (t b c)"), 0.0)
            for a in range(2):
                for t in (x0[a], x1[a]):
                    dve.memset(t[:, 0:L + 2:L + 1].bitcast(F32), 0.0)
                for t in (x2[a], x3[a]):
                    dve.memset(t[:, :, 0:L + 2:L + 1].bitcast(F32), 0.0)
            link(dve.memset(cum[:].rearrange("p a e -> p (a e)"), 0.0))
            dve.wait_ge(S["iota_done"], 9)
            link(dve.memset(listinit[:].rearrange("p n w -> p (n w)"), 0.0))
            dve.tensor_copy(listinit[:, :, 0].rearrange("p (n a) -> p n a", a=2),
                            pad_i[:].rearrange("p (n a) -> p n a", n=1).broadcast_to([P, E * COLS // 2, 2]))
            link(dve.tensor_copy(iota_e[:], iota_ei[:]))
            dve.tensor_copy(tok[:], tok_i[:])
            dve.tensor_scalar(region[:], iota_e[:], float(T), None, ALU.mult)
            link(dve.tensor_scalar(thresh[:], iota_e[:], float(JOB), None, ALU.mult))
            link(dve.tensor_copy(iota_bf[:], iota_b[:]))
            dve.tensor_tensor(before[:], iota_bf[:].rearrange("p (i a) -> p i a", a=1).broadcast_to([P, E + 1, E]),
                              iota_e[:].rearrange("p (a e) -> p a e", a=1).broadcast_to([P, E + 1, E]), ALU.is_gt)
            dve.memset(tsum[:], 0.0).then_inc(S["consts_done"], 1)

            dve.wait_ge(S["setup_loaded"], 16 * (NL * NB + 2 * NB + 4))
            for l in (0, 2):
                dve.tensor_copy(mats[:, TAP0[l]:TAP0[l] + 3, :], wnat[:, l].rearrange("p i k -> p k i"))
            w = lambda l, k: wnat[:, l, :, k]
            plans = []
            for dd in range(-3, 3):
                plans.append((TAP0[1] + dd + 3, 1, [(UPK[q], dd + q) for q in range(4) if 0 <= dd + q < K]))
            for q in range(6):
                plans.append((TAP0[3] + q, 3, [(BK[q - m], m) for m in range(K) if 0 <= q - m < 4]))
            for n in range(K):
                for at, l, terms in plans:
                    if n < len(terms):
                        c, k = terms[n]
                        if n == 0:
                            r = dve.tensor_scalar(mats[:, at, :], w(l, k), c, None, ALU.mult)
                        else:
                            r = dve.scalar_tensor_tensor(out=mats[:, at, :], in0=w(l, k), scalar=c, in1=mats[:, at, :],
                                                         op0=ALU.mult, op1=ALU.add)
                link(r)
            link(dve.tensor_tensor(wsq[:].rearrange("p l i k -> p (l i k)"), wnat[:].rearrange("p l i k -> p (l i k)"),
                                   wnat[:].rearrange("p l i k -> p (l i k)"), ALU.mult))
            link(dve.reduce_sum(mats[:, NT:NT + 4, :].rearrange("p l i -> p (l i)"), flat(wsq[:]), AX_X))
            for b in range(NB):
                r = dve.tensor_copy(diag[C * b:C * b + C, :, b, :], mats[C * b:C * b + C])
            r.then_inc(S["mats_ready"], 2)
            dve.wait_ge(S["modt_ready"], 1)
            dve.tensor_copy(styt[:], bank[6][0:SD, P:2 * P])
            dve.tensor_copy(modwt[:], bank[6][0:SD, 0:P].rearrange("d (l a c) -> d l a c", l=NL, a=1).broadcast_to([SD, NL, NB, C])).then_inc(S["modt_copied"], 1)
            dve.wait_ge(S["s_psum"], 1)
            for b in range(NB):
                q = slice(C * b, C * b + C)
                r = dve.tensor_tensor(s[q], bank[4][q].rearrange("p (l g r) -> p l g r", l=NL, r=NB)[:, :, :, b],
                                      modb[q].rearrange("p (l a) -> p l a", a=1).broadcast_to([C, NL, G]), ALU.add)
            link(r)
            link(dve.tensor_tensor(s2[:].rearrange("p l g -> p (l g)"), s[:].rearrange("p l g -> p (l g)"),
                                   s[:].rearrange("p l g -> p (l g)"), ALU.mult))
            dve.wait_ge(S["diag_t"], 4)
            dve.tensor_copy(wsqt[:].rearrange("p l m -> p (l m)"), bank[5][:]).then_inc(S["modt_copied"], 1)
            dve.wait_ge(S["sqrt_done"], 1)
            link(dve.reciprocal(d[:].rearrange("p l g -> p (l g)"), dv[:].rearrange("p l g -> p (l g)")))
            stt = dve.scalar_tensor_tensor
            stt(out=cA[:, 0, :], in0=d[:, 0, :], scalar=SCALE, in1=d[:, 1, :], op0=ALU.mult, op1=ALU.mult)
            stt(out=cA[:, 1, :], in0=s[:, 1, :], scalar=SCALE, in1=s[:, 2, :], op0=ALU.mult, op1=ALU.mult)
            stt(out=cA[:, 2, :], in0=d[:, 2, :], scalar=SCALE, in1=s[:, 3, :], op0=ALU.mult, op1=ALU.mult)
            dve.tensor_scalar(cA[:, 3, :], d[:, 3, :], SCALE, None, ALU.mult)
            dve.tensor_scalar(cB[:, 0, :], d[:, 1, :], cbias[:, 0:1], None, ALU.mult)
            dve.tensor_scalar(cB[:, 1, :], s[:, 2, :], cbias[:, 1:2], sum(UPK), ALU.mult, ALU.mult)
            dve.tensor_scalar(cB[:, 2, :], s[:, 3, :], cbias[:, 2:3], None, ALU.mult)
            dve.tensor_scalar(cB[:, 3, :], ones[:, 0:G], cbias[:, 3:4], None, ALU.mult)
            dve.tensor_scalar(edge[:], s[:, 2, :], cbias[:, 1:2], -UPK[0], ALU.mult, ALU.mult).then_inc(S["scales_ready"], 1)
            for n, (src, at, m) in enumerate(((bank[0], 0, 3), (bank[1], 9, 3), (bank[2], 12, 3), (bank[3], 15, 3), (None, 3, 6))):
                dve.wait_ge(S["wts_hi"], n + 1)
                a = diag[:, 3:9].rearrange("p t b c -> p (t b c)") if src is None else src[:, 0:m * P]
                dve.tensor_tensor(cwt[1][:, at:at + m, :].rearrange("p t m -> p (t m)"), a,
                                  cwt[0][:, at:at + m, :].rearrange("p t m -> p (t m)").bitcast(F32), ALU.subtract).then_inc(S["wts_lo"], 1)
            dve.wait_ge(S["wts_hi"], 6)
            dve.tensor_tensor(gwt[:, :, 1, :], bank[6][:, 0:HC * E].rearrange("p (c e) -> p c e", c=HC),
                              gwt[:, :, 0, :].bitcast(F32), ALU.subtract).then_inc(S["wts_lo"], 1)

            def weights_lo(n, b, c):
                dst = wup[b][1][:, c, :] if c < HC else wdn[b][1][:, c - HC, :]
                hi = wup[b][0][:, c, :] if c < HC else wdn[b][0][:, c - HC, :]
                dve.wait_ge(S["w_hi"], n * (HC + IC) + (c + 1))
                dve.tensor_tensor(dst, bank[WBANK[c]][:], hi.bitcast(F32), ALU.subtract).then_inc(S["w_lo"], 1)

            for c in range(HC + IC):
                weights_lo(0, 0, c)
            dve.memset(tsum[:], 0.0).then_inc(S["pads_zero"], 1)

            base = [count[0], 0, None]

            def step(ins):
                base[1] += 1
                ins.then_inc(S["dve_step"], 1)
                dve.wait_ge(S["dve_step"], base[0] + base[1] if base[2] is None else base[2] + base[1])

            def split(hi, lo, src, ready):
                ins = dve.tensor_copy(hi, src)
                ins.then_inc(ready, 1)
                return lambda n: (dve.wait_ge(ready, n), dve.tensor_tensor(lo, src, hi.bitcast(F32), ALU.subtract).then_inc(ready, 1))

            def first_in(g, par, k):
                dve.wait_ge(S["x0_hi"], g + 1)
                dve.scalar_tensor_tensor(out=x0[1][:, 1:L + 1], in0=xraw[:, par, :], scalar=s[:, 0, bass.ds(g, 1)],
                                         in1=x0[0][:, 1:L + 1].bitcast(F32), op0=ALU.mult, op1=ALU.subtract).then_inc(S["x0_lo"], 1)

            def layer0(g):
                dve.wait_ge(S["t1_ready"], g + 1)
                split(x1[0][:, 1:L + 1], x1[1][:, 1:L + 1], t1[:], S["x1_ready"])(g * 2 + 1)

            def body(g, par, k, tail=0):
                early = isinstance(g, int)
                stage = tail < 3 and not (early and g == 0)
                if tail < 1:
                    first_in(g + 1, 1 - par, None)
                if tail < 2:
                    for ph in range(2):
                        dve.wait_ge(S["t2_ready"], g * 2 + (ph + 1))
                        at = t2[:, ph, 0:1] if ph == 0 else t2[:, ph, L - 1:L]
                        step(dve.tensor_tensor(at, at, edge[:, bass.ds(g, 1)], ALU.add))
                        split(x2[0][:, ph, 1:L + 1], x2[1][:, ph, 1:L + 1], t2[:, ph, :], S["x2_ready"])(g * 4 + (2 * ph + 1))
                if stage:
                    dve.wait_ge(S["xt_hi"], g)
                    dve.tensor_tensor(xt[1][:, 0].rearrange("p c t -> p (c t)"), bank[5][:],
                                      xt[0][:, 0].rearrange("p c t -> p (c t)").bitcast(F32), ALU.subtract).then_inc(S["xt_lo"], 1)
                if not (early and g < 2):
                    dve.wait_ge(S["prefix_done"], g - 1)
                    dve.tensor_tensor(cum[:, 1 - par, :], cum[:, par, :], mask[:], ALU.add)
                    step(dve.tensor_tensor(pos[:], bank[7][:, 0:E], region[:], ALU.add))
                    step(dve.tensor_tensor(hotpos[:], hot[:], pos[:].rearrange("p (a e) -> p a e", a=1).broadcast_to([P, TOPK, E]), ALU.mult))
                    step(dve.reduce_sum(key[:], hotpos[:], AX_X))
                    step(dve.tensor_copy(key_i[:], key[:]))
                    dve.tensor_scalar(lane_i[:], key_i[:], P - 1, 9, ALU.bitwise_and, ALU.logical_shift_left)
                    step(dve.tensor_scalar(col_i[:], key_i[:], 7, None, ALU.logical_shift_right))
                    land(dve)
                    dve.tensor_tensor(place[:, par, :], lane_i[:], col_i[:], ALU.add).then_inc(S["place_ready"], 1)
                if tail < 2:
                    for ph in range(2):
                        dve.wait_ge(S["t3_ready"], g * 2 + (ph + 1))
                        split(x3[0][:, ph, 1:L + 1], x3[1][:, ph, 1:L + 1], t3[:, ph, :], S["x3_ready"])(g * 4 + (2 * ph + 1))
                if tail < 1:
                    layer0(g + 1)
                if stage:
                    dve.wait_ge(S["sg_ready"], g)
                    step(dve.tensor_tensor(z[:, 0, :], sg[:, 0, :], bank[6][:, 0:I], ALU.mult))
                    dve.tensor_tensor(z[:, 0, :], z[:, 0, :], bank[6][:, I:2 * I], ALU.mult).then_inc(S["z_ready"], 1)
                    dve.wait_ge(S["zt_hi"], g)
                    dve.tensor_tensor(zt[1][:, 0].rearrange("p c t -> p (c t)"), bank[7][:, 0:I],
                                      zt[0][:, 0].rearrange("p c t -> p (c t)").bitcast(F32), ALU.subtract).then_inc(S["zt_lo"], 1)
                    dve.wait_ge(S["logits_done"], g)
                    step(dve.tensor_copy(lpart[:], bank[0][:, E:2 * E]))
                    dve.tensor_tensor(logit[:], bank[0][:, 0:E], lpart[:], ALU.add).then_inc(S["logit_ready"], 1)
                    dve.wait_ge(S["sig_ready"], g)
                    step(dve.tensor_tensor(sc[:], sig[:], biasrow[:], ALU.add))
                    land(dve)
                    step(dve.max(top[:], sc[:]))
                    dve.reduce_sum(tsum[:], top[:, 0:TOPK], AX_X)
                    step(dve.max_index(topi[:], top[:], sc[:]))
                    dve.tensor_scalar(tsum2[:], tsum[:], 1e-20, None, ALU.add)
                    step(dve.tensor_copy(topf[:], topi[:, 0:TOPK]))
                    dve.reciprocal(trec[:], tsum2[:])
                    step(dve.tensor_tensor(hot[:], iota_e[:].rearrange("p (a e) -> p a e", a=1).broadcast_to([P, TOPK, E]),
                                           topf[:].rearrange("p (k a) -> p k a", a=1).broadcast_to([P, TOPK, E]), ALU.is_equal))
                    with nc.allow_low_precision(reason="zeros and ones"):
                        dve.reduce_sum(mask[:], hot[:].rearrange("p k e -> p e k"), AX_X).then_inc(S["mask_ready"], 1)
                    if not (early and g < 3):
                        dve.wait_ge(S[f"scattered{1 - par}"], k * (16 * TOPK))
                    dve.tensor_scalar(entry[:, 1 - par, :, 1], top[:, 0:TOPK], trec[:], None, ALU.mult)
                    step(dve.tensor_copy(entry[:, 1 - par, :, 0], tok[:].broadcast_to([P, TOPK])))
                    dve.tensor_scalar(tok[:], tok[:], float(P), None, ALU.add)
                    dve.wait_ge(S["down_done"], g)
                    dve.wait_ge(S[f"base_loaded{1 - par}"], (k + 1) * 16)
                    if not (early and g < 3):
                        dve.wait_ge(S[f"o_written{1 - par}"], k * 16)
                    dve.tensor_tensor(orow[:, 1 - par, :], xbase[:, 1 - par, :], bank[5][:], ALU.add).then_inc(S["o_ready"], 1)

            assert P * E * COLS == P << 9 and COLS * P == T and P == 1 << 7
            first_in(0, 0, None)
            layer0(0)
            for g in range(3):
                body(g, g % 2, (g - 1) // 2)
            start, base[1] = base[0] + base[1], 0
            per_group = 15
            with dve.Fori(0, (G - 6) // 2) as it:
                base[2] = it * (2 * per_group) + start
                body(it * 2 + 3, 1, it + 1)
                assert base[1] == per_group, base[1]
                body(it * 2 + 4, 0, it + 1)
            base[:] = [start + (G - 6) * per_group, 0, None]
            for g in range(G - 3, G + 2):
                body(g, g % 2, (g - 1) // 2, tail=max(0, g - G + 2))
            count[0] = base[0] + base[1]

            dve.wait_ge(S["count_done"], 1)
            wide = lambda a: a.rearrange("p (i a) -> p i a", a=1).broadcast_to([P, a.shape[1], E])
            rows = lambda a: a.rearrange("p (a e) -> p a e", a=1).broadcast_to([P, E + 1, E])
            link(dve.tensor_copy(cnt[:], bank[7][:, 0:E]))
            link(dve.tensor_tensor(over[:], wide(cnt[:]), thresh[:].rearrange("p (a m) -> p a m", a=1).broadcast_to([P, E, E]), ALU.is_gt))
            some = over[:, :, 0]
            dve.tensor_tensor(spread[:, 1], before[:], rows(some), ALU.mult)
            link(dve.reduce_sum(njobs[:], over[:], AX_X))
            dve.reduce_sum(rank[:], spread[:, 1], AX_X)
            link(dve.tensor_tensor(spread[:, 0], before[:], rows(njobs[:]), ALU.mult))
            dve.reduce_sum(job0[:], spread[:, 0], AX_X)
            link(dve.tensor_tensor(found[:], wide(iota_bf[:]), rows(rank[:, 0:E]), ALU.is_equal))
            dve.tensor_scalar(beyond[:], iota_bf[:], rank[:, E:E + 1], job0[:, E:E + 1], ALU.is_ge, ALU.mult)
            dve.tensor_scalar(ahalf[:], iota_e[:, 0:E // 2], 2.0, rank[:, E:E + 1], ALU.mult, ALU.is_lt)
            link(dve.tensor_tensor(found[:], found[:], rows(some), ALU.mult))
            dve.reduce_sum(pairs[:], ahalf[:], AX_X)
            dve.tensor_tensor(spread[:, 2], found[:], rows(iota_e[:]), ALU.mult)
            link(dve.tensor_tensor(spread[:, 3], found[:], rows(job0[:, 0:E]), ALU.mult))
            dve.reduce_sum(order[:], spread[:, 2], AX_X)
            link(dve.reduce_sum(first[:], spread[:, 3], AX_X))
            dve.tensor_copy(meta[:, 0:1], pairs[:])
            dve.tensor_copy(meta[:, 1:2], rank[:, E:E + 1])
            dve.tensor_copy(meta[:, 2:3], job0[:, E:E + 1])
            dve.tensor_copy(table[:, :, 0], order[:])
            dve.tensor_scalar(table[:, :, 1], order[:], float(COLS), None, ALU.mult)
            link(dve.tensor_tensor(first[:], first[:], beyond[:], ALU.add))
            dve.tensor_copy(table[:, :, 2], first[:])
            dve.tensor_scalar(table[:, 0:E, 4], first[:, 1:E + 1], 1.0, None, ALU.subtract)
            dve.tensor_copy(table[:, 0:E, 3], first[:, 1:E + 1]).then_inc(S["table_ready"], 1)
            dve.wait_ge(S["lists_loaded"], 16)
            dve.tensor_copy(all_ids[:], all_lists[:, :, 0]).then_inc(S["ids_ready"], 1)

            def turned_in(j, u):
                dve.wait_ge(S["b_xt_hi"], j * 2 + (u + 1))
                dve.tensor_tensor(xt[1][:, u].rearrange("p c t -> p (c t)"), bank[4 + u][:],
                                  xt[0][:, u].rearrange("p c t -> p (c t)").bitcast(F32), ALU.subtract).then_inc(S["b_xt_lo"], 1)

            dve.memset(tsum[:], 0.0).then_inc(S["b_zt_lo"], 2)
            dve.memset(yb[:, 1, :], 0.0).then_inc(S["b_y"], 2)
            for c in range(HC + IC):
                weights_lo(1, 1, c)
            for u in range(2):
                turned_in(0, u)

            def job(j, ahead, b, at):
                def w(*chunks):
                    for c in chunks if ahead is not None else ():
                        weights_lo(ahead, 1 - b, c)

                def glu(u):
                    dve.wait_ge(S["b_sg"], j * 2 + (u + 1))
                    dve.tensor_tensor(z[:, u, :], sg[:, u, :], bank[u][:, 0:I], ALU.mult).then_inc(S["dve_step"], 1)
                    dve.wait_ge(S["dve_step"], j * 2 + (count[0] + u + 1))
                    dve.tensor_tensor(z[:, u, :], z[:, u, :], bank[u][:, I:2 * I], ALU.mult).then_inc(S["b_z"], 1)

                def z_in(u):
                    dve.wait_ge(S["b_zt_hi"], j * 2 + (u + 1))
                    dve.tensor_tensor(zt[1][:, u].rearrange("p c t -> p (c t)"), bank[2 + u][:, 0:I],
                                      zt[0][:, u].rearrange("p c t -> p (c t)").bitcast(F32), ALU.subtract).then_inc(S["b_zt_lo"], 1)

                def weighted(u):
                    dve.wait_ge(S["b_down"], j * 2 + (u + 1))
                    dve.wait_ge(S[f"b_added{u}"], 16 * (j + 1 + u))
                    dve.tensor_scalar(yb[:, u, :], bank[6 + u][:], all_lists[:, bass.ds(at + u, 1), 1], None,
                                      ALU.mult).then_inc(S["b_y"], 1)

                w(0, 1)
                glu(0)
                w(2, 3)
                z_in(0)
                glu(1)
                turned_in(j + 1, 0)
                w(4)
                z_in(1)
                weighted(0)
                turned_in(j + 1, 1)
                w(5)
                weighted(1)

            def expert(i, first, end, b):
                at = dve.value_load(table[0:1, bass.ds(i, 1), 1], min_val=0, max_val=(E - 1) * COLS)
                job(first, i + 2, b, at)
                with dve.If(first + 1 < end):
                    with dve.Fori(first + 1, end) as j:
                        job(j, None, b, in_lists((j - first) * 2 + at, 0, E * COLS - 2))
                land(dve)

            routed(dve, expert)

        @block.tensor
        def _(pe):
            pe.wait_ge(S["setup_loaded"], 16 * (NL * NB + 2 * NB + 4))
            pe.wait_ge(S["iota_done"], 9)
            pe.transpose(bank[6][0:SD, 0:P], modw[:], ident[:])
            pe.transpose(bank[6][0:SD, P:2 * P], sty[:], ident[:]).then_inc(S["modt_ready"], 1)
            pe.wait_ge(S["modt_copied"], 1)
            for l in range(NL):
                r = pe.matmul(bank[4][:, l * B:(l + 1) * B], modwt[:, l].rearrange("d a c -> d (a c)"), styt[:], start=True, stop=True)
            r.then_inc(S["s_psum"], 1)
            pe.wait_ge(S["mats_ready"], 2)
            for dst, at, n, done in ((0, 0, 3, 1), (1, 9, 3, 1), (2, 12, 3, 0), (3, 15, 3, 1), (5, NT, 4, 1)):
                for t in range(n):
                    r = pe.transpose(bank[dst][:, P * t:P * t + P], diag[:, at + t].rearrange("p b c -> p (b c)"), ident[:])
                if done:
                    r.then_inc(S["diag_t"], 1)
            for c in range(HC):
                r = pe.transpose(bank[6][:, c * E:(c + 1) * E], gnat[:, P * c:P * c + P], ident[0:E, 0:E])
            r.then_inc(S["gate_t"], 1)
            pe.wait_ge(S["modt_copied"], 2)
            for l in range(NL):
                r = pe.matmul(bank[5][:, l * G:(l + 1) * G], wsqt[:, l, :], s2[:, l, :], start=True, stop=True)
            r.then_inc(S["dem_psum"], 1)

            def turn_weights(n, c):
                if c == 0:
                    pe.wait_ge(S["raw_loaded"], n * 48 + 48)
                for m in range(2 * IC if c < HC else HC):
                    src = wraw[:, m, P * c:P * c + P] if c < HC else wdraw[:, m, P * (c - HC):P * (c - HC) + P]
                    r = pe.transpose(bank[WBANK[c]][:, P * m:P * m + P], src, ident[:])
                r.then_inc(S["w_t"], 1)

            pe.wait_ge(S["wts_lo"], 6)
            pe.wait_ge(S["sqrt_done"], 1)
            for c in range(HC + IC):
                turn_weights(0, c)

            def expert_passes(u, x, w, chunks, dst):
                return in_passes(dst, [[w[a][:, c, :] for a in range(2)] for c in range(chunks)],
                                 [[x[a][:, u, c, :] for a in range(2)] for c in range(chunks)], False, True, True)

            def up(u, b, dst):
                return expert_passes(u, xt, wup[b], HC, dst)

            def down(u, b, dst):
                return expert_passes(u, zt, wdn[b], IC, dst)

            def turn_z(u, dst):
                for c in range(IC):
                    r = pe.transpose(dst[:, P * c:P * c + P], z[:, u, P * c:P * c + P], ident[:])
                return r

            def layer0(g):
                if isinstance(g, int) and g == 0:
                    pe.wait_ge(S["w_lo"], HC + IC)
                else:
                    pe.wait_ge(S["t1_ready"], g)
                products(pe, *taps(bank[0][:], [(k, x0, k) for k in range(K)]),
                         (S["x0_hi"], g + 1), (S["x0_lo"], g + 1)).then_inc(S["l0_done"], 1)

            E2, O2 = [[t[:, ph] for t in x2] for ph in range(2)]
            E3, O3 = [[t[:, ph] for t in x3] for ph in range(2)]

            def taps(dst, terms, first=True, last=True):
                return in_passes(dst, [[cwt[a][:, t, :] for a in range(2)] for t, _, _ in terms],
                                 [[planes[a][:, at:at + L] for a in range(2)] for _, planes, at in terms], True, first, last)

            def body(g, par, tail=0):
                early = isinstance(g, int)
                stage = tail < 3 and not (early and g == 0)
                if tail < 2:
                    if stage:
                        pe.wait_ge(S["h_ready"], g)
                        pe.wait_ge(S["t2_ready"], g * 2)
                    for ph in range(2):
                        products(pe, *taps(bank[1 + ph][:], [(TAP0[1] + 3 + ph - 1 - 2 * dk, x1, 1 + dk) for dk in (-1, 0, 1)]),
                                 (S["x1_ready"], g * 2 + 1), (S["x1_ready"], g * 2 + 2)).then_inc(S["l1_done"], 1)
                if stage:
                    pe.wait_ge(S["h_ready"], g)
                    if not (early and g == 1):
                        pe.wait_ge(S["o_ready"], g - 1)
                    for c in range(HC):
                        r = pe.transpose(bank[5][:, P * c:P * c + P], hrow[:, 1 - par, P * c:P * c + P], ident[:])
                    r.then_inc(S["xt_t"], 1)
                if not (early and g < 2):
                    pe.wait_ge(S["mask_ready"], g - 1)
                    pe.wait_ge(S["zt_lo"], g - 1)
                    pe.matmul(bank[7][:, 0:E], tri[:], mask[:], start=True, stop=False)
                    pe.matmul(bank[7][:, 0:E], ones[:], cum[:, par, :], start=False, stop=True).then_inc(S["prefix_done"], 1)
                if tail < 2:
                    if stage:
                        pe.wait_ge(S["t3_ready"], g * 2)
                    w0, w1, w2 = (TAP0[2] + n for n in range(3))
                    even = taps(bank[3][:], [(w1, E2, 1)], last=False), taps(bank[4][:], [(w0, E2, 1), (w2, E2, 2)], last=False)
                    odd = taps(bank[3][:], [(w0, O2, 0), (w2, O2, 1)], first=False), taps(bank[4][:], [(w1, O2, 1)], first=False)
                    products(pe, even[0][0] + even[1][0], even[0][1] + even[1][1],
                             (S["x2_ready"], g * 4 + 1), (S["x2_ready"], g * 4 + 2))
                    products(pe, *odd[0], (S["x2_ready"], g * 4 + 3), (S["x2_ready"], g * 4 + 4)).then_inc(S["l2_done"], 1)
                    products(pe, *odd[1]).then_inc(S["l2_done"], 1)
                if tail < 1:
                    if not (early and g < 2):
                        pe.wait_ge(S["logit_ready"], g - 1)
                    layer0(g + 1)
                if stage:
                    if not (early and g == 1):
                        pe.wait_ge(S["z_ready"], g - 1)
                    products(pe, *up(0, 0, bank[6][:]), (S["xt_hi"], g), (S["xt_lo"], g)).then_inc(S["up_done"], 1)
                if tail < 2:
                    pe.wait_ge(S["t2_ready"], g * 2 + 1)
                    products(pe, *taps(bank[1][:], [(TAP0[3] + 2 * n, E3, n) for n in range(3)], last=False),
                             (S["x3_ready"], g * 4 + 1), (S["x3_ready"], g * 4 + 2))
                if stage:
                    pe.wait_ge(S["z_ready"], g)
                    if not (early and g == 1):
                        pe.wait_ge(S["place_ready"], g - 1)
                    turn_z(0, bank[7]).then_inc(S["zt_t"], 1)
                if tail < 2:
                    products(pe, *taps(bank[1][:], [(TAP0[3] + 2 * n + 1, O3, n) for n in range(3)], first=False),
                             (S["x3_ready"], g * 4 + 3), (S["x3_ready"], g * 4 + 4)).then_inc(S["l3_done"], 1)
                if stage:
                    if tail < 1:
                        pe.wait_ge(S["t1_ready"], g + 2)
                    elif not (early and g == 1):
                        pe.wait_ge(S["logit_ready"], g - 1)
                    for c in range(HC):
                        if c == HC - 1:
                            for d_ in range(HC):
                                pe.matmul(bank[0][:, 0:E], xt[1][:, 0, d_, :], gwt[:, d_, 0, :], start=False, stop=False)
                        r = pe.matmul(bank[0][:, 0:2 * E], xt[0][:, 0, c, :], gwt[:, c].rearrange("p a e -> p (a e)"),
                                      start=c == 0, stop=c == HC - 1)
                    r.then_inc(S["logits_done"], 1)
                    products(pe, *down(0, 0, bank[5][:]), (S["zt_hi"], g), (S["zt_lo"], g)).then_inc(S["down_done"], 1)

            layer0(0)
            for g in range(3):
                body(g, g % 2)
            with pe.Fori(0, (G - 6) // 2) as it:
                body(it * 2 + 3, 1)
                body(it * 2 + 4, 0)
            body(G - 3, 1)
            body(G - 2, 0)
            body(G - 1, 1, tail=1)
            body(G, 0, tail=2)
            body(G + 1, 1, tail=3)
            pe.wait_ge(S["place_ready"], G)
            pe.matmul(bank[7][:, 0:E], ones[:], cum[:, G % 2, :], start=True, stop=True).then_inc(S["count_done"], 1)

            def turn_in(j, u):
                pe.wait_ge(S[f"b_gathered{u}"], 16 * (j + 1))
                if isinstance(j, int):
                    pe.wait_ge(S["o_ready"], G)
                else:
                    pe.wait_ge(S["b_xt_lo"], j * 2 + (u - 1))
                for c in range(HC):
                    r = pe.transpose(bank[4 + u][:, P * c:P * c + P], xg[:, u, P * c:P * c + P], ident[:])
                r.then_inc(S["b_xt_t"], 1)

            for c in range(HC + IC):
                turn_weights(1, c)
            for u in range(2):
                turn_in(0, u)
            pe.wait_ge(S["w_lo"], 2 * (HC + IC))

            def job(j, ahead, b):
                def w(*chunks):
                    for c in chunks if ahead is not None else ():
                        turn_weights(ahead, c)

                def w_taken(n):
                    if ahead is not None:
                        pe.wait_ge(S["w_lo"], ahead * (HC + IC) + n)

                pe.wait_ge(S["b_zt_lo"], j * 2 + 2)
                w(0, 1)
                products(pe, *up(0, b, bank[0][:]), (S["b_xt_hi"], j * 2 + 1), (S["b_xt_lo"], j * 2 + 1)).then_inc(S["b_up"], 1)
                pe.wait_ge(S["b_y"], j * 2 + 2)
                w(2, 3)
                of_hi, of_lo = up(1, b, bank[1][:])
                products(pe, of_hi, [], (S["b_xt_hi"], j * 2 + 2))
                w_taken(1)
                pe.wait_ge(S["b_z"], j * 2 + 1)
                turn_z(0, bank[2]).then_inc(S["b_zt_t"], 1)
                products(pe, [], of_lo, None, (S["b_xt_lo"], j * 2 + 2)).then_inc(S["b_up"], 1)
                turn_in(j + 1, 0)
                w(4)
                w_taken(3)
                products(pe, *down(0, b, bank[6][:]), (S["b_zt_hi"], j * 2 + 1), (S["b_zt_lo"], j * 2 + 3)).then_inc(S["b_down"], 1)
                pe.wait_ge(S["b_z"], j * 2 + 2)
                turn_z(1, bank[3]).then_inc(S["b_zt_t"], 1)
                turn_in(j + 1, 1)
                w(5)
                w_taken(4)
                products(pe, *down(1, b, bank[7][:]), (S["b_zt_hi"], j * 2 + 2), (S["b_zt_lo"], j * 2 + 4)).then_inc(S["b_down"], 1)
                w_taken(HC + IC)

            def expert(i, first, end, b):
                job(first, i + 2, b)
                with pe.If(first + 1 < end):
                    with pe.Fori(first + 1, end) as j:
                        job(j, None, b)
                land(pe)

            routed(pe, expert)


_INS = ["x", "cond_512", "L0_cond_weights", "L0_cond_biases", "L0_cond_mod_w", "L0_cond_mod_b", "L0_ffn_gate_w",
        "L0_ffn_bias", "L0_ffn_Wg", "L0_ffn_Wu", "L0_ffn_Wd", "L0_ffn_Sg", "L0_ffn_Su", "L0_ffn_Sd"]


def kernel(**inputs):
    import numpy as _np
    import concourse.bacc as _bacc
    from concourse import mybir as _mybir
    from concourse.bass_utils import run_bass_kernel_spmd as _run

    nc = _bacc.Bacc("TRN2", target_bir_lowering=False, num_devices=1)
    arrays, args = {}, []
    for name in _INS:
        a = _np.ascontiguousarray(inputs[name])
        arrays[f"in_{name}"] = a
        args.append(nc.dram_tensor(f"in_{name}", a.shape, _mybir.dt.from_np(a.dtype), kind="ExternalInput").ap())
    B, C, L = inputs["x"].shape
    out = nc.dram_tensor("out_rows", [B * C + 256, L], _mybir.dt.float32, kind="ExternalOutput").ap()
    mk_adaln_ffn(nc, *args, out)
    r = _run(nc, [arrays], core_ids=[0])
    return r.results[0]["out_rows"][:B * C].reshape(B, C, L)
```

```python
from contextlib import ExitStack

import concourse.bass as bass
from concourse import mybir

P = 128
F32 = mybir.dt.float32
F32R = mybir.dt.float32r
BF16 = mybir.dt.bfloat16
I32 = mybir.dt.int32
U32 = mybir.dt.uint32
ALU = mybir.AluOpType
ACT = mybir.ActivationFunctionType
AX_X = mybir.AxisListType.X



def mk_adaln_ffn(nc, x, style, cw, cb, mod_w, mod_b, gate_w, ebias, Wg, Wu, Wd, Sg, Su, Sd, out):
    B, C, L = x.shape
    NL, _, _, K = cw.shape
    SD = style.shape[1]
    E, I, H = Wg.shape
    TOPK = 4
    T = B * C
    G = T // P
    NB = P // C
    HC = H // P
    IC = I // P
    JOB = 2 * P
    MAXJOBS = T // JOB
    assert 2 * MAXJOBS == T // P
    COLS = T // P
    PAD = 2 * P
    TAPS = (3, 6, 3, 6)
    TAP0 = (0, 3, 9, 12)
    NT = sum(TAPS)
    UP, SAME, DOWN, SQ = K, K + 1, K + 3, K + 7
    NM = K + 7
    Q = P // C
    W = 2 * L // Q
    SCALE = 1.0 / float(C * K * K) ** 0.5
    assert L == 512 and H == L and C * NB == P and 2 * I == 512 and NL == 4 and K == 3
    JOBS = TOPK * T // JOB + E
    WBANK = (2, 3, 6, 7, 0, 2)
    EARLY_WBANK = ((2, 3, 6, 7, 4, 5), (1, 2, 3, 6, 0, 4))
    BK = (1 / 8, 3 / 8, 3 / 8, 1 / 8)
    UPK = tuple(2 * b for b in BK)

    x_rows = x.rearrange("b c l -> (b c) l")
    h_rows = nc.dram_tensor("h_rows", [T + PAD, H], F32, kind="Internal").ap()
    lists = nc.dram_tensor("lists", [P * E * COLS, 2], F32, kind="Internal").ap()

    with ExitStack() as ctx:
        def sb(name, shape, dt=F32):
            return ctx.enter_context(nc.sbuf_tensor(name, shape, dt))

        def sem(name):
            return ctx.enter_context(nc.semaphore(name))

        bank = [ctx.enter_context(nc.psum_tensor(f"bank{i}", [P, 512], F32)) for i in range(8)]

        ident = sb("ident", [P, P])
        tri = sb("tri", [P, P], BF16)
        ones = sb("ones", [P, P], BF16)
        iota_e = sb("iota_e", [P, E])
        iota_ei = sb("iota_ei", [P, E], I32)
        region = sb("region", [P, E])
        thresh = sb("thresh", [P, E])
        tok = sb("tok", [P, 1])
        tok_i = sb("tok_i", [P, 1], I32)
        pad_i = sb("pad_i", [P, 2], I32)
        wnat = sb("wnat", [P, NL, C, K])
        mats = sb("mats", [P, NT + 4, C])
        wsq = sb("wsq", [P, NL, C, K])
        big = sb("big", [P, NM + 4, Q, C])
        cwt = [sb("cwt_hi", [P, NM, P], F32R), sb("cwt_lo", [P, NM, P], F32R)]
        wsqt = sb("wsqt", [P, NL, P])
        modw = sb("modw", [P, SD])
        modwt = sb("modwt", [SD, NL, NB, C])
        sty = sb("sty", [P, SD])
        styt = sb("styt", [SD, B])
        modb = sb("modb", [P, NL])
        cbias = sb("cbias", [P, NL])
        s = sb("s", [P, NL, B])
        s2 = sb("s2", [P, NL, B])
        dv = sb("dv", [P, NL, B])
        d = sb("d", [P, NL, B])
        cA = sb("cA", [P, NL, B])
        cB = sb("cB", [P, NL, B])
        edge = sb("edge", [P, B])
        own = sb("own", [P, 3, G])
        epsb = sb("epsb", [P, 1])
        biasrow = sb("biasrow", [P, E])
        gnat = sb("gnat", [E, H])
        gwt = sb("gwt", [P, HC, 2, E], F32R)
        all_lists = sb("all_lists", [P, E * COLS, 2])
        zrow = sb("zrow", [P, H])

        wraw = sb("wraw", [P, 2 * IC, H])
        wdraw = sb("wdraw", [P, HC, I])
        wup = [[sb(f"wup{b}_{x}", [P, HC, 2 * I], F32R) for x in ("hi", "lo")] for b in range(2)]
        wdn = [[sb(f"wdn{b}_{x}", [P, IC, H], F32R) for x in ("hi", "lo")] for b in range(2)]

        xraw = sb("xraw", [P, 2, L])
        xbase = sb("xbase", [P, 2, L])
        x0 = [sb("x0_hi", [P, L + 2], F32R), sb("x0_lo", [P, L + 2], F32R)]
        x1p = sb("x1p", [P, 2, 2, L // 2], F32R)
        x1 = sb("x1", [P, 2, NB, W], F32R)
        x2 = [sb("x2_hi", [P, NB, W + 1], F32R), sb("x2_lo", [P, NB, W + 1], F32R)]
        x3 = [sb("x3_hi", [P, NB, W + 2], F32R), sb("x3_lo", [P, NB, W + 2], F32R)]
        t1 = sb("t1", [P, 2, L // 2])
        t2 = sb("t2", [P, NB, W])
        t3 = sb("t3", [P, NB, W + 1])
        hrow = sb("hrow", [P, 2, NB, L // Q])
        orow = sb("orow", [P, 2, L])
        xt = [sb("xt_hi", [P, 2, HC, P], F32R), sb("xt_lo", [P, 2, HC, P], F32R)]
        sg = sb("sg", [P, 2, I])
        z = sb("z", [P, 2, I])
        zt = [sb("zt_hi", [P, 2, IC, P], F32R), sb("zt_lo", [P, 2, IC, P], F32R)]
        logit = sb("logit", [P, E])
        lpart = sb("lpart", [P, E])
        sig = sb("sig", [P, E])
        sc = sb("sc", [P, E])
        top = sb("top", [P, 8])
        topi = sb("topi", [P, 8], U32)
        topf = sb("topf", [P, TOPK])
        tsum = sb("tsum", [P, 1])
        tsum2 = sb("tsum2", [P, 1])
        trec = sb("trec", [P, 1])
        hot = sb("hot", [P, TOPK, E])
        mask = sb("mask", [P, E], BF16)
        cum = sb("cum", [P, 2, E], BF16)
        pos = sb("pos", [P, E])
        hotpos = sb("hotpos", [P, TOPK, E])
        key = sb("key", [P, TOPK])
        key_i = sb("key_i", [P, TOPK], I32)
        lane_i = sb("lane_i", [P, TOPK], I32)
        col_i = sb("col_i", [P, TOPK], I32)
        place = sb("place", [P, 2, TOPK], I32)
        entry = sb("entry", [P, 2, TOPK, 2])
        cnt = sb("cnt", [P, E])
        over = sb("over", [P, E, E])
        njobs = sb("njobs", [P, E])
        before = sb("before", [P, E + 1, E])
        iota_b = sb("iota_b", [P, E + 1], I32)
        iota_bf = sb("iota_bf", [P, E + 1])
        spread = sb("spread", [P, 4, E + 1, E])
        job0 = sb("job0", [P, E + 1])
        rank = sb("rank", [P, E + 1])
        found = sb("found", [P, E + 1, E])
        order = sb("order", [P, E + 1])
        first = sb("first", [P, E + 1])
        beyond = sb("beyond", [P, E + 1])
        table = sb("table", [P, E + 1, 5], I32)
        ahalf = sb("ahalf", [P, E // 2])
        pairs = sb("pairs", [P, 1])
        meta = sb("meta", [P, 3], I32)
        all_ids = sb("all_ids", [P, E * COLS], I32)
        gid = sb("gid", [P, 2, 1], I32)
        sid = sb("sid", [P, 2, 1], I32)
        sid_next = sb("sid_next", [P, 2, 1], I32)
        xg = sb("xg", [P, 2, H])
        yb = sb("yb", [P, 2, H])

        names = ("style_loaded taps_loaded bias_loaded gate_loaded iota_done consts_done dve_step taps_ready mats_ready modt_ready modt_copied "
                 "s_psum diag_t wts_hi wts_lo dem_psum sqrt_done s_ready scales_ready gate_t "
                 "raw_loaded w_t w_hi w_lo fill_written "
                 "x_loaded0 x_loaded1 base_loaded0 base_loaded1 x0_hi x0_lo "
                 "l0_done l1_done l2_done l3_done t1_ready t2_ready t3_ready h_ready "
                 "x1_ready x1_stacked x2_ready x3_ready xt_t xt_hi xt_lo up_done sg_ready z_ready "
                 "logits_done sig_ready mask_ready prefix_done place_ready zt_t zt_hi zt_lo down_done "
                 "o_ready h_written0 h_written1 o_written0 o_written1 scattered0 scattered1 "
                 "lists_loaded count_done table_ready ids_ready logit_ready "
                 "gather_id b_gathered0 b_gathered1 b_xt_t b_xt_hi b_xt_lo b_up b_sg b_z b_zt_t b_zt_hi b_zt_lo "
                 "b_down b_y scatter_id b_added0 b_added1 landed_pool landed_act landed_dve landed_pe landed_sp").split()
        S = {n: sem(n) for n in names}

        LANDS = {nc.gpsimd.engine: "pool", nc.scalar.engine: "act", nc.vector.engine: "dve", nc.tensor.engine: "pe"}

        def land(eng):
            eng.sem_inc(S[f"landed_{LANDS[eng.engine]}"], 1)

        def hi_passes(pe, dst, terms):
            for n, (lhs, rhs, data_moves) in enumerate(terms):
                for a in range(2):
                    r = pe.matmul(dst, lhs[a if data_moves else 0], rhs[0 if data_moves else a],
                                  start=n == 0 and a == 0, stop=False)
            return r

        def lo_passes(pe, dst, terms, last=True):
            for n, (lhs, rhs, data_moves) in enumerate(terms):
                r = pe.matmul(dst, lhs[0 if data_moves else 1], rhs[1 if data_moves else 0],
                              start=False, stop=last and n == len(terms) - 1)
            return r

        def in_lists(value, least, most):
            return nc.s_assert_within(value, least, most, skip_runtime_bounds_check_because=
                                      "an expert has at most MAXJOBS jobs, so its columns are its own in the lists")

        def routed(eng, first_job, other_jobs):
            eng.wait_ge(S["table_ready"], 1)
            turns = eng.value_load(meta[0:1, 0:1], min_val=1, max_val=E // 2)
            experts = eng.value_load(meta[0:1, 1:2], min_val=1, max_val=E)
            with eng.Fori(0, turns) as p:
                first = eng.value_load(table[0:1, bass.ds(p * 2, 1), 2], min_val=0, max_val=JOBS)
                for u in range(2):
                    i = p * 2 + u

                    def one():
                        at = first_job(i, first, 1 - u)
                        end = eng.value_load(table[0:1, bass.ds(i, 1), 3], min_val=1, max_val=JOBS)
                        with eng.If(first + 1 < end):
                            other_jobs(first, end, at, 1 - u)
                        land(eng)
                        return end

                    if u == 0:
                        first = one()
                    else:
                        with eng.If(i < experts):
                            one()

        MATRICES = ((0, 0, K), (1, SAME, 2), (2, DOWN, 4), (None, UP, 1))

        def wbank(n, c):
            return bank[(EARLY_WBANK[n] if isinstance(n, int) else WBANK)[c]]

        def matrices(eng, blocks, copy):
            for q in blocks:
                rows = slice(C * q, C * q + C)
                copy(big[rows, 0:K, q, :], mats[rows, 0:K])
                copy(big[rows, SQ:SQ + 4, q, :], mats[rows, NT:NT + 4])
                lo, hi = max(0, 2 * q - 4), min(Q, 2 * q + 2)
                copy(big[rows, UP, lo:hi, :], mats[rows, TAP0[1] + 4 - 2 * q + lo:TAP0[1] + 4 - 2 * q + hi])
                for at, many, l, back in ((SAME, 2, 2, q), (DOWN, 4, 3, 2 * q + 1)):
                    for m in range(many):
                        lo, hi = max(0, back - Q * m), min(Q, back - Q * m + TAPS[l])
                        if lo < hi:
                            tap = TAP0[l] + Q * m - back
                            r = copy(big[rows, at + m, lo:hi, :], mats[rows, tap + lo:tap + hi])
            return r

        def of_matrices(src, at, m):
            return big[:, at:at + m].rearrange("p t q c -> p (t q c)") if src is None else bank[src][:, 0:m * P]

        block = ctx.enter_context(nc.Block())

        @block.sync
        def _(sp):
            sp.dma_start(modw[:], mod_w.rearrange("l c d -> (l c) d")).then_inc(S["style_loaded"], 16)
            sp.dma_start(sty[:], style).then_inc(S["style_loaded"], 16)
            for q in range(Q):
                sp.dma_start(wnat[C * q:C * q + C].rearrange("o l i k -> o l (i k)"),
                             cw.rearrange("l o i k -> o l (i k)")).then_inc(S["taps_loaded"], 16)
            sp.dma_start(xraw[:, 0, :], x_rows[0:P, :]).then_inc(S["x_loaded0"], 16)
            sp.dma_start(gnat[:], gate_w).then_inc(S["gate_loaded"], 16)
            sp.dma_start(wraw[:, 0:IC, :], Sg.rearrange("(m p) h -> p m h", p=P)).then_inc(S["raw_loaded"], 16)
            sp.dma_start(wraw[:, IC:, :], Su.rearrange("(m p) h -> p m h", p=P)).then_inc(S["raw_loaded"], 16)
            sp.dma_start(wdraw[:], Sd.rearrange("(m p) i -> p m i", p=P)).then_inc(S["raw_loaded"], 16)
            sp.dma_start(xraw[:, 1, :], x_rows[P:2 * P, :]).then_inc(S["x_loaded1"], 16)
            for g in range(2):
                sp.dma_start(xbase[:, g, :], x_rows[P * g:P * g + P, :]).then_inc(S[f"base_loaded{g}"], 16)
            sp.wait_ge(S["consts_done"], 1)
            for n in range(PAD // P):
                sp.dma_start(h_rows[T + P * n:T + P * n + P, :], zrow[:]).then_inc(S["fill_written"], 16)
            sp.dma_start(lists.rearrange("(p n) w -> p n w", p=P), all_lists[:]).then_inc(S["fill_written"], 16)
            def stack(g):
                sp.wait_ge(S["x1_ready"], g * 2 + 2)
                if not (isinstance(g, int) and g == 0):
                    sp.wait_ge(S["l1_done"], g * 2)
                for q, (plane, src, dst) in enumerate(((1, 0, 1), (0, 0, 0), (1, 0, 0), (0, 1, 0))):
                    n = W - src - dst
                    for b in range(NB):
                        sp.dma_start(x1[C * q:C * q + C, :, b, dst:dst + n].bitcast(F32),
                                     x1p[C * b:C * b + C, :, plane, src:src + n].bitcast(F32)).then_inc(S["x1_stacked"], 16)

            stack(0)
            sp.wait_ge(S["x0_hi"], 1)
            sp.wait_ge(S["x0_lo"], 1)
            sp.dma_start(xraw[:, 0, :], x_rows[P * 2:P * 3, :]).then_inc(S["x_loaded0"], 16)

            def body(g, par, k, head=False, tail=0):
                if tail < 2:
                    if tail < 1 or g < G - 1:
                        stack(g + 1)
                    if tail < 1 and not (isinstance(g, int) and g == G - 3):
                        sp.wait_ge(S["x0_hi"], g + 2)
                        sp.wait_ge(S["x0_lo"], g + 2)
                        sp.dma_start(xraw[:, 1 - par, :], x_rows[bass.ds(P * (g + 3), P), :]).then_inc(S[f"x_loaded{1 - par}"], 16)
                if not head:
                    sp.wait_ge(S["o_ready"], g)
                    sp.dma_start(out[bass.ds(P * (g - 1), P), :], orow[:, 1 - par, :]).then_inc(S[f"o_written{1 - par}"], 16)
                    if tail < 1:
                        sp.dma_start(xbase[:, 1 - par, :], x_rows[bass.ds(P * (g + 1), P), :]).then_inc(S[f"base_loaded{1 - par}"], 16)
                if tail < 2:
                    sp.wait_ge(S["h_ready"], g + 1)
                    for q in range(Q):
                        sp.dma_start(h_rows[bass.ds(P * g, P), q * (L // Q):(q + 1) * (L // Q)].rearrange("(b c) w -> c b w", b=NB),
                                     hrow[C * q:C * q + C, par]).then_inc(S[f"h_written{par}"], 16)

            def load_expert(number):
                sp.dma_start(wraw[:, 0:IC, :], Wg[bass.ds(number, 1)].rearrange("a (m p) h -> p (a m) h", p=P)).then_inc(S["raw_loaded"], 16)
                sp.dma_start(wraw[:, IC:, :], Wu[bass.ds(number, 1)].rearrange("a (m p) h -> p (a m) h", p=P)).then_inc(S["raw_loaded"], 16)
                sp.dma_start(wdraw[:], Wd[bass.ds(number, 1)].rearrange("a (m p) i -> p (a m) i", p=P)).then_inc(S["raw_loaded"], 16)

            body(0, 0, 0, head=True)
            body(1, 1, None)
            body(2, 0, None)
            sp.wait_ge(S["w_t"], HC + IC)
            load_expert(0)
            with sp.Fori(1, (G - 4) // 2) as it:
                for u in range(2):
                    body(it * 2 + (1 + u), (1 + u) % 2, None)
            body(G - 3, 1, None)
            body(G - 2, 0, None, tail=1)
            sp.dma_start(xbase[:, 1, :], x_rows[P * (G - 1):P * G, :]).then_inc(S["base_loaded1"], 16)
            body(G - 1, 1, None, tail=1)
            body(G, 0, None, tail=2)
            sp.wait_ge(S["scattered0"], 16 * TOPK * (G // 2))
            sp.wait_ge(S["scattered1"], 16 * TOPK * (G // 2))
            sp.dma_start(all_lists[:], lists.rearrange("(p n) w -> p n w", p=P)).then_inc(S["lists_loaded"], 16)

            sp.wait_ge(S["table_ready"], 1)
            experts = sp.value_load(meta[0:1, 1:2], min_val=1, max_val=E)
            with sp.Fori(0, experts) as i:
                sp.wait_ge(S["w_t"], (i + 2) * (HC + IC))
                load_expert(sp.value_load(table[0:1, bass.ds(i + 1, 1), 0], min_val=0, max_val=E - 1))
            sp.wait_ge(S["raw_loaded"], (experts + 2) * 48)
            sp.sem_inc(S["landed_sp"], 1)

        @block.gpsimd
        def _(pool):
            pool.iota(iota_ei[:], pattern=[[1, E]], base=0, channel_multiplier=0).then_inc(S["iota_done"], 1)
            pool.iota(iota_b[:], pattern=[[1, E + 1]], base=0, channel_multiplier=0).then_inc(S["iota_done"], 1)
            pool.iota(tok_i[:], pattern=[[0, 1]], base=0, channel_multiplier=1).then_inc(S["iota_done"], 1)
            pool.iota(pad_i[:], pattern=[[P, 2]], base=T, channel_multiplier=1).then_inc(S["iota_done"], 1)
            pool.memset(ident[:], 0.0).then_inc(S["iota_done"], 1)
            pool.memset(tri[:], 1.0).then_inc(S["iota_done"], 1)
            pool.memset(ones[:], 1.0).then_inc(S["iota_done"], 1)
            pool.wait_ge(S["iota_done"], 7)
            pool.affine_select(out=ident[:], in_=ident[:], compare_op=ALU.not_equal, fill=1.0, base=0,
                               pattern=[[-1, P]], channel_multiplier=1).then_inc(S["iota_done"], 1)
            pool.affine_select(out=tri[:], in_=tri[:], compare_op=ALU.is_gt, fill=0.0, base=0,
                               pattern=[[1, P]], channel_multiplier=-1).then_inc(S["iota_done"], 1)
            pool.wait_ge(S["fill_written"], 16 * (PAD // P + 1))
            assert PAD // P == 2
            for n in range(PAD // P):
                pool.dma_start(out[T + P * n:T + P * n + P, :], zrow[:]).then_inc(S[f"b_added{n}"], 16)

            def scatter(g, par):
                pool.wait_ge(S["place_ready"], g + 1)
                land(pool)
                for k in range(TOPK):
                    pool.indirect_dma_start(
                        out=lists, out_offset=bass.IndirectOffsetOnAxis(ap=place[:, par, k:k + 1], axis=0),
                        in_=entry[:, par, k, :], in_offset=None).then_inc(S[f"scattered{par}"], 16)

            with pool.Fori(0, G // 2) as it:
                for u in range(2):
                    scatter(it * 2 + u, u)

            pool.wait_ge(S["table_ready"], 1)
            pool.wait_ge(S["ids_ready"], 1)
            pool.wait_ge(S["h_written0"], 16 * Q * (G // 2))
            pool.wait_ge(S["h_written1"], 16 * Q * (G // 2))

            def column(i):
                return pool.value_load(table[0:1, bass.ds(i, 1), 1], min_val=0, max_val=(E - 1) * COLS)

            def gather(u):
                pool.indirect_dma_start(out=xg[:, u, :], out_offset=None, in_=h_rows,
                                        in_offset=bass.IndirectOffsetOnAxis(ap=gid[:, u, :], axis=0)).then_inc(S[f"b_gathered{u}"], 16)

            for u in range(2):
                pool.tensor_copy(gid[:, u, :], all_ids[:, u:u + 1]).then_inc(S["gather_id"], 1)
            pool.wait_ge(S["gather_id"], 2)
            for u in range(2):
                gather(u)
            pool.wait_ge(S["o_written0"], 16 * (G // 2))
            pool.wait_ge(S["o_written1"], 16 * (G // 2))

            def add(u):
                pool.indirect_dma_start(out=out, out_offset=bass.IndirectOffsetOnAxis(ap=sid[:, u, :], axis=0),
                                        in_=yb[:, u, :], in_offset=None, compute_op=ALU.add).then_inc(S[f"b_added{u}"], 16)

            def add_last(j):
                pool.wait_ge(S["b_added0"], 16 * (j + 1))
                pool.wait_ge(S["b_added1"], 16 * (j + 1))
                pool.wait_ge(S["scatter_id"], j * 4 + 2)
                land(pool)
                for u in range(2):
                    pool.tensor_copy(sid[:, u, :], sid_next[:, u, :]).then_inc(S["scatter_id"], 1)
                for u in range(2):
                    pool.wait_ge(S["scatter_id"], j * 4 + 4)
                    pool.wait_ge(S["b_y"], j * 2 + (1 + u))
                    land(pool)
                    add(u)

            def job(j, here, ahead):
                for u in range(2):
                    pool.wait_ge(S[f"b_gathered{u}"], 16 * (j + 1))
                    land(pool)
                    pool.tensor_copy(gid[:, u, :], all_ids[:, bass.ds(ahead + u, 1)]).then_inc(S["gather_id"], 1)
                for u in range(2):
                    pool.wait_ge(S["gather_id"], j * 2 + (3 + u))
                    pool.wait_ge(S["b_xt_t"], j * 2 + (1 + u))
                    land(pool)
                    gather(u)
                add_last(j)
                for u in range(2):
                    pool.tensor_copy(sid_next[:, u, :], all_ids[:, bass.ds(here + u, 1)]).then_inc(S["scatter_id"], 1)

            for u in range(2):
                pool.tensor_copy(sid_next[:, u, :], pad_i[:, u:u + 1]).then_inc(S["scatter_id"], 1)
            experts = pool.value_load(meta[0:1, 1:2], min_val=1, max_val=E)
            with pool.Fori(0, experts) as i:
                here, ahead = column(i), column(i + 1)
                first = pool.value_load(table[0:1, bass.ds(i, 1), 2], min_val=0, max_val=JOBS)
                last = pool.value_load(table[0:1, bass.ds(i, 1), 4], min_val=0, max_val=JOBS - 1)
                with pool.If(first < last):
                    with pool.Fori(first, last) as j:
                        at = in_lists((j - first) * 2 + here, 0, E * COLS - 4)
                        job(j, at, at + 2)
                job(last, in_lists((last - first) * 2 + here, 0, E * COLS - 2), ahead)
            jobs = pool.value_load(meta[0:1, 2:3], min_val=1, max_val=JOBS)
            add_last(jobs)
            pool.wait_ge(S["b_added0"], 16 * (jobs + 2))
            pool.wait_ge(S["b_added1"], 16 * (jobs + 2))
            pool.wait_ge(S["b_gathered0"], 16 * (jobs + 1))
            pool.wait_ge(S["b_gathered1"], 16 * (jobs + 1))

        @block.scalar
        def _(act):
            def weights_hi(n, b, c):
                dst = wup[b][0][:, c, :] if c < HC else wdn[b][0][:, c - HC, :]
                act.wait_ge(S["w_t"], n * (HC + IC) + (c + 1))
                act.activation(dst, wbank(n, c)[:], ACT.Copy).then_inc(S["w_hi"], 1)

            for q in range(Q):
                act.dma_start(modb[C * q:C * q + C, :], mod_b.rearrange("l c -> c l"), allow_slow_non_contiguous=True).then_inc(S["bias_loaded"], 16)
                act.dma_start(cbias[C * q:C * q + C, :], cb.rearrange("l c -> c l"), allow_slow_non_contiguous=True).then_inc(S["bias_loaded"], 16)
            act.dma_start(biasrow[:], ebias.rearrange("(a e) -> a e", a=1).broadcast_to([P, E])).then_inc(S["bias_loaded"], 16)
            act.wait_ge(S["taps_ready"], 1)
            matrices(act, range(Q // 2, Q), lambda dst, src: act.activation(dst, src, ACT.Copy)).then_inc(S["mats_ready"], 1)
            for n, (src, at, m) in enumerate(MATRICES):
                act.wait_ge(S["diag_t"], n + 1) if src is not None else act.wait_ge(S["mats_ready"], 2)
                act.activation(cwt[0][:, at:at + m, :].rearrange("p t m -> p (t m)"), of_matrices(src, at, m),
                               ACT.Copy).then_inc(S["wts_hi"], 1)

            def first_in(g, par, k):
                act.wait_ge(S[f"x_loaded{par}"], 16 * (k + 1))
                land(act)
                act.activation(x0[0][:, 1:L + 1], xraw[:, par, :], ACT.Copy, scale=own[:, 0, bass.ds(g, 1)]).then_inc(S["x0_hi"], 1)

            def evac(g, samples, src, dst, l, done):
                for n, b in enumerate(samples):
                    r = act.activation(dst[:, n], src[:, n], ACT.Identity, scale=cA[:, l, bass.ds(g * NB + b, 1)],
                                       bias=cB[:, l, bass.ds(g * NB + b, 1)])
                r.then_inc(done, 1)

            def layer0(g):
                act.wait_ge(S["l0_done"], g + 1)
                if not (isinstance(g, int) and g == 0):
                    act.wait_ge(S["x1_ready"], g * 2)
                land(act)
                act.activation(t1[:], bank[0][:].rearrange("p (w two) -> p two w", two=2), ACT.Identity,
                               scale=own[:, 1, bass.ds(g, 1)], bias=own[:, 2, bass.ds(g, 1)]).then_inc(S["t1_ready"], 1)

            def body(g, par, k, tail=0):
                early = isinstance(g, int)
                stage = not (early and g == 0)
                if stage:
                    act.wait_ge(S["xt_t"], g)
                    act.activation(xt[0][:, 0].rearrange("p q (b c) -> p q b c", b=NB),
                                   bank[5][:].rearrange("p (b q c) -> p q b c", b=NB, q=Q), ACT.Copy).then_inc(S["xt_hi"], 1)
                if tail < 1:
                    layer0(g + 1)
                if tail < 2:
                    for ph in range(2):
                        act.wait_ge(S["l1_done"], g * 2 + (ph + 1))
                        if stage:
                            act.wait_ge(S["x2_ready"], g * 4 - 2 + 2 * ph)
                        land(act)
                        evac(g, (2 * ph, 2 * ph + 1), bank[1 + ph][:].rearrange("p (b w) -> p b w", b=2),
                             t2[:, 2 * ph:2 * ph + 2, :], 1, S["t2_ready"])
                if tail < 1 and not (early and g == G - 2):
                    act.wait_ge(S["l0_done"], g + 2)
                    first_in(g + 2, par, k[0] + 1)
                if stage:
                    act.wait_ge(S["up_done"], g)
                    if not (early and g == 1):
                        act.wait_ge(S["z_ready"], g - 1)
                    act.activation(sg[:, 0, :], bank[6][:, 0:I], ACT.Sigmoid).then_inc(S["sg_ready"], 1)
                for ph in range(2):
                    if ph == 1 and stage:
                        act.wait_ge(S["zt_t"], g)
                        act.activation(zt[0][:, 0].rearrange("p c t -> p (c t)"), bank[7][:, 0:I], ACT.Copy).then_inc(S["zt_hi"], 1)
                    if tail < 2:
                        act.wait_ge(S["l2_done"], g * 2 + (ph + 1))
                        if stage:
                            act.wait_ge(S["x3_ready"], g * 4 - 2 + 2 * ph)
                        land(act)
                        evac(g, (2 * ph, 2 * ph + 1), bank[3 + ph][:].rearrange("p (b w) -> p b w", b=2),
                             t3[:, 2 * ph:2 * ph + 2, 1:W + 1], 2, S["t3_ready"])
                if stage:
                    act.wait_ge(S["logit_ready"], g)
                    if not (early and g == 1):
                        act.wait_ge(S["mask_ready"], g - 1)
                    act.activation(sig[:], logit[:], ACT.Sigmoid).then_inc(S["sig_ready"], 1)
                if tail < 2:
                    act.wait_ge(S["l3_done"], g + 1)
                    if not (early and g < 2):
                        act.wait_ge(S[f"h_written{par}"], k[0] * (16 * Q))
                        act.wait_ge(S["xt_t"], g - 1)
                    land(act)
                    evac(g, range(NB), bank[1][:].rearrange("p (b w) -> p b w", b=NB), hrow[:, par], 3, S["h_ready"])

            act.wait_ge(S["s_ready"], 1)
            first_in(0, 0, 0)
            act.wait_ge(S["dem_psum"], 1)
            act.activation(dv[:].rearrange("p l g -> p (l g)"), bank[4][:, 0:NL * B], ACT.Sqrt,
                           scale=SCALE * SCALE, bias=epsb[:]).then_inc(S["sqrt_done"], 1)
            act.wait_ge(S["gate_t"], 1)
            act.activation(gwt[:, :, 0, :], bank[6][:, 0:HC * E].rearrange("p (c e) -> p c e", c=HC), ACT.Copy).then_inc(S["wts_hi"], 1)
            act.wait_ge(S["scales_ready"], 1)
            layer0(0)
            first_in(1, 1, 0)
            for c in range(HC + IC):
                weights_hi(0, 0, c)
            act.wait_ge(S["scales_ready"], 2)
            for g in range(3):
                body(g, g % 2, (g // 2, (g + 1) // 2))
            with act.Fori(0, (G - 6) // 2) as it:
                body(it * 2 + 3, 1, (it + 1, it + 2))
                body(it * 2 + 4, 0, (it + 2, it + 2))
            for g in range(G - 3, G + 1):
                body(g, g % 2, (g // 2, (g + 1) // 2), tail=max(0, g - G + 2))

            for c in range(HC + IC):
                weights_hi(1, 1, c)

            def turned_in(j, u):
                act.wait_ge(S["b_xt_t"], j * 2 + (u + 1))
                act.activation(xt[0][:, u].rearrange("p c t -> p (c t)"), bank[4 + u][:], ACT.Copy).then_inc(S["b_xt_hi"], 1)

            for u in range(2):
                turned_in(0, u)

            def job(j, ahead, b):
                def w(*chunks):
                    for c in chunks if ahead is not None else ():
                        weights_hi(ahead, 1 - b, c)

                def gate(u):
                    act.wait_ge(S["b_up"], j * 2 + (u + 1))
                    act.activation(sg[:, u, :], bank[u][:, 0:I], ACT.Sigmoid).then_inc(S["b_sg"], 1)

                def z_in(u):
                    act.wait_ge(S["b_zt_t"], j * 2 + (u + 1))
                    act.activation(zt[0][:, u].rearrange("p c t -> p (c t)"), bank[2 + u][:, 0:I], ACT.Copy).then_inc(S["b_zt_hi"], 1)

                w(0, 1)
                gate(0)
                w(2, 3)
                z_in(0)
                gate(1)
                turned_in(j + 1, 0)
                w(4)
                z_in(1)
                w(5)
                turned_in(j + 1, 1)

            def first_job(i, first, b):
                job(first, i + 2, b)

            def other_jobs(first, end, at, b):
                with act.Fori(first + 1, end) as j:
                    job(j, None, b)

            routed(act, first_job, other_jobs)

        @block.vector
        def _(dve):
            count = [0]

            def link(ins):
                ins.then_inc(S["dve_step"], 1)
                count[0] += 1
                dve.wait_ge(S["dve_step"], count[0])

            flat = lambda a: a.rearrange("p l i k -> p (l i) k")
            dve.memset(zrow[:], 0.0)
            dve.memset(epsb[:], 1e-8)
            dve.memset(big[:].rearrange("p t b c -> p (t b c)"), 0.0)
            for a in range(2):
                dve.memset(x0[a][:, 0:L + 2:L + 1].bitcast(F32), 0.0)
                dve.memset(x1[:, a, :, 0:W:W - 1].bitcast(F32), 0.0)
                dve.memset(x2[a][:, :, W:W + 1].bitcast(F32), 0.0)
                dve.memset(x3[a][:, :, W + 1:W + 2].bitcast(F32), 0.0)
                dve.memset(x3[a][:, :, 0:1].bitcast(F32), 0.0)
            dve.memset(t3[:, :, 0:1], 0.0)
            link(dve.memset(cum[:].rearrange("p a e -> p (a e)"), 0.0))
            dve.wait_ge(S["iota_done"], 9)
            link(dve.memset(all_lists[:].rearrange("p n w -> p (n w)"), 0.0))
            dve.tensor_copy(all_lists[:, :, 0].rearrange("p (n a) -> p n a", a=2),
                            pad_i[:].rearrange("p (n a) -> p n a", n=1).broadcast_to([P, E * COLS // 2, 2]))
            link(dve.tensor_copy(iota_e[:], iota_ei[:]))
            dve.tensor_copy(tok[:], tok_i[:])
            dve.tensor_scalar(region[:], iota_e[:], float(T), None, ALU.mult)
            link(dve.tensor_scalar(thresh[:], iota_e[:], float(JOB), None, ALU.mult))
            link(dve.tensor_copy(iota_bf[:], iota_b[:]))
            dve.tensor_tensor(before[:], iota_bf[:].rearrange("p (i a) -> p i a", a=1).broadcast_to([P, E + 1, E]),
                              iota_e[:].rearrange("p (a e) -> p a e", a=1).broadcast_to([P, E + 1, E]), ALU.is_gt)
            dve.memset(tsum[:], 0.0).then_inc(S["consts_done"], 1)

            def owns(n, a):
                for b in range(NB):
                    rows = slice(C * b, C * b + C)
                    r = dve.tensor_copy(own[rows, n, :], a[rows, 0, :].rearrange("p (g b) -> p g b", b=NB)[:, :, b])
                return r

            dve.wait_ge(S["modt_ready"], 1)
            dve.tensor_copy(styt[:], bank[6][0:SD, P:2 * P])
            dve.tensor_copy(modwt[:], bank[6][0:SD, 0:P].rearrange("d (l a c) -> d l a c", l=NL, a=1).broadcast_to([SD, NL, NB, C])).then_inc(S["modt_copied"], 1)
            dve.wait_ge(S["taps_loaded"], 16 * Q)
            for l in (0, 2):
                dve.tensor_copy(mats[:, TAP0[l]:TAP0[l] + 3, :], wnat[:, l].rearrange("p i k -> p k i"))
            w = lambda l, k: wnat[:, l, :, k]
            plans = []
            for dd in range(-3, 3):
                plans.append((TAP0[1] + dd + 3, 1, [(UPK[q], dd + q) for q in range(4) if 0 <= dd + q < K]))
            for q in range(6):
                plans.append((TAP0[3] + q, 3, [(BK[q - m], m) for m in range(K) if 0 <= q - m < 4]))
            for n in range(K):
                for at, l, terms in plans:
                    if n < len(terms):
                        c, k = terms[n]
                        if n == 0:
                            r = dve.tensor_scalar(mats[:, at, :], w(l, k), c, None, ALU.mult)
                        else:
                            r = dve.scalar_tensor_tensor(out=mats[:, at, :], in0=w(l, k), scalar=c, in1=mats[:, at, :],
                                                         op0=ALU.mult, op1=ALU.add)
                link(r)
            link(dve.tensor_tensor(wsq[:].rearrange("p l i k -> p (l i k)"), wnat[:].rearrange("p l i k -> p (l i k)"),
                                   wnat[:].rearrange("p l i k -> p (l i k)"), ALU.mult))
            ins = dve.reduce_sum(mats[:, NT:NT + 4, :].rearrange("p l i -> p (l i)"), flat(wsq[:]), AX_X)
            link(ins)
            dve.memset(tsum[:], 0.0).then_inc(S["taps_ready"], 1)
            matrices(dve, range(Q // 2), dve.tensor_copy).then_inc(S["mats_ready"], 1)
            dve.wait_ge(S["s_psum"], 1)
            dve.wait_ge(S["bias_loaded"], 16 * (2 * Q + 1))
            link(dve.tensor_tensor(s[:], bank[4][:].rearrange("p (l b) -> p l b", l=NL),
                                   modb[:].rearrange("p (l a) -> p l a", a=1).broadcast_to([P, NL, B]), ALU.add))
            link(dve.tensor_tensor(s2[:], s[:], s[:], ALU.mult))
            owns(0, s).then_inc(S["s_ready"], 1)
            dve.wait_ge(S["diag_t"], 4)
            dve.tensor_copy(wsqt[:].rearrange("p l m -> p (l m)"), bank[5][:]).then_inc(S["modt_copied"], 1)
            for n, (src, at, m) in enumerate(MATRICES):
                dve.wait_ge(S["wts_hi"], n + 1)
                dve.tensor_tensor(cwt[1][:, at:at + m, :].rearrange("p t m -> p (t m)"), of_matrices(src, at, m),
                                  cwt[0][:, at:at + m, :].rearrange("p t m -> p (t m)").bitcast(F32), ALU.subtract).then_inc(S["wts_lo"], 1)
            def first_in(g, par, k):
                dve.wait_ge(S["x0_hi"], g + 1)
                dve.scalar_tensor_tensor(out=x0[1][:, 1:L + 1], in0=xraw[:, par, :], scalar=own[:, 0, bass.ds(g, 1)],
                                         in1=x0[0][:, 1:L + 1].bitcast(F32), op0=ALU.mult, op1=ALU.subtract).then_inc(S["x0_lo"], 1)

            first_in(0, 0, None)
            dve.wait_ge(S["sqrt_done"], 1)
            def inverse(l):
                return dve.reciprocal(d[:, l:l + 2].rearrange("p l g -> p (l g)"), dv[:, l:l + 2].rearrange("p l g -> p (l g)"))

            link(inverse(0))
            stt = dve.scalar_tensor_tensor
            stt(out=cA[:, 0, :], in0=d[:, 0, :], scalar=SCALE, in1=d[:, 1, :], op0=ALU.mult, op1=ALU.mult)
            link(dve.tensor_scalar(cB[:, 0, :], d[:, 1, :], cbias[:, 0:1], None, ALU.mult))
            owns(1, cA)
            owns(2, cB).then_inc(S["scales_ready"], 1)
            link(inverse(2))
            stt(out=cA[:, 1, :], in0=s[:, 1, :], scalar=SCALE, in1=s[:, 2, :], op0=ALU.mult, op1=ALU.mult)
            stt(out=cA[:, 2, :], in0=d[:, 2, :], scalar=SCALE, in1=s[:, 3, :], op0=ALU.mult, op1=ALU.mult)
            dve.tensor_scalar(cA[:, 3, :], d[:, 3, :], SCALE, None, ALU.mult)
            dve.tensor_scalar(cB[:, 1, :], s[:, 2, :], cbias[:, 1:2], sum(UPK), ALU.mult, ALU.mult)
            dve.tensor_scalar(cB[:, 2, :], s[:, 3, :], cbias[:, 2:3], None, ALU.mult)
            dve.tensor_scalar(cB[:, 3, :], ones[:, 0:B], cbias[:, 3:4], None, ALU.mult)
            link(dve.tensor_scalar(edge[:], s[:, 2, :], cbias[:, 1:2], -UPK[0], ALU.mult, ALU.mult))
            dve.memset(tsum[:], 0.0).then_inc(S["scales_ready"], 1)
            dve.wait_ge(S["wts_hi"], len(MATRICES) + 1)
            dve.tensor_tensor(gwt[:, :, 1, :], bank[6][:, 0:HC * E].rearrange("p (c e) -> p c e", c=HC),
                              gwt[:, :, 0, :].bitcast(F32), ALU.subtract).then_inc(S["wts_lo"], 1)

            def weights_lo(n, b, c):
                dst = wup[b][1][:, c, :] if c < HC else wdn[b][1][:, c - HC, :]
                hi = wup[b][0][:, c, :] if c < HC else wdn[b][0][:, c - HC, :]
                dve.wait_ge(S["w_hi"], n * (HC + IC) + (c + 1))
                dve.tensor_tensor(dst, wbank(n, c)[:], hi.bitcast(F32), ALU.subtract).then_inc(S["w_lo"], 1)

            base = [count[0], 0, None]

            def step(ins):
                base[1] += 1
                ins.then_inc(S["dve_step"], 1)
                dve.wait_ge(S["dve_step"], base[0] + base[1] if base[2] is None else base[2] + base[1])

            def minus(lo, src, hi):
                return dve.tensor_tensor(lo, src, hi.bitcast(F32), ALU.subtract)

            def layer0(g):
                dve.wait_ge(S["t1_ready"], g + 1)
                if not (isinstance(g, int) and g == 0):
                    dve.wait_ge(S["x1_stacked"], g * (16 * Q * NB))
                dve.tensor_copy(x1p[:, 0], t1[:]).then_inc(S["x1_ready"], 1)
                dve.wait_ge(S["x1_ready"], g * 2 + 1)
                minus(x1p[:, 1], t1[:], x1p[:, 0]).then_inc(S["x1_ready"], 1)

            def body(g, par, k, tail=0):
                early = isinstance(g, int)
                stage = tail < 3 and not (early and g == 0)
                if not (early and g < 2):
                    dve.wait_ge(S["prefix_done"], g - 1)
                    dve.tensor_tensor(cum[:, 1 - par, :], cum[:, par, :], mask[:], ALU.add)
                    step(dve.tensor_tensor(pos[:], bank[7][:, 0:E], region[:], ALU.add))
                    step(dve.tensor_tensor(hotpos[:], hot[:], pos[:].rearrange("p (a e) -> p a e", a=1).broadcast_to([P, TOPK, E]), ALU.mult))
                    step(dve.reduce_sum(key[:], hotpos[:], AX_X))
                    step(dve.tensor_copy(key_i[:], key[:]))
                    dve.tensor_scalar(lane_i[:], key_i[:], P - 1, 9, ALU.bitwise_and, ALU.logical_shift_left)
                    step(dve.tensor_scalar(col_i[:], key_i[:], 7, None, ALU.logical_shift_right))
                    land(dve)
                    dve.tensor_tensor(place[:, par, :], lane_i[:], col_i[:], ALU.add).then_inc(S["place_ready"], 1)
                if stage:
                    dve.wait_ge(S["xt_hi"], g)
                    turned = lambda a: a[:, 0].rearrange("p q (b c) -> p q b c", b=NB)
                    dve.tensor_tensor(turned(xt[1]), bank[5][:].rearrange("p (b q c) -> p q b c", b=NB, q=Q),
                                      turned(xt[0]).bitcast(F32), ALU.subtract).then_inc(S["xt_lo"], 1)
                if tail < 1:
                    layer0(g + 1)
                if tail < 2:
                    for ph in range(2):
                        dve.wait_ge(S["t2_ready"], g * 2 + (ph + 1))
                        two = slice(2 * ph, 2 * ph + 2)
                        for q, w in ((0, 0), (Q - 1, W - 1)):
                            at = t2[C * q:C * q + C, two, w]
                            r = dve.tensor_tensor(at, at, edge[C * q:C * q + C, bass.ds(g * NB + 2 * ph, 2)], ALU.add)
                        step(r)
                        dve.tensor_copy(x2[0][:, two, 0:W], t2[:, two, :]).then_inc(S["x2_ready"], 1)
                        dve.wait_ge(S["x2_ready"], g * 4 + (2 * ph + 1))
                        minus(x2[1][:, two, 0:W], t2[:, two, :], x2[0][:, two, 0:W]).then_inc(S["x2_ready"], 1)
                if stage:
                    dve.wait_ge(S["sg_ready"], g)
                    step(dve.tensor_tensor(z[:, 0, :], sg[:, 0, :], bank[6][:, 0:I], ALU.mult))
                    dve.tensor_tensor(z[:, 0, :], z[:, 0, :], bank[6][:, I:2 * I], ALU.mult).then_inc(S["z_ready"], 1)
                for ph in range(2):
                    if ph == 1 and stage:
                        dve.wait_ge(S["zt_hi"], g)
                        dve.tensor_tensor(zt[1][:, 0].rearrange("p c t -> p (c t)"), bank[7][:, 0:I],
                                          zt[0][:, 0].rearrange("p c t -> p (c t)").bitcast(F32), ALU.subtract).then_inc(S["zt_lo"], 1)
                    if tail < 2:
                        two = slice(2 * ph, 2 * ph + 2)
                        last = slice(P - C, P)
                        cols = slice(1 - ph, W + 1)
                        if ph == 1:
                            samples = bass.ds(g * NB, NB)
                            dve.wait_ge(S["l2_done"], g * 2 + 2)
                            step(dve.tensor_tensor(t3[last, :, 0], bank[1][last, 0:NB], cA[last, 2, samples], ALU.mult))
                            dve.tensor_tensor(t3[last, :, 0], t3[last, :, 0], cB[last, 2, samples], ALU.add)
                        dve.wait_ge(S["t3_ready"], g * 2 + (ph + 1))
                        step(dve.memset(t3[last, two, W], 0.0))
                        if ph == 1:
                            dve.tensor_copy(x3[0][last, 0:2, 0], t3[last, 0:2, 0])
                        dve.tensor_copy(x3[0][:, two, cols], t3[:, two, cols]).then_inc(S["x3_ready"], 1)
                        dve.wait_ge(S["x3_ready"], g * 4 + (2 * ph + 1))
                        if ph == 1:
                            minus(x3[1][last, 0:2, 0], t3[last, 0:2, 0], x3[0][last, 0:2, 0])
                        minus(x3[1][:, two, cols], t3[:, two, cols], x3[0][:, two, cols]).then_inc(S["x3_ready"], 1)
                if stage:
                    dve.wait_ge(S["logits_done"], g)
                    step(dve.tensor_copy(lpart[:], bank[0][:, E:2 * E]))
                    dve.tensor_tensor(logit[:], bank[0][:, 0:E], lpart[:], ALU.add).then_inc(S["logit_ready"], 1)
                    dve.wait_ge(S["sig_ready"], g)
                    step(dve.tensor_tensor(sc[:], sig[:], biasrow[:], ALU.add))
                    land(dve)
                    step(dve.max(top[:], sc[:]))
                    dve.reduce_sum(tsum[:], top[:, 0:TOPK], AX_X)
                    step(dve.max_index(topi[:], top[:], sc[:]))
                    dve.tensor_scalar(tsum2[:], tsum[:], 1e-20, None, ALU.add)
                    step(dve.tensor_copy(topf[:], topi[:, 0:TOPK]))
                    dve.reciprocal(trec[:], tsum2[:])
                    step(dve.tensor_tensor(hot[:], iota_e[:].rearrange("p (a e) -> p a e", a=1).broadcast_to([P, TOPK, E]),
                                           topf[:].rearrange("p (k a) -> p k a", a=1).broadcast_to([P, TOPK, E]), ALU.is_equal))
                    with nc.allow_low_precision(reason="zeros and ones"):
                        dve.reduce_sum(mask[:], hot[:].rearrange("p k e -> p e k"), AX_X).then_inc(S["mask_ready"], 1)
                    if not (early and g < 3):
                        dve.wait_ge(S[f"scattered{1 - par}"], k * (16 * TOPK))
                    dve.tensor_scalar(entry[:, 1 - par, :, 1], top[:, 0:TOPK], trec[:], None, ALU.mult)
                    step(dve.tensor_copy(entry[:, 1 - par, :, 0], tok[:].broadcast_to([P, TOPK])))
                    dve.tensor_scalar(tok[:], tok[:], float(P), None, ALU.add)
                if tail < 1 and not (early and g == G - 2):
                    first_in(g + 2, par, None)
                if stage:
                    dve.wait_ge(S["down_done"], g)
                    dve.wait_ge(S[f"base_loaded{1 - par}"], (k + 1) * 16)
                    if not (early and g < 3):
                        dve.wait_ge(S[f"o_written{1 - par}"], k * 16)
                    dve.tensor_tensor(orow[:, 1 - par, :], xbase[:, 1 - par, :], bank[5][:], ALU.add).then_inc(S["o_ready"], 1)

            assert P * E * COLS == P << 9 and COLS * P == T and P == 1 << 7
            layer0(0)
            first_in(1, 1, None)
            for c in range(HC + IC):
                weights_lo(0, 0, c)
            for g in range(3):
                body(g, g % 2, (g - 1) // 2)
            start, base[1] = base[0] + base[1], 0
            per_group = 18
            with dve.Fori(0, (G - 6) // 2) as it:
                base[2] = it * (2 * per_group) + start
                body(it * 2 + 3, 1, it + 1)
                assert base[1] == per_group, base[1]
                body(it * 2 + 4, 0, it + 1)
            base[:] = [start + (G - 6) * per_group, 0, None]
            for g in range(G - 3, G + 2):
                body(g, g % 2, (g - 1) // 2, tail=max(0, g - G + 2))
            count[0] = base[0] + base[1]

            dve.wait_ge(S["count_done"], 1)
            wide = lambda a: a.rearrange("p (i a) -> p i a", a=1).broadcast_to([P, a.shape[1], E])
            rows = lambda a: a.rearrange("p (a e) -> p a e", a=1).broadcast_to([P, E + 1, E])
            dve.tensor_copy(cnt[:, 1:E], bank[7][:, 1:E])
            link(dve.tensor_scalar(cnt[:, 0:1], bank[7][:, 0:1], 1.0, None, ALU.max))
            link(dve.tensor_tensor(over[:], wide(cnt[:]), thresh[:].rearrange("p (a m) -> p a m", a=1).broadcast_to([P, E, E]), ALU.is_gt))
            some = over[:, :, 0]
            dve.tensor_tensor(spread[:, 1], before[:], rows(some), ALU.mult)
            link(dve.reduce_sum(njobs[:], over[:], AX_X))
            dve.reduce_sum(rank[:], spread[:, 1], AX_X)
            link(dve.tensor_tensor(spread[:, 0], before[:], rows(njobs[:]), ALU.mult))
            dve.reduce_sum(job0[:], spread[:, 0], AX_X)
            link(dve.tensor_tensor(found[:], wide(iota_bf[:]), rows(rank[:, 0:E]), ALU.is_equal))
            dve.tensor_scalar(beyond[:], iota_bf[:], rank[:, E:E + 1], job0[:, E:E + 1], ALU.is_ge, ALU.mult)
            dve.tensor_scalar(ahalf[:], iota_e[:, 0:E // 2], 2.0, rank[:, E:E + 1], ALU.mult, ALU.is_lt)
            link(dve.tensor_tensor(found[:], found[:], rows(some), ALU.mult))
            dve.reduce_sum(pairs[:], ahalf[:], AX_X)
            dve.tensor_tensor(spread[:, 2], found[:], rows(iota_e[:]), ALU.mult)
            link(dve.tensor_tensor(spread[:, 3], found[:], rows(job0[:, 0:E]), ALU.mult))
            dve.reduce_sum(order[:], spread[:, 2], AX_X)
            link(dve.reduce_sum(first[:], spread[:, 3], AX_X))
            dve.tensor_copy(meta[:, 0:1], pairs[:])
            dve.tensor_copy(meta[:, 1:2], rank[:, E:E + 1])
            dve.tensor_copy(meta[:, 2:3], job0[:, E:E + 1])
            dve.tensor_copy(table[:, :, 0], order[:])
            dve.tensor_scalar(table[:, :, 1], order[:], float(COLS), None, ALU.mult)
            link(dve.tensor_tensor(first[:], first[:], beyond[:], ALU.add))
            dve.tensor_copy(table[:, :, 2], first[:])
            dve.tensor_scalar(table[:, 0:E, 4], first[:, 1:E + 1], 1.0, None, ALU.subtract)
            dve.tensor_copy(table[:, 0:E, 3], first[:, 1:E + 1]).then_inc(S["table_ready"], 1)
            for c in range(3):
                weights_lo(1, 1, c)
            dve.wait_ge(S["lists_loaded"], 16)
            dve.tensor_copy(all_ids[:], all_lists[:, :, 0]).then_inc(S["ids_ready"], 1)
            for c in range(3, HC + IC):
                weights_lo(1, 1, c)

            def turned_in(j, u):
                dve.wait_ge(S["b_xt_hi"], j * 2 + (u + 1))
                dve.tensor_tensor(xt[1][:, u].rearrange("p c t -> p (c t)"), bank[4 + u][:],
                                  xt[0][:, u].rearrange("p c t -> p (c t)").bitcast(F32), ALU.subtract).then_inc(S["b_xt_lo"], 1)

            dve.memset(tsum[:], 0.0).then_inc(S["b_zt_lo"], 2)
            dve.memset(yb[:].rearrange("p u h -> p (u h)"), 0.0).then_inc(S["b_y"], 2)
            for u in range(2):
                turned_in(0, u)

            def job(j, ahead, b, at):
                def w(*chunks):
                    for c in chunks if ahead is not None else ():
                        weights_lo(ahead, 1 - b, c)

                def glu(u):
                    dve.wait_ge(S["b_sg"], j * 2 + (u + 1))
                    dve.tensor_tensor(z[:, u, :], sg[:, u, :], bank[u][:, 0:I], ALU.mult).then_inc(S["dve_step"], 1)
                    dve.wait_ge(S["dve_step"], j * 2 + (count[0] + u + 1))
                    dve.tensor_tensor(z[:, u, :], z[:, u, :], bank[u][:, I:2 * I], ALU.mult).then_inc(S["b_z"], 1)

                def z_in(u):
                    dve.wait_ge(S["b_zt_hi"], j * 2 + (u + 1))
                    dve.tensor_tensor(zt[1][:, u].rearrange("p c t -> p (c t)"), bank[2 + u][:, 0:I],
                                      zt[0][:, u].rearrange("p c t -> p (c t)").bitcast(F32), ALU.subtract).then_inc(S["b_zt_lo"], 1)

                def weighted(u):
                    dve.wait_ge(S["b_down"], j * 2 + (u + 1))
                    dve.wait_ge(S[f"b_added{u}"], 16 * (j + 2))
                    dve.tensor_scalar(yb[:, u, :], bank[6 + u][:], all_lists[:, bass.ds(at + u, 1), 1], None,
                                      ALU.mult).then_inc(S["b_y"], 1)

                w(0, 1)
                glu(0)
                w(2, 3)
                z_in(0)
                glu(1)
                turned_in(j + 1, 0)
                w(4)
                z_in(1)
                w(5)
                weighted(0)
                turned_in(j + 1, 1)
                weighted(1)

            def first_job(i, first, b):
                at = dve.value_load(table[0:1, bass.ds(i, 1), 1], min_val=0, max_val=(E - 1) * COLS)
                job(first, i + 2, b, at)
                return at

            def other_jobs(first, end, at, b):
                with dve.Fori(first + 1, end) as j:
                    job(j, None, b, in_lists((j - first) * 2 + at, 0, E * COLS - 2))

            routed(dve, first_job, other_jobs)

        @block.tensor
        def _(pe):
            pe.wait_ge(S["style_loaded"], 32)
            pe.wait_ge(S["iota_done"], 9)
            pe.transpose(bank[6][0:SD, 0:P], modw[:], ident[:])
            pe.transpose(bank[6][0:SD, P:2 * P], sty[:], ident[:]).then_inc(S["modt_ready"], 1)
            pe.wait_ge(S["modt_copied"], 1)
            for l in range(NL):
                r = pe.matmul(bank[4][:, l * B:(l + 1) * B], modwt[:, l].rearrange("d a c -> d (a c)"), styt[:], start=True, stop=True)
            r.then_inc(S["s_psum"], 1)
            pe.wait_ge(S["mats_ready"], 2)
            for dst, at, n in [m for m in MATRICES if m[0] is not None] + [(5, SQ, 4)]:
                for t in range(n):
                    r = pe.transpose(bank[dst][:, P * t:P * t + P], big[:, at + t].rearrange("p q c -> p (q c)"), ident[:])
                r.then_inc(S["diag_t"], 1)
            pe.wait_ge(S["gate_loaded"], 16)
            for c in range(HC):
                r = pe.transpose(bank[6][:, c * E:(c + 1) * E], gnat[:, c:H:HC], ident[0:E, 0:E])
            r.then_inc(S["gate_t"], 1)
            pe.wait_ge(S["modt_copied"], 2)
            for l in range(NL):
                r = pe.matmul(bank[4][:, l * B:(l + 1) * B], wsqt[:, l, :], s2[:, l, :], start=True, stop=True)
            r.then_inc(S["dem_psum"], 1)

            def turn_weights(n, c):
                if c == 0:
                    pe.wait_ge(S["raw_loaded"], n * 48 + 48)
                for m in range(2 * IC if c < HC else HC):
                    src = wraw[:, m, c:H:HC] if c < HC else wdraw[:, m, P * (c - HC):P * (c - HC) + P]
                    r = pe.transpose(wbank(n, c)[:, P * m:P * m + P], src, ident[:])
                r.then_inc(S["w_t"], 1)

            def up(u, b):
                return [([x[:, u, c, :] for x in xt], [w[:, c, :] for w in wup[b]], False) for c in range(HC)]

            def down(u, b):
                return [([x[:, u, c, :] for x in zt], [w[:, c, :] for w in wdn[b]], False) for c in range(IC)]

            def turn_z(u, dst):
                for c in range(IC):
                    r = pe.transpose(dst[:, P * c:P * c + P], z[:, u, P * c:P * c + P], ident[:])
                return r

            def layer0(g):
                if isinstance(g, int) and g == 0:
                    pe.wait_ge(S["wts_lo"], len(MATRICES))
                else:
                    pe.wait_ge(S["t1_ready"], g)
                same = [([w[:, k, :] for w in cwt], [x[:, k:k + L] for x in x0], True) for k in range(K)]
                pe.wait_ge(S["x0_hi"], g + 1)
                hi_passes(pe, bank[0][:], same)
                pe.wait_ge(S["x0_lo"], g + 1)
                lo_passes(pe, bank[0][:], same).then_inc(S["l0_done"], 1)

            def columns(m, rows, data):
                return [w[0:rows, m, :] for w in cwt], [data(a) for a in range(2)], True

            def body(g, par, tail=0):
                early = isinstance(g, int)
                stage = tail < 3 and not (early and g == 0)
                if not (early and g < 2):
                    pe.wait_ge(S["mask_ready"], g - 1)
                    pe.wait_ge(S["zt_lo"], g - 1)
                    pe.matmul(bank[7][:, 0:E], tri[:], mask[:], start=True, stop=False)
                    pe.matmul(bank[7][:, 0:E], ones[:], cum[:, par, :], start=False, stop=True).then_inc(S["prefix_done"], 1)
                if tail < 1:
                    if not (early and g < 2):
                        pe.wait_ge(S["logit_ready"], g - 1)
                    layer0(g + 1)
                if stage:
                    pe.wait_ge(S["h_ready"], g)
                    if not (early and g == 1):
                        pe.wait_ge(S["o_ready"], g - 1)
                    for c in range(HC):
                        r = pe.transpose(bank[5][:, P * c:P * c + P], hrow[:, 1 - par, c, :], ident[:])
                    r.then_inc(S["xt_t"], 1)
                if tail < 2:
                    if early and g == 0:
                        pe.wait_ge(S["wts_lo"], len(MATRICES) + 1)
                        pe.wait_ge(S["sqrt_done"], 1)
                        for c in range(HC + IC):
                            turn_weights(0, c)
                        pe.wait_ge(S["w_lo"], HC + IC)
                    if stage:
                        pe.wait_ge(S["h_ready"], g)
                        pe.wait_ge(S["t2_ready"], g * 2)
                    for ph in range(2):
                        both = slice(2 * ph, 2 * ph + 2)
                        dst = bank[1 + ph][:].rearrange("p (b w) -> p b w", b=2)
                        terms = [columns(UP, P, lambda a: x1[:, a, both, :])]
                        pe.wait_ge(S["x1_stacked"], (g + 1) * (16 * Q * NB))
                        hi_passes(pe, dst, terms)
                        lo_passes(pe, dst, terms).then_inc(S["l1_done"], 1)
                if stage:
                    if not (early and g == 1):
                        pe.wait_ge(S["z_ready"], g - 1)
                    pe.wait_ge(S["xt_hi"], g)
                    hi_passes(pe, bank[6][:], up(0, 0))
                    pe.wait_ge(S["xt_lo"], g)
                    lo_passes(pe, bank[6][:], up(0, 0)).then_inc(S["up_done"], 1)
                if tail < 2:
                    if stage:
                        pe.wait_ge(S["t3_ready"], g * 2)
                    for ph in range(2):
                        both = slice(2 * ph, 2 * ph + 2)
                        dst = bank[3 + ph][:].rearrange("p (b w) -> p b w", b=2)
                        terms = [columns(SAME, P, lambda a: x2[a][:, both, 0:W]),
                                 columns(SAME + 1, 2 * C, lambda a: x2[a][0:2 * C, both, 1:W + 1])]
                        first = [columns(SAME + 1, 2 * C, lambda a: x2[a][0:2 * C, :, 0])]
                        pe.wait_ge(S["x2_ready"], g * 4 + (2 * ph + 1))
                        if ph == 1:
                            hi_passes(pe, bank[1][:, 0:NB], first)
                        hi_passes(pe, dst, terms)
                        pe.wait_ge(S["x2_ready"], g * 4 + (2 * ph + 2))
                        if ph == 1:
                            lo_passes(pe, bank[1][:, 0:NB], first)
                        lo_passes(pe, dst, terms).then_inc(S["l2_done"], 1)
                if stage:
                    pe.wait_ge(S["z_ready"], g)
                    if not (early and g == 1):
                        pe.wait_ge(S["place_ready"], g - 1)
                    turn_z(0, bank[7]).then_inc(S["zt_t"], 1)
                if stage:
                    if tail < 1:
                        pe.wait_ge(S["t1_ready"], g + 2)
                    elif not (early and g == 1):
                        pe.wait_ge(S["logit_ready"], g - 1)
                    for c in range(HC):
                        if c == HC - 1:
                            for d_ in range(HC):
                                pe.matmul(bank[0][:, 0:E], xt[1][:, 0, d_, :], gwt[:, d_, 0, :], start=False, stop=False)
                        r = pe.matmul(bank[0][:, 0:2 * E], xt[0][:, 0, c, :], gwt[:, c].rearrange("p a e -> p (a e)"),
                                      start=c == 0, stop=c == HC - 1)
                    r.then_inc(S["logits_done"], 1)
                    pe.wait_ge(S["zt_hi"], g)
                    hi_passes(pe, bank[5][:], down(0, 0))
                    pe.wait_ge(S["zt_lo"], g)
                    lo_passes(pe, bank[5][:], down(0, 0)).then_inc(S["down_done"], 1)
                if tail < 2:
                    pe.wait_ge(S["t2_ready"], g * 2 + 1)
                    dst = bank[1][:].rearrange("p (b w) -> p b w", b=NB)
                    terms = [columns(DOWN + n, P, lambda a: x3[a][:, :, n:n + W - 1:2]) for n in range(3)]
                    terms.append(columns(DOWN + 3, C, lambda a: x3[a][0:C, :, 3:W + 2:2]))
                    pe.wait_ge(S["x3_ready"], g * 4 + 3)
                    hi_passes(pe, dst, terms)
                    pe.wait_ge(S["x3_ready"], g * 4 + 4)
                    lo_passes(pe, dst, terms).then_inc(S["l3_done"], 1)

            layer0(0)
            for g in range(3):
                body(g, g % 2)
            with pe.Fori(0, (G - 6) // 2) as it:
                body(it * 2 + 3, 1)
                body(it * 2 + 4, 0)
            body(G - 3, 1)
            body(G - 2, 0)
            body(G - 1, 1, tail=1)
            body(G, 0, tail=2)
            pe.wait_ge(S["logit_ready"], G)
            for c in range(HC + IC):
                turn_weights(1, c)
            body(G + 1, 1, tail=3)
            pe.wait_ge(S["place_ready"], G)
            pe.matmul(bank[7][:, 0:E], ones[:], cum[:, G % 2, :], start=True, stop=True).then_inc(S["count_done"], 1)

            def turn_in(j, u):
                pe.wait_ge(S[f"b_gathered{u}"], 16 * (j + 1))
                if isinstance(j, int):
                    pe.wait_ge(S["o_ready"], G)
                else:
                    pe.wait_ge(S["b_xt_lo"], j * 2 + (u - 1))
                for c in range(HC):
                    r = pe.transpose(bank[4 + u][:, P * c:P * c + P], xg[:, u, P * c:P * c + P], ident[:])
                r.then_inc(S["b_xt_t"], 1)

            pe.wait_ge(S["w_lo"], 2 * (HC + IC))
            for u in range(2):
                turn_in(0, u)

            def job(j, ahead, b):
                def w(*chunks):
                    for c in chunks if ahead is not None else ():
                        turn_weights(ahead, c)

                def w_taken(n):
                    if ahead is not None:
                        pe.wait_ge(S["w_lo"], ahead * (HC + IC) + n)

                pe.wait_ge(S["b_zt_lo"], j * 2 + 2)
                w_taken(0)
                w(0, 1)
                pe.wait_ge(S["b_xt_hi"], j * 2 + 1)
                hi_passes(pe, bank[0][:], up(0, b))
                pe.wait_ge(S["b_xt_lo"], j * 2 + 1)
                lo_passes(pe, bank[0][:], up(0, b)).then_inc(S["b_up"], 1)
                pe.wait_ge(S["b_y"], j * 2 + 2)
                w(2, 3)
                pe.wait_ge(S["b_xt_hi"], j * 2 + 2)
                hi_passes(pe, bank[1][:], up(1, b))
                w_taken(1)
                pe.wait_ge(S["b_z"], j * 2 + 1)
                turn_z(0, bank[2]).then_inc(S["b_zt_t"], 1)
                pe.wait_ge(S["b_xt_lo"], j * 2 + 2)
                lo_passes(pe, bank[1][:], up(1, b)).then_inc(S["b_up"], 1)
                turn_in(j + 1, 0)
                w(4)
                w_taken(3)
                pe.wait_ge(S["b_zt_hi"], j * 2 + 1)
                hi_passes(pe, bank[6][:], down(0, b))
                pe.wait_ge(S["b_zt_lo"], j * 2 + 3)
                lo_passes(pe, bank[6][:], down(0, b)[:1], last=False)
                pe.wait_ge(S["b_z"], j * 2 + 2)
                turn_z(1, bank[3]).then_inc(S["b_zt_t"], 1)
                turn_in(j + 1, 1)
                lo_passes(pe, bank[6][:], down(0, b)[1:]).then_inc(S["b_down"], 1)
                w(5)
                w_taken(4)
                pe.wait_ge(S["b_zt_hi"], j * 2 + 2)
                hi_passes(pe, bank[7][:], down(1, b))
                pe.wait_ge(S["b_zt_lo"], j * 2 + 4)
                lo_passes(pe, bank[7][:], down(1, b)).then_inc(S["b_down"], 1)

            def first_job(i, first, b):
                job(first, i + 2, b)

            def other_jobs(first, end, at, b):
                with pe.Fori(first + 1, end) as j:
                    job(j, None, b)

            routed(pe, first_job, other_jobs)


_INS = ["x", "cond_512", "L0_cond_weights", "L0_cond_biases", "L0_cond_mod_w", "L0_cond_mod_b", "L0_ffn_gate_w",
        "L0_ffn_bias", "L0_ffn_Wg", "L0_ffn_Wu", "L0_ffn_Wd", "L0_ffn_Sg", "L0_ffn_Su", "L0_ffn_Sd"]


def kernel(**inputs):
    import numpy as _np
    import concourse.bacc as _bacc
    from concourse import mybir as _mybir
    from concourse.bass_utils import run_bass_kernel_spmd as _run

    nc = _bacc.Bacc("TRN2", target_bir_lowering=False, num_devices=1)
    arrays, args = {}, []
    for name in _INS:
        a = _np.ascontiguousarray(inputs[name])
        arrays[f"in_{name}"] = a
        args.append(nc.dram_tensor(f"in_{name}", a.shape, _mybir.dt.from_np(a.dtype), kind="ExternalInput").ap())
    B, C, L = inputs["x"].shape
    out = nc.dram_tensor("out_rows", [B * C + 256, L], _mybir.dt.float32, kind="ExternalOutput").ap()
    mk_adaln_ffn(nc, *args, out)
    r = _run(nc, [arrays], core_ids=[0])
    return r.results[0]["out_rows"][:B * C].reshape(B, C, L)
```
